# Optimizing a Trainium2 kernel written in Bass

```python
import numpy as np
import jax
import jax.numpy as jnp

def _softmax(x, axis=-1):
    return jax.nn.softmax(x, axis=axis)

def _gelu(x):
    return jax.nn.gelu(x, approximate=True)

def _silu(x):
    return jax.nn.silu(x)

def _sigmoid(x):
    return jax.nn.sigmoid(x)

def _layernorm(x, axis=-1, eps=1e-05):
    m = jnp.mean(x, axis=axis, keepdims=True)
    v = jnp.var(x, axis=axis, keepdims=True)
    return (x - m) / jnp.sqrt(v + eps)

def _scatter_add(tgt, idx, src, axis=0):
    return tgt.at[idx].add(src)

def _segment_sum(src, seg, n):
    return jax.ops.segment_sum(src, seg, n)
kernel_name = 'mk_gnn_resnorm_d4_gnn_r8_bb705a'

def setup_inputs(seed: int=0):
    np.random.seed(seed)
    _w = jnp.asarray

    def _rec_inputs():
        import jax
        import jax.numpy as jnp
        _gk = jax.random.key(seed)
        x = -0.0003713 + 1 * jax.random.normal(jax.random.fold_in(_gk, 1), (6250, 128), jnp.float32)
        _s = jax.random.randint(jax.random.fold_in(_gk, 2), (100000,), 0, 6250, jnp.int32)
        _d = jax.random.randint(jax.random.fold_in(_gk, 3), (100000,), 0, 6250, jnp.int32)
        _loop = jnp.arange(6250, dtype=jnp.int32)
        src = jnp.concatenate([_s, _d, _loop])
        dst = jnp.concatenate([_d, _s, _loop])
        _o = jnp.argsort(dst, stable=True)
        src = src[_o]
        dst = dst[_o]
        edge_attr_64 = 0.000189758 + 1.00013 * jax.random.normal(jax.random.fold_in(_gk, 12), (206250, 64), jnp.float32)
        edge_type_8 = jax.random.randint(jax.random.fold_in(_gk, 14), (206250,), 0, 8, jnp.int32)
        edge_weight = jax.random.uniform(jax.random.fold_in(_gk, 15), (206250,), jnp.float32, 0.0, 1)
        return (x, src, dst, edge_attr_64, edge_type_8, edge_weight)
    x, src, dst, edge_attr_64, edge_type_8, edge_weight = _rec_inputs()

    def _L0_gnn_setup():
        import jax, jax.numpy as jnp
        import numpy as np
        N_NODES = 12500
        N_EDGES = 400000
        IN_FEATS = 128
        H_FEATS = 128
        NUM_HEADS = 4
        NEG_SLOPE = 0.2

        def gat_layer(h, src, dst, ew, W, al, ar, b, n_nodes):
            H, Dh = al.shape
            feat = (h @ W).reshape(n_nodes, H, Dh)
            el = jnp.sum(feat * al[None], axis=-1)
            er = jnp.sum(feat * ar[None], axis=-1)
            e = jax.nn.leaky_relu(el[src] + er[dst], NEG_SLOPE)
            m = jax.ops.segment_max(e, dst, num_segments=n_nodes)
            m = jnp.where(jnp.isfinite(m), m, 0.0)
            ex = jnp.exp(e - m[dst])
            s = jax.ops.segment_sum(ex, dst, num_segments=n_nodes)
            a = ex / jnp.maximum(s[dst], 1e-20)
            a = a * ew[:, None]
            msg = a[:, :, None] * feat[src]
            out = jax.ops.segment_sum(msg, dst, num_segments=n_nodes)
            out = out + b.reshape(1, H, Dh)
            return jax.nn.elu(out).reshape(n_nodes, H * Dh)
        key = jax.random.key(seed)
        ks = jax.random.split(key, 12)
        d = {}
        d['in_feat'] = jax.random.normal(ks[0], (N_NODES, IN_FEATS), jnp.float32)
        d['edge_weights'] = jax.random.uniform(ks[1], (N_EDGES,), jnp.float32)
        d['src'] = jax.random.randint(ks[2], (N_EDGES,), 0, N_NODES, jnp.int32)
        d['dst'] = jax.random.randint(ks[3], (N_EDGES,), 0, N_NODES, jnp.int32)
        s = 1.0 / np.sqrt(IN_FEATS)
        d['W0'] = jax.random.normal(ks[4], (IN_FEATS, H_FEATS), jnp.float32) * s
        d['attn_l0'] = jax.random.normal(ks[5], (NUM_HEADS, H_FEATS // NUM_HEADS), jnp.float32) * s
        d['attn_r0'] = jax.random.normal(ks[6], (NUM_HEADS, H_FEATS // NUM_HEADS), jnp.float32) * s
        d['bias0'] = jnp.zeros((H_FEATS,), jnp.float32)
        d['W1'] = jax.random.normal(ks[7], (H_FEATS, H_FEATS), jnp.float32) * s
        d['attn_l1'] = jax.random.normal(ks[8], (NUM_HEADS, H_FEATS // NUM_HEADS), jnp.float32) * s
        d['attn_r1'] = jax.random.normal(ks[9], (NUM_HEADS, H_FEATS // NUM_HEADS), jnp.float32) * s
        d['bias1'] = jnp.zeros((H_FEATS,), jnp.float32)
        return d
    _L0_gnn_all = _L0_gnn_setup()
    _L0_gnn_in = {k: v for k, v in _L0_gnn_all.items() if k in ('W0', 'attn_l0', 'attn_r0', 'bias0', 'W1', 'attn_l1', 'attn_r1', 'bias1')}
    del _L0_gnn_all

    def _L1_gnn_setup():
        import jax, jax.numpy as jnp
        import numpy as np
        N = 12500
        NNZ = 200000
        F_IN = 128
        F_OUT = 128

        def _spmm(edge_val, edge_row, edge_col, x, n):
            gathered = edge_val[:, None] * x[edge_col]
            return jax.ops.segment_sum(gathered, edge_row, num_segments=n)
        key = jax.random.key(seed)
        ks = jax.random.split(key, 8)
        return {'features': jax.random.normal(ks[0], (N, F_IN), dtype=jnp.float32), 'edge_val': jax.random.uniform(ks[1], (NNZ,), dtype=jnp.float32), 'W1': jax.random.normal(ks[2], (F_IN, F_OUT), dtype=jnp.float32) * 0.05, 'b1': jax.random.normal(ks[3], (F_OUT,), dtype=jnp.float32) * 0.05, 'W2': jax.random.normal(ks[4], (F_IN, F_OUT), dtype=jnp.float32) * 0.05, 'b2': jax.random.normal(ks[5], (F_OUT,), dtype=jnp.float32) * 0.05, 'edge_row': jax.random.randint(ks[6], (NNZ,), 0, N, dtype=jnp.int32), 'edge_col': jax.random.randint(ks[7], (NNZ,), 0, N, dtype=jnp.int32)}
    _L1_gnn_all = _L1_gnn_setup()
    _L1_gnn_in = {k: v for k, v in _L1_gnn_all.items() if k in ('W1', 'b1', 'W2', 'b2')}
    del _L1_gnn_all

    def _L2_gnn_setup():
        import jax, jax.numpy as jnp
        import numpy as np
        N_NODES = 12500
        N_EDGES = 100000
        IN_CH = 128
        EDGE_CH = 64
        OUT_CH = 128
        EPS = 1e-12

        def l2_normalize(v, axis=-1):
            norm = jnp.sqrt(jnp.sum(v * v, axis=axis, keepdims=True))
            return v / jnp.maximum(norm, EPS)
        key = jax.random.key(seed)
        k1, k2, k3, k4, k5 = jax.random.split(key, 5)
        x = jax.random.normal(k1, (N_NODES, IN_CH), dtype=jnp.float32)
        edge_index = jax.random.randint(k2, (2, N_EDGES), 0, N_NODES, dtype=jnp.int64)
        edge_attr = jax.random.normal(k3, (N_EDGES, EDGE_CH), dtype=jnp.float32)
        fan_in = IN_CH + EDGE_CH
        bound = 1.0 / np.sqrt(fan_in)
        W = jax.random.uniform(k4, (OUT_CH, fan_in), minval=-bound, maxval=bound, dtype=jnp.float32)
        b = jax.random.uniform(k5, (OUT_CH,), minval=-bound, maxval=bound, dtype=jnp.float32)
        return {'x': x, 'edge_index': edge_index, 'edge_attr': edge_attr, 'W': W, 'b': b}
    _L2_gnn_all = _L2_gnn_setup()
    _L2_gnn_in = {k: v for k, v in _L2_gnn_all.items() if k in ('W', 'b')}
    del _L2_gnn_all

    def _L3_gnn_setup():
        import jax, jax.numpy as jnp
        import numpy as np
        N_NODES = 12500
        N_REL = 8
        EMB = 128
        N_EDGES = 200000
        key = jax.random.key(seed)
        k1, k2, k3, k4, k5 = jax.random.split(key, 5)
        node_emb = jax.random.normal(k1, (N_NODES, EMB), dtype=jnp.float32)
        weights = jax.random.normal(k2, (N_REL, EMB, EMB), dtype=jnp.float32) / np.sqrt(EMB)
        src = jax.random.randint(k3, (N_EDGES,), 0, N_NODES, dtype=jnp.int32)
        rel = jax.random.randint(k4, (N_EDGES,), 0, N_REL, dtype=jnp.int32)
        dst = jax.random.randint(k5, (N_EDGES,), 0, N_NODES, dtype=jnp.int32)
        return {'node_emb': node_emb, 'weights': weights, 'src': src, 'rel': rel, 'dst': dst}
    _L3_gnn_all = _L3_gnn_setup()
    _L3_gnn_in = {k: v for k, v in _L3_gnn_all.items() if k in ('weights',)}
    del _L3_gnn_all
    return {'x': x, 'src': src, 'dst': dst, 'edge_attr_64': edge_attr_64, 'edge_type_8': edge_type_8, 'edge_weight': edge_weight, 'L0_gnn_W0': _L0_gnn_in['W0'], 'L0_gnn_attn_l0': _L0_gnn_in['attn_l0'], 'L0_gnn_attn_r0': _L0_gnn_in['attn_r0'], 'L0_gnn_bias0': _L0_gnn_in['bias0'], 'L0_gnn_W1': _L0_gnn_in['W1'], 'L0_gnn_attn_l1': _L0_gnn_in['attn_l1'], 'L0_gnn_attn_r1': _L0_gnn_in['attn_r1'], 'L0_gnn_bias1': _L0_gnn_in['bias1'], 'L1_gnn_W1': _L1_gnn_in['W1'], 'L1_gnn_b1': _L1_gnn_in['b1'], 'L1_gnn_W2': _L1_gnn_in['W2'], 'L1_gnn_b2': _L1_gnn_in['b2'], 'L2_gnn_W': _L2_gnn_in['W'], 'L2_gnn_b': _L2_gnn_in['b'], 'L3_gnn_weights': _L3_gnn_in['weights']}

def reference(x, src, dst, edge_attr_64, edge_type_8, edge_weight, L0_gnn_W0, L0_gnn_attn_l0, L0_gnn_attn_r0, L0_gnn_bias0, L0_gnn_W1, L0_gnn_attn_l1, L0_gnn_attn_r1, L0_gnn_bias1, L1_gnn_W1, L1_gnn_b1, L1_gnn_W2, L1_gnn_b2, L2_gnn_W, L2_gnn_b, L3_gnn_weights):
    import jax
    import jax.numpy as jnp

    def _L0_gnn_ref(in_feat, edge_weights, src, dst, W0, attn_l0, attn_r0, bias0, W1, attn_l1, attn_r1, bias1):
        import jax, jax.numpy as jnp
        import numpy as np
        N_NODES = 12500
        N_EDGES = 400000
        IN_FEATS = 128
        H_FEATS = 128
        NUM_HEADS = 4
        NEG_SLOPE = 0.2

        def gat_layer(h, src, dst, ew, W, al, ar, b, n_nodes):
            H, Dh = al.shape
            feat = (h @ W).reshape(n_nodes, H, Dh)
            el = jnp.sum(feat * al[None], axis=-1)
            er = jnp.sum(feat * ar[None], axis=-1)
            e = jax.nn.leaky_relu(el[src] + er[dst], NEG_SLOPE)
            m = jax.ops.segment_max(e, dst, num_segments=n_nodes)
            m = jnp.where(jnp.isfinite(m), m, 0.0)
            ex = jnp.exp(e - m[dst])
            s = jax.ops.segment_sum(ex, dst, num_segments=n_nodes)
            a = ex / jnp.maximum(s[dst], 1e-20)
            a = a * ew[:, None]
            msg = a[:, :, None] * feat[src]
            out = jax.ops.segment_sum(msg, dst, num_segments=n_nodes)
            out = out + b.reshape(1, H, Dh)
            return jax.nn.elu(out).reshape(n_nodes, H * Dh)
        n = in_feat.shape[0]
        h = gat_layer(in_feat, src, dst, edge_weights, W0, attn_l0, attn_r0, bias0, n)
        h = gat_layer(h, src, dst, edge_weights, W1, attn_l1, attn_r1, bias1, n)
        return h

    def _L1_gnn_ref(features, edge_val, W1, b1, W2, b2, edge_row, edge_col):
        import jax, jax.numpy as jnp
        import numpy as np
        N = 12500
        NNZ = 200000
        F_IN = 128
        F_OUT = 128

        def _spmm(edge_val, edge_row, edge_col, x, n):
            gathered = edge_val[:, None] * x[edge_col]
            return jax.ops.segment_sum(gathered, edge_row, num_segments=n)
        n = features.shape[0]
        Lf = _spmm(edge_val, edge_row, edge_col, features, n)
        inter_feature = Lf * features
        inter_part1 = (Lf + features) @ W1 + b1
        Li = _spmm(edge_val, edge_row, edge_col, inter_feature, n)
        inter_part2 = Li @ W2 + b2
        return inter_part1 + inter_part2

    def _L2_gnn_ref(x, edge_index, edge_attr, W, b):
        import jax, jax.numpy as jnp
        import numpy as np
        N_NODES = 12500
        N_EDGES = 100000
        IN_CH = 128
        EDGE_CH = 64
        OUT_CH = 128
        EPS = 1e-12

        def l2_normalize(v, axis=-1):
            norm = jnp.sqrt(jnp.sum(v * v, axis=axis, keepdims=True))
            return v / jnp.maximum(norm, EPS)
        row, col = (edge_index[0], edge_index[1])
        n_nodes = x.shape[0]
        msg = jnp.concatenate([x[row], edge_attr], axis=1)
        msg = l2_normalize(msg, axis=1)
        sums = jax.ops.segment_sum(msg, col, num_segments=n_nodes)
        counts = jax.ops.segment_sum(jnp.ones((msg.shape[0],), dtype=msg.dtype), col, num_segments=n_nodes)
        agg = sums / jnp.maximum(counts, 1.0)[:, None]
        out = agg @ W.T + b
        return l2_normalize(out, axis=1)

    def _L3_gnn_ref(node_emb, weights, src, rel, dst):
        import jax, jax.numpy as jnp
        import numpy as np
        N_NODES = 12500
        N_REL = 8
        EMB = 128
        N_EDGES = 200000
        n, e = node_emb.shape
        r = weights.shape[0]
        fr = src + n * rel
        vals = jnp.ones(src.shape[0], dtype=node_emb.dtype)
        rowsum = jax.ops.segment_sum(vals, fr, num_segments=r * n)
        vals = vals / rowsum[fr]
        msgs = vals[:, None] * node_emb[dst]
        agg = jax.ops.segment_sum(msgs, fr, num_segments=r * n)
        agg = agg.reshape(r, n, e)
        out = jnp.einsum('rij,rnj->ni', weights, agg)
        return jax.nn.relu(out)
    edge_index = jnp.stack([src, dst])
    x = _layernorm(x + _L0_gnn_ref(x, edge_weight, src, dst, L0_gnn_W0, L0_gnn_attn_l0, L0_gnn_attn_r0, L0_gnn_bias0, L0_gnn_W1, L0_gnn_attn_l1, L0_gnn_attn_r1, L0_gnn_bias1), axis=-1)
    x = _layernorm(x + _L1_gnn_ref(x, edge_weight, L1_gnn_W1, L1_gnn_b1, L1_gnn_W2, L1_gnn_b2, src, dst), axis=-1)
    x = _layernorm(x + _L2_gnn_ref(x, edge_index, edge_attr_64, L2_gnn_W, L2_gnn_b), axis=-1)
    x = _layernorm(x + _L3_gnn_ref(x, L3_gnn_weights, src, edge_type_8, dst), axis=-1)
    return x

_drawn_inputs = setup_inputs


def setup_inputs(seed=0):
    import zlib

    import numpy as np

    out = dict(_drawn_inputs(seed))
    spreads = {'L0_gnn_bias0': (0.0, 0.1), 'L0_gnn_bias1': (0.0, 0.1)}
    factors = {'edge_attr_64': 30.833,
     'L0_gnn_attn_r0': 64.0,
     'L0_gnn_attn_l1': 27.918,
     'L0_gnn_attn_r1': 64.0,
     'L1_gnn_b1': 8.0,
     'L1_gnn_b2': 7.073,
     'L2_gnn_W': 3.0}
    for name, (base, spread) in spreads.items():
        noise = np.random.default_rng([zlib.crc32(name.encode()), seed]).standard_normal(out[name].shape)
        drawn = base * np.exp(spread * noise) if base else spread * noise
        out[name] = jnp.asarray(drawn.astype(out[name].dtype))
    for name, factor in factors.items():
        out[name] = (out[name] * factor).astype(out[name].dtype)
    return out
```

```python
from contextlib import ExitStack

import concourse.bass as bass
from concourse import mybir

F32 = mybir.dt.float32
BF16 = mybir.dt.bfloat16
I32 = mybir.dt.int32
ALU = mybir.AluOpType
ACT = mybir.ActivationFunctionType
AX = mybir.AxisListType.X
At = bass.IndirectOffsetOnAxis

P = 128
NODES, FEAT, HEADS, RELS, ATTR = 6250, 128, 4, 8, 64
DH = FEAT // HEADS
EDGES = 206250

REAL_WIN = -(-NODES // P)
WIN = REAL_WIN + 1
ROWS = WIN * P
PAD_NODE = REAL_WIN * P
LAST_ROWS = NODES - (REAL_WIN - 1) * P

COLS_REAL = -(-EDGES // P)
LAST_COLS = EDGES - (P - 1) * COLS_REAL
SG = 4
COLS = -(-COLS_REAL // SG) * SG + SG
SCAT = COLS // SG

PADS = COLS * P - EDGES
TILES = (EDGES + REAL_WIN * (P - 1)) // P + -(-PADS // P)
G = 8
TILES = -(-TILES // G) * G
GROUPS = TILES // G
SLOTS = 4
NOWHERE = 200.0
TCOLS = TILES // P
assert TILES % P == 0 and GROUPS % SLOTS == 0 and SCAT % SLOTS == 0

REC = 4
DREC = REC + ATTR
BIG = 1e30
SLOPE = 0.2
R_GAT = FEAT + HEADS


def since(g, n):
    return not isinstance(g, int) or g >= n


def each_group(eng, body, groups=GROUPS):
    for g in range(SLOTS):
        body(g, g, 0)
    with eng.Fori(0, groups // SLOTS - 1) as i:
        for s in range(SLOTS):
            body(i * SLOTS + (SLOTS + s), s, i + 1)


class Chain:

    def __init__(self, eng, sem):
        self.eng, self.sem, self.base, self.n = eng, sem, 0, 0

    def begin(self, base):
        self.base, self.n = base, 0

    def did(self, ins):
        ins.then_inc(self.sem, 1)
        self.n += 1
        return ins

    def wait(self):
        self.eng.wait_ge(self.sem, self.base + self.n)

    def step(self, ins):
        self.did(ins)
        self.wait()


class Mem:

    def __init__(self, nc, ctx, tag):
        self.nc, self.ctx, self.tag, self.sems = nc, ctx, tag, []

    def sb(self, name, shape, dt=F32):
        return self.ctx.enter_context(self.nc.sbuf_tensor(f"{self.tag}_{name}", shape, dt))

    def ps(self, name, shape, dt=F32):
        return self.ctx.enter_context(self.nc.psum_tensor(f"{self.tag}_{name}", shape, dt))

    def sem(self, name):
        if not self.sems:
            self.ctx.callback(self.zero)
        self.sems.append(self.nc.alloc_semaphore(f"{self.tag}_{name}"))
        return self.sems[-1]

    def zero(self):
        with self.nc.Block() as block:
            @block.gpsimd
            def _(pool):
                for s in self.sems:
                    pool.sem_clear(s)
        for s in self.sems:
            self.nc.release_semaphore(s)


def constants(nc, k, top):
    k.ident = top.sb("ident", [P, P])
    k.ident16 = top.sb("ident16", [P, P], BF16)
    k.count = top.sb("count", [P, P])
    k.before = top.sb("before", [P, P])
    k.ones = top.sb("ones", [P, P])
    k.pick = top.sb("pick", [3 * HEADS, HEADS, P], BF16)
    with ExitStack() as ctx:
        m = Mem(nc, ctx, "const")
        made = m.sem("made")
        block = ctx.enter_context(nc.Block())

        @block.gpsimd
        def _(pool):
            c = Chain(pool, made)
            c.step(nc.gpsimd.memset(k.ident[:], 0.0))
            c.step(nc.gpsimd.memset(k.ones[:], 1.0))
            c.step(nc.gpsimd.memset(k.pick[:], 0.0))
            c.step(nc.gpsimd.affine_select(out=k.ident[:], in_=k.ident[:], compare_op=ALU.not_equal, fill=1.0,
                                           base=0, pattern=[[-1, P]], channel_multiplier=1))
            c.step(nc.gpsimd.iota(k.count[:], pattern=[[1, P]], base=0, channel_multiplier=0,
                                  allow_small_or_imprecise_dtypes=True))
            c.step(nc.gpsimd.affine_select(out=k.before[:], in_=k.ones[:], compare_op=ALU.is_gt, fill=0.0,
                                           base=0, pattern=[[1, P]], channel_multiplier=-1))
            for part in range(3):
                c.step(nc.gpsimd.affine_select(out=k.pick[:], in_=k.pick[:], compare_op=ALU.not_equal, fill=1.0,
                                               base=-HEADS * part, pattern=[[-1, HEADS], [0, P]],
                                               channel_multiplier=1))
            c.step(nc.gpsimd.tensor_copy(k.ident16[:], k.ident[:]))


def sort_edges(nc, k, src, dst, etype, ew, attr):
    with ExitStack() as outer:
        keep = Mem(nc, outer, "sort")
        row = {w: keep.sb(f"row_{w}", [P, COLS], I32) for w in "ds"}
        with ExitStack() as ctx:
            m = Mem(nc, ctx, "rank")
            raw = {w: m.sb(f"raw_{w}", [P, COLS], I32) for w in ("src", "dst", "rel")}
            weight = m.sb("weight", [P, COLS])
            win = {w: m.sb(f"win_{w}", [P, COLS]) for w in "ds"}
            num = m.sb("num", [P, COLS])
            shifted = m.sb("shifted", [P, COLS], I32)
            hit = m.sb("hit", [P, COLS], I32)
            hitf = m.sb("hitf", [P, COLS])
            run = m.sb("run", [P, COLS])
            at = {w: m.sb(f"at_{w}", [P, COLS]) for w in "ds"}
            total = m.sb("total", [P, 2, WIN])
            wins = m.sb("wins", [P, 2, WIN])
            winsi = m.sb("winsi", [P, 2, WIN], I32)
            tend = m.sb("tend", [P, 2, WIN])
            tstart = m.sb("tstart", [P, 2, WIN])
            base = m.sb("base", [P, 2, WIN])
            zero = m.sb("zero", [P, WIN])
            tile_no = m.sb("tile_no", [P, TCOLS])
            le = m.sb("le", [P, TCOLS, WIN])
            tw = m.sb("tw", [P, 2, TCOLS])
            twi = m.sb("twi", [P, 2, TCOLS], I32)
            fill = m.sb("fill", [P, TILES // 64, DREC])
            fill_s = m.sb("fill_s", [P, TILES // 8, REC])
            sums = m.ps("sums", [P, 2, 512])
            padded, landed, filled = m.sem("padded"), m.sem("landed"), m.sem("filled")
            counted, summed, tiled, wrote, cleared, made, chain, tick = (
                m.sem(x) for x in ("counted", "summed", "tiled", "wrote", "cleared", "made", "chain", "tick"))
            block = ctx.enter_context(nc.Block())
            real = {"src": src, "dst": dst, "rel": etype, "ew": ew}

            @block.sync
            def _(sp):
                sp.wait_ge(padded, 1)
                n = 0
                for name, a in real.items():
                    t = weight if name == "ew" else raw[name]
                    flat = (P - 1) * COLS_REAL
                    sp.dma_start(t[0:P - 1, 0:COLS_REAL],
                                 a[0:flat].rearrange("(p c) -> p c", p=P - 1)).then_inc(landed, 16)
                    sp.dma_start(t[P - 1:P, 0:LAST_COLS],
                                 a[flat:EDGES].rearrange("(p c) -> p c", p=1)).then_inc(landed, 16)
                sp.wait_ge(made, 1)
                for j in range(64):
                    sp.dma_start(k.rec_d[:, bass.ts(j, TILES // 64), :], fill[:]).then_inc(filled, 16)
                for j in range(8):
                    sp.dma_start(k.rec_s[:, bass.ts(j, TILES // 8), :], fill_s[:]).then_inc(filled, 16)
                sp.wait_ge(filled, 16 * (64 + 8))
                sp.wait_ge(landed, 16 * 8)
                sp.wait_ge(tiled, 1)
                for n, w in enumerate("ds"):
                    sp.dma_start(k.tile_win[n].rearrange("(p c) -> p c", p=P), twi[:, n, :]).then_inc(wrote, 16)
                sp.wait_ge(wrote, 32)

            @block.tensor
            def _(pe):
                pe.wait_ge(counted, 1)
                t = total[:].rearrange("p a w -> p (a w)")
                nc.tensor.matmul(sums[:, 0, 0:2 * WIN], k.before[:], t, start=True, stop=True)
                nc.tensor.matmul(sums[:, 1, 0:2 * WIN], k.ones[:], t, start=True, stop=True).then_inc(summed, 1)

            @block.gpsimd
            def _(pool):
                nc.gpsimd.iota(tile_no[:], pattern=[[1, TCOLS]], base=0, channel_multiplier=TCOLS,
                               allow_small_or_imprecise_dtypes=True)
                nc.gpsimd.memset(fill_s[:], 0.0)
                nc.gpsimd.memset(fill[:], 0.0).then_inc(cleared, 1)
                pool.wait_ge(cleared, 1)
                nc.gpsimd.memset(fill_s[:, :, 1:2], NOWHERE)
                nc.gpsimd.memset(fill[:, :, 1:2], NOWHERE).then_inc(made, 1)

            @block.vector
            def _(v):
                c = Chain(v, chain)
                for t in (raw["src"], raw["dst"]):
                    nc.vector.memset(t[:, COLS_REAL:COLS], PAD_NODE)
                    nc.vector.memset(t[P - 32:P, LAST_COLS:COLS_REAL], PAD_NODE)
                for t in (raw["rel"], weight):
                    nc.vector.memset(t[:, COLS_REAL:COLS], 0)
                    last = nc.vector.memset(t[P - 32:P, LAST_COLS:COLS_REAL], 0)
                c.did(nc.vector.memset(zero[:], 0.0))
                for w in "ds":
                    c.did(nc.vector.memset(at[w][:], 0.0))
                nc.vector.memset(num[:], 0.0).then_inc(padded, 1)
                v.wait_ge(landed, 16 * 8)
                v.wait_ge(padded, 1)
                c.wait()
                for w, key, other in (("d", "dst", "src"), ("s", "src", "dst")):
                    rec = k.sorted[w]
                    c.step(nc.vector.tensor_scalar(shifted[:], raw[key][:], 7, None, ALU.arith_shift_right))
                    c.step(nc.vector.tensor_copy(win[w][:], shifted[:]))
                    c.step(nc.vector.tensor_copy(num[:], raw[key][:]))
                    c.step(nc.vector.scalar_tensor_tensor(rec[:, 0:COLS, 1], win[w][:], -float(P), num[:],
                                                          ALU.mult, ALU.add))
                    c.step(nc.vector.tensor_copy(rec[:, 0:COLS, 0], raw[other][:]))
                    c.step(nc.vector.tensor_copy(rec[:, 0:COLS, 2], weight[:]))
                    c.step(nc.vector.tensor_copy(rec[:, 0:COLS, 3], raw["rel"][:]))
                c.begin(c.n)
                start = c.base
                with v.Fori(0, WIN) as i:
                    for n, w in enumerate("ds"):
                        nc.vector.tensor_scalar(hitf[:], win[w][:], k.count[:, bass.ds(i, 1)], 0.0, ALU.is_equal,
                                                ALU.add, accum_out=total[:, n, bass.ds(i, 1)]).then_inc(chain, 1)
                        v.wait_ge(chain, i * 2 + (start + n + 1))
                v.sem_inc(counted, 1)
                c.begin(start + 2 * WIN)
                v.wait_ge(summed, 1)
                flat = lambda t: t[:].rearrange("p a w -> p (a w)")
                c.step(nc.vector.tensor_scalar(flat(winsi), sums[:, 1, 0:2 * WIN], float(P - 1), None, ALU.add))
                c.step(nc.vector.tensor_scalar(flat(winsi), flat(winsi), 7, None, ALU.arith_shift_right))
                c.step(nc.vector.tensor_copy(flat(wins), flat(winsi)))
                for n in range(2):
                    c.step(nc.vector.tensor_tensor_scan(tend[:, n, :], wins[:, n, :], zero[:], 0.0,
                                                        ALU.add, ALU.add))
                c.step(nc.vector.tensor_sub(flat(tstart), flat(tend), flat(wins)))
                c.step(nc.vector.scalar_tensor_tensor(flat(base), flat(tstart), float(P), sums[:, 0, 0:2 * WIN],
                                                      ALU.mult, ALU.add))
                v.wait_ge(made, 1)
                for n in range(2):
                    c.step(nc.vector.tensor_tensor(
                        le[:], tstart[:, n, :].unsqueeze(1).broadcast_to([P, TCOLS, WIN]),
                        tile_no[:].unsqueeze(2).broadcast_to([P, TCOLS, WIN]), ALU.is_le))
                    c.step(nc.vector.tensor_reduce(tw[:, n, :], le[:], AX, ALU.add))
                c.step(nc.vector.tensor_scalar(flat(twi), flat(tw), -1.0, None, ALU.add))
                v.sem_inc(tiled, 1)
                start = c.base + c.n
                with v.Fori(0, WIN) as i:
                    for n, w in enumerate("ds"):
                        done = i * 6 + (start + 3 * n)
                        nc.vector.tensor_scalar(hit[:], win[w][:], k.count[:, bass.ds(i, 1)], None,
                                                ALU.is_equal).then_inc(chain, 1)
                        v.wait_ge(chain, done + 1)
                        nc.vector.tensor_tensor_scan(run[:], hit[:], hit[:], base[:, n, bass.ds(i, 1)],
                                                     ALU.add, ALU.max).then_inc(chain, 1)
                        v.wait_ge(chain, done + 2)
                        v.sem_inc(tick, 1)
                        nc.vector.copy_predicated(at[w][:], hit[:], run[:]).then_inc(chain, 1)
                        v.wait_ge(chain, done + 3)
                        v.sem_inc(tick, 1)
                c.begin(start + 6 * WIN)
                for w in "ds":
                    c.step(nc.vector.tensor_scalar(hit[:], at[w][:], -1.0, None, ALU.add))
                    c.step(nc.vector.tensor_scalar(shifted[:], hit[:], 7, None, ALU.arith_shift_right))
                    c.step(nc.vector.tensor_scalar(hit[:], hit[:], P - 1, None, ALU.bitwise_and))
                    c.step(nc.vector.tensor_copy(run[:], shifted[:]))
                    c.step(nc.vector.tensor_copy(num[:], hit[:]))
                    c.step(nc.vector.scalar_tensor_tensor(row[w][:], num[:], float(TILES), run[:],
                                                          ALU.mult, ALU.add))

        scatter(nc, k, row, attr)


def scatter(nc, k, row, attr):
    with ExitStack() as ctx:
        m = Mem(nc, ctx, "scatter")
        out_d = m.sb("out_d", [P, SLOTS, SG, DREC])
        out_s = m.sb("out_s", [P, SLOTS, SG, REC])
        where = m.sb("where", [P, SLOTS, 2, SG], I32)
        attr_in = [m.sem(f"attr_in{s}") for s in range(SLOTS)]
        staged, sent_tick = m.sem("staged"), m.sem("sent_tick")
        sent, base = k.pool_dma, k.pool_dma_count
        whole = (P - 1) * COLS_REAL
        attr_a = attr[0:whole, :].rearrange("(p c) f -> p c f", p=P - 1)
        attr_b = attr[whole:EDGES, :].rearrange("(p c) f -> p c f", p=1)
        per_slot = 2 * SG * 16
        full = LAST_COLS // SG
        block = ctx.enter_context(nc.Block())

        @block.sync
        def _(sp):
            def body(g, s, u):
                if since(g, SLOTS):
                    sp.wait_ge(sent[s], u * per_slot + base)
                sp.dma_start(out_d[0:P - 1, s, :, REC:], attr_a[:, bass.ds(g * SG, SG), :]).then_inc(attr_in[s], 16)
                sp.dma_start(out_d[P - 1:P, s, :, REC:], attr_b[:, bass.ds(g * SG, SG), :]).then_inc(attr_in[s], 16)

            lo = full // SLOTS * SLOTS
            for g in range(SLOTS):
                body(g, g, 0)
            with sp.Fori(0, lo // SLOTS - 1) as i:
                for s in range(SLOTS):
                    body(i * SLOTS + (SLOTS + s), s, i + 1)
            for g in range(lo, SCAT):
                s, u = g % SLOTS, g // SLOTS
                sp.wait_ge(sent[s], u * per_slot + base)
                c0 = g * SG
                a = min(SG, COLS_REAL - c0)
                b = min(SG, LAST_COLS - c0)
                if a > 0:
                    sp.dma_start(out_d[0:P - 1, s, 0:a, REC:], attr_a[:, c0:c0 + a, :]).then_inc(attr_in[s], 16)
                else:
                    sp.sem_inc(attr_in[s], 16)
                if b > 0:
                    sp.dma_start(out_d[P - 1:P, s, 0:b, REC:], attr_b[:, c0:c0 + b, :]).then_inc(attr_in[s], 16)
                else:
                    sp.sem_inc(attr_in[s], 16)

        @block.vector
        def _(v):
            def body(g, s, u):
                v.wait_ge(attr_in[s], (u + 1) * 32)
                v.sem_inc(sent_tick, 1)
                for n, (w, o) in enumerate((("d", out_d), ("s", out_s))):
                    nc.vector.tensor_copy(o[:, s, :, 0:REC], k.sorted[w][:, bass.ds(g * SG, SG), :])
                    last = nc.vector.tensor_copy(where[:, s, n, :], row[w][:, bass.ds(g * SG, SG)])
                    last.then_inc(staged, 1)

            each_group(v, body, SCAT)

        @block.gpsimd
        def _(pool):
            def body(g, s, u):
                pool.wait_ge(staged, g * 2 + 2)
                pool.sem_inc(sent_tick, 1)
                for j in range(SG):
                    for n, (o, to) in enumerate(((out_d, k.rec_d), (out_s, k.rec_s))):
                        nc.gpsimd.indirect_dma_start(
                            to.rearrange("p t r -> (p t) r"), At(where[:, s, n, j:j + 1], 0),
                            o[:, s, j, :], None).then_inc(sent[s], 16)

            each_group(pool, body, SCAT)
            for s in range(SLOTS):
                pool.wait_ge(sent[s], SCAT // SLOTS * per_slot + base)
        k.pool_dma_count += SCAT // SLOTS * per_slot


def load_edges(nc, k):
    with ExitStack() as ctx:
        m = Mem(nc, ctx, "edges")
        landed = m.sem("landed")
        block = ctx.enter_context(nc.Block())

        @block.sync
        def _(sp):
            for j in range(8):
                part = bass.ts(j, TILES // 8)
                sp.dma_start(k.sorted["d"][:, part, :], k.rec_d[:, part, 0:REC]).then_inc(landed, 16)
            sp.dma_start(k.sorted["s"][:], k.rec_s[:]).then_inc(landed, 16)
            sp.wait_ge(landed, 16 * 9)


def load_nodes(nc, k, x_in):
    with ExitStack() as ctx:
        m = Mem(nc, ctx, "nodes")
        zeroed, landed = m.sem("zeroed"), m.sem("landed")
        block = ctx.enter_context(nc.Block())

        @block.vector
        def _(v):
            nc.vector.memset(k.x[:, REAL_WIN - 1:WIN, :], 0.0).then_inc(zeroed, 1)

        @block.sync
        def _(sp):
            whole = (REAL_WIN - 1) * P
            sp.wait_ge(zeroed, 1)
            sp.dma_start(k.x[:, 0:REAL_WIN - 1, :],
                         x_in[0:whole, :].rearrange("(w p) f -> p w f", p=P)).then_inc(landed, 16)
            sp.dma_start(k.x[0:LAST_ROWS, REAL_WIN - 1, :], x_in[whole:NODES, :]).then_inc(landed, 16)
            sp.wait_ge(landed, 32)


def table_view(table):
    return table.rearrange("(w p) f -> p w f", p=P)


def attention_rows(nc, k, name, nodes, weight, left, right):
    with ExitStack() as ctx:
        m = Mem(nc, ctx, name)
        w = m.sb("w", [P, FEAT])
        sides = m.sb("sides", [P, 2, FEAT])
        turned = m.sb("turned", [P, 2, P])
        out = m.sb("out", [P, WIN, R_GAT])
        prod = m.sb("prod", [P, 2, 2, FEAT])
        ps_t = m.ps("ps_t", [P, 2, 512])
        ps_f = m.ps("ps_f", [P, 2, 512])
        landed, turn, copied, product, used, chain, wrote = (
            m.sem(x) for x in ("landed", "turn", "copied", "product", "used", "chain", "wrote"))
        block = ctx.enter_context(nc.Block())

        @block.sync
        def _(sp):
            sp.dma_start(w[:], weight).then_inc(landed, 16)
            for n, a in enumerate((left, right)):
                sp.dma_start(sides[:, n, :], a.rearrange("h d -> (h d)").unsqueeze(0).broadcast_to([P, FEAT])
                             ).then_inc(landed, 16)
            sp.wait_ge(used, WIN)
            sp.dma_start(table_view(k.gat_rows), out[:]).then_inc(wrote, 16)
            sp.wait_ge(wrote, 16)

        @block.tensor
        def _(pe):
            pe.wait_ge(landed, 48)
            for g in range(WIN + 1):
                if g < WIN:
                    if g >= 2:
                        pe.wait_ge(copied, g - 1)
                    nc.tensor.transpose(ps_t[:, g % 2, 0:P], nodes[:, g, :], k.ident[:]).then_inc(turn, 1)
                if g >= 1:
                    pe.wait_ge(copied, g)
                    if g >= 3:
                        pe.wait_ge(used, g - 2)
                    nc.tensor.matmul(ps_f[:, (g - 1) % 2, 0:FEAT], turned[:, (g - 1) % 2, :], w[:],
                                     start=True, stop=True).then_inc(product, 1)

        @block.scalar
        def _(act):
            for g in range(WIN):
                act.wait_ge(turn, g + 1)
                if g >= 2:
                    act.wait_ge(product, g - 1)
                nc.scalar.copy(turned[:, g % 2, :], ps_t[:, g % 2, 0:P]).then_inc(copied, 1)

        @block.vector
        def _(v):
            c = Chain(v, chain)
            v.wait_ge(landed, 48)
            for g in range(WIN):
                b = g % 2
                f = ps_f[:, b, 0:FEAT]
                v.wait_ge(product, g + 1)
                for n in range(2):
                    c.did(nc.vector.tensor_mul(prod[:, b, n, :], f, sides[:, n, :]))
                c.wait()
                heads = prod[:, b].rearrange("p n (h d) -> p n h d", h=HEADS)
                nc.vector.tensor_reduce(out[:, g, FEAT:R_GAT], heads[:, 0], AX, ALU.add)
                nc.vector.tensor_reduce(k.pair[:, g, 0:HEADS], heads[:, 1], AX, ALU.add)
                nc.vector.tensor_copy(out[:, g, 0:FEAT], f).then_inc(used, 1)


def attention_maxima(nc, k, name):
    with ExitStack() as ctx:
        m = Mem(nc, ctx, name)
        index = m.sb("index", [P, TILES], I32)
        wins = m.sb("wins", [1, TILES], I32)
        slot_index = m.sb("slot_index", [P, SLOTS, G], I32)
        rows = m.sb("rows", [P, SLOTS, G, R_GAT])
        parts = m.sb("parts", [P, 2, G, 3 * HEADS], BF16)
        rest = m.sb("rest", [P, 2, 2, G, HEADS])
        hide = m.sb("hide", [P, 2, G, P], BF16)
        scores = m.sb("scores", [3 * HEADS, 2, G * P], BF16)
        best = m.sb("best", [P, WIN, HEADS])
        tile_best = m.sb("tile_best", [P, 2, G, HEADS])
        z = m.sb("z", [P, 2, WIN, HEADS])
        ps_s = m.ps("ps_s", [P, 2, 512])
        ps_z = m.ps("ps_z", [P, 4, HEADS, P])
        made, landed, chain, tick, best_done = (m.sem(x) for x in ("made", "landed", "chain", "tick", "best_done"))
        indexed = [m.sem(f"indexed{s}") for s in range(SLOTS)]
        gathered, base = k.pool_dma, k.pool_dma_count
        stored = [m.sem(f"stored{s}") for s in range(SLOTS)]
        split, turned, copied, masked, reduced = (m.sem(x) for x in ("split", "turned", "copied", "masked", "reduced"))
        ptick, atick, etick, stick = (m.sem(x) for x in ("ptick", "atick", "etick", "stick"))
        regs = [nc.vector.alloc_register(f"{name}_w{t}") for t in range(G)]
        rec = k.sorted["d"]
        block = ctx.enter_context(nc.Block())

        @block.sync
        def _(sp):
            sp.dma_start(wins[:], k.tile_win[0].unsqueeze(0)).then_inc(landed, 16)
            sp.wait_ge(made, 1)

            def body(g, s, u):
                if since(g, SLOTS):
                    sp.wait_ge(split, g - (SLOTS - 1))
                    sp.sem_inc(stick, 1)
                    sp.wait_ge(stored[s], u * 16)
                    sp.sem_inc(stick, 1)
                sp.dma_start(slot_index[:, s, :], index[:, bass.ds(g * G, G)]).then_inc(indexed[s], 16)

            each_group(sp, body)
            sp.wait_ge(landed, 16)

        @block.gpsimd
        def _(pool):
            def body(g, s, u):
                pool.wait_ge(indexed[s], (u + 1) * 16)
                pool.sem_inc(ptick, 1)
                for t in range(G):
                    nc.gpsimd.indirect_dma_start(rows[:, s, t, :], None, k.gat_rows,
                                                 At(slot_index[:, s, t:t + 1], 0)).then_inc(gathered[s], 16)

            each_group(pool, body)

        @block.scalar
        def _(act):
            def body(g, s, u):
                act.wait_ge(gathered[s], u * (16 * G) + (16 * G + base))
                act.sem_inc(atick, 1)
                act.dma_start(k.gat_edges[:, bass.ds(g * G, G), :], rows[:, s]).then_inc(stored[s], 16)
                act.wait_ge(turned, g + 1)
                act.sem_inc(atick, 1)
                if since(g, 2):
                    act.wait_ge(masked, g * G - G)
                    act.sem_inc(atick, 1)
                nc.scalar.copy(scores[:, s % 2, :], ps_s[0:3 * HEADS].rearrange("p a b -> p (a b)")
                               ).then_inc(copied, 1)

            each_group(act, body)
            for s in range(SLOTS):
                act.wait_ge(stored[s], GROUPS // SLOTS * 16)

        @block.tensor
        def _(pe):
            def body(g, s, u):
                pe.wait_ge(split, g + 1)
                if since(g, 1):
                    pe.wait_ge(copied, g)
                pe.sem_inc(etick, 1)
                for t in range(G):
                    last = nc.tensor.matmul(ps_s[0:3 * HEADS, t // 4, bass.ts(t % 4, P)], parts[:, s % 2, t, :],
                                            k.ident16[:], start=True, stop=True)
                last.then_inc(turned, 1)
                pe.wait_ge(copied, g + 1)
                pe.sem_inc(etick, 1)
                for t in range(G):
                    if since(g, 1) or t >= 4:
                        pe.wait_ge(reduced, g * G + (t - 3))
                        pe.sem_inc(etick, 1)
                    bank = ps_z[:, t % 4]
                    for h in range(HEADS):
                        nc.tensor.matmul(bank[:, h, :], hide[:, s % 2, t, :], k.ident16[:], start=True, stop=False)
                        last = nc.tensor.matmul(bank[:, h, :], k.pick[:, h, :], scores[:, s % 2, bass.ts(t, P)],
                                                start=False, stop=True)
                    last.then_inc(masked, 1)

            each_group(pe, body)

        @block.vector
        def _(v):
            c = Chain(v, chain)
            c.did(nc.vector.memset(best[:], -BIG))
            nc.vector.tensor_copy(index[:], rec[:, :, 0]).then_inc(made, 1)
            v.wait_ge(landed, 16)
            c.wait()
            start, per = c.n, 5 + G

            def body(g, s, u):
                b = s % 2
                c.begin(g * per + start)
                v.reg_load(regs, wins[0:1, bass.ds(g * G, G)])
                win = [v.snap(r, min_val=0, max_val=WIN - 1) for r in regs]
                v.wait_ge(gathered[s], u * (16 * G) + (16 * G + base))
                v.sem_inc(tick, 1)
                if since(g, 2):
                    v.wait_ge(masked, g * G - G)
                    v.sem_inc(tick, 1)
                score, r1, r2 = rows[:, s, :, FEAT:R_GAT], rest[:, b, 0], rest[:, b, 1]
                hi, mid, lo = (parts[:, b, :, bass.ts(q, HEADS)] for q in range(3))
                c.step(nc.vector.tensor_copy(hi, score))
                c.step(nc.vector.tensor_sub(r1, score, hi))
                c.step(nc.vector.tensor_copy(mid, r1))
                c.step(nc.vector.tensor_sub(r2, r1, mid))
                for t in range(G):
                    nc.vector.tensor_scalar(hide[:, b, t, :], k.count[:], rec[:, bass.ds(g * G + t, 1), 1], -BIG,
                                            ALU.not_equal, ALU.mult)
                c.did(nc.vector.tensor_copy(lo, r2))
                c.wait()
                v.sem_inc(split, 1)
                for t in range(G):
                    v.wait_ge(masked, g * G + (t + 1))
                    v.sem_inc(tick, 1)
                    nc.vector.tensor_reduce(tile_best[:, b, t, :], ps_z[:, t % 4], AX, ALU.max).then_inc(reduced, 1)
                    v.wait_ge(reduced, g * G + (t + 1))
                    v.sem_inc(tick, 1)
                    at = best[:, bass.ds(win[t], 1), :]
                    c.wait()
                    c.did(nc.vector.tensor_tensor(at, at, tile_best[:, b, t:t + 1, :], ALU.max))

            each_group(v, body)
            k.pool_dma_count += GROUPS // SLOTS * 16 * G
            c.begin(GROUPS * per + start)
            c.wait()
            c.step(nc.vector.tensor_add(z[:, 0], best[:], k.pair[:, :, 0:HEADS]))
            c.step(nc.vector.scalar_tensor_tensor(k.pair[:, :, HEADS:2 * HEADS], z[:, 0], SLOPE, z[:, 0],
                                                  ALU.mult, ALU.max))


def edge_pass(nc, k, name, order, width, weigh, steps, *, index=None, table=None, stream=None, row_width=FEAT,
              attributes=False, pair=None, func=None, words=1, counts=False):
    with ExitStack() as ctx:
        m = Mem(nc, ctx, name)
        n_win = 0 if order == "d" else 1
        rec = k.sorted[order]
        wins = m.sb("wins", [1, TILES], I32)
        rows = m.sb("rows", [P, SLOTS, G, row_width])
        hot = m.sb("hot", [P, 2, G, P])
        msg = m.sb("msg", [P, 2, G, width])
        if table is not None:
            indexes = m.sb("indexes", [P, TILES], I32)
            slot_index = m.sb("slot_index", [P, SLOTS, G], I32)
        if attributes:
            attrs = m.sb("attrs", [P, SLOTS, G, ATTR])
        if pair is not None:
            hot_t = m.sb("hot_t", [P, 2, G, P])
            ps_t = m.ps("ps_t", [P, 4, P])
            ps_own = m.ps("ps_own", [P, 2, G, 8])
        tmp = m.sb("tmp", [P, 2, 4, G, 8])
        per_bank = 512 // width
        banks = -(-G // per_bank)
        ps_sum = m.ps("ps_sum", [P, 2, banks, 512])
        gathered, base = k.pool_dma, k.pool_dma_count
        loaded = [m.sem(f"loaded{s}") for s in range(SLOTS)]
        loads = (table is None) + attributes
        indexed = [m.sem(f"indexed{s}") for s in range(SLOTS)]
        made, landed, chain = m.sem("made"), m.sem("landed"), m.sem("chain")
        hot_made, turned, copied, owned, asked, raised, weighed, summed, added = (
            m.sem(x) for x in ("hot_made", "turned", "copied", "owned", "asked", "raised", "weighed", "summed",
                               "added"))
        vtick, ptick, atick, etick, stick = (m.sem(x) for x in ("vtick", "ptick", "atick", "etick", "stick"))
        vregs = [nc.vector.alloc_register(f"{name}_v{t}") for t in range(G)]
        block = ctx.enter_context(nc.Block())

        def sums(b, t):
            at = t % per_bank * width
            return ps_sum[:, b, t // per_bank, at:at + width]

        @block.sync
        def _(sp):
            sp.dma_start(wins[:], k.tile_win[n_win].unsqueeze(0)).then_inc(landed, 16)
            sp.wait_ge(made, 1)

            def body(g, s, u):
                if since(g, SLOTS):
                    sp.wait_ge(weighed, g - (SLOTS - 1))
                    sp.sem_inc(stick, 1)
                if table is not None:
                    sp.dma_start(slot_index[:, s, :], indexes[:, bass.ds(g * G, G)]).then_inc(indexed[s], 16)
                else:
                    sp.dma_start(rows[:, s], stream[:, bass.ds(g * G, G), :]).then_inc(loaded[s], 16)
                if attributes:
                    sp.dma_start(attrs[:, s], k.rec_d[:, bass.ds(g * G, G), REC:DREC]).then_inc(loaded[s], 16)

            each_group(sp, body)
            sp.wait_ge(landed, 16)

        if table is not None:
            @block.gpsimd
            def _(pool):
                def body(g, s, u):
                    pool.wait_ge(indexed[s], (u + 1) * 16)
                    pool.sem_inc(ptick, 1)
                    for t in range(G):
                        nc.gpsimd.indirect_dma_start(rows[:, s, t, :], None, table,
                                                     At(slot_index[:, s, t:t + 1], 0)).then_inc(gathered[s], 16)

                each_group(pool, body)

        if pair is not None or func is not None:
            @block.scalar
            def _(act):
                def body(g, s, u):
                    if pair is not None:
                        for half in range(2):
                            act.wait_ge(turned, g * 2 + (half + 1))
                            act.sem_inc(atick, 1)
                            nc.scalar.copy(hot_t[:, s % 2, bass.ts(half, 4), :], ps_t[:]).then_inc(copied, 1)
                    if func is not None:
                        act.wait_ge(asked, g + 1)
                        act.sem_inc(atick, 1)
                        nc.scalar.activation(tmp[:, s % 2, 1, :, 0:words], tmp[:, s % 2, 0, :, 0:words],
                                             func).then_inc(raised, 1)

                each_group(act, body)

        @block.tensor
        def _(pe):
            pregs = [nc.tensor.alloc_register(f"{name}_p{t}") for t in range(G)] if pair is not None else None
            pe.wait_ge(landed, 16)

            def body(g, s, u):
                b = s % 2
                if pair is not None:
                    pe.reg_load(pregs, wins[0:1, bass.ds(g * G, G)])
                    win = [pe.snap(r, min_val=0, max_val=WIN - 1) for r in pregs]
                pe.wait_ge(hot_made, g + 1)
                pe.sem_inc(etick, 1)
                if pair is not None:
                    for half in range(2):
                        if since(g, 1) or half:
                            pe.wait_ge(copied, g * 2 + half)
                            pe.sem_inc(etick, 1)
                        for t in range(4):
                            last = nc.tensor.transpose(ps_t[:, t, :], hot[:, b, 4 * half + t, :], k.ident[:])
                        last.then_inc(turned, 1)
                    pe.wait_ge(copied, g * 2 + 2)
                    pe.sem_inc(etick, 1)
                    for t in range(G):
                        last = nc.tensor.matmul(ps_own[:, b, t, :], hot_t[:, b, t, :],
                                                pair[:, bass.ds(win[t], 1), :].rearrange("p a w -> p (a w)"),
                                                start=True, stop=True)
                    last.then_inc(owned, 1)
                pe.wait_ge(weighed, g + 1)
                pe.sem_inc(etick, 1)
                if since(g, 2):
                    pe.wait_ge(added, g * G - G)
                    pe.sem_inc(etick, 1)
                for t in range(G):
                    last = nc.tensor.matmul(sums(b, t), hot[:, b, t, :], msg[:, b, t, :], start=True, stop=True)
                last.then_inc(summed, 1)

            each_group(pe, body)

        @block.vector
        def _(v):
            c = Chain(v, chain)
            nc.vector.memset(k.acc[:, :, 0:width], 0.0).then_inc(added, G)
            if table is not None:
                index(v, c, indexes)
            if counts:
                c.step(nc.vector.memset(msg[:, :, :, width - 1:width], 1.0))
            v.sem_inc(made, 1)
            v.wait_ge(landed, 16)
            v.wait_ge(added, G)
            start = c.n

            def add_up(g, s):
                v.reg_load(vregs, wins[0:1, bass.ds(g * G, G)])
                win = [v.snap(r, min_val=0, max_val=WIN - 1) for r in vregs]
                v.wait_ge(summed, g + 1)
                v.sem_inc(vtick, 1)
                for t in range(G):
                    at = k.acc[:, bass.ds(win[t], 1), 0:width].rearrange("p a w -> p (a w)")
                    v.wait_ge(added, g * G + (t + G))
                    nc.vector.tensor_add(at, at, sums(s % 2, t)).then_inc(added, 1)

            def body(g, s, u):
                b = s % 2
                c.begin(g * steps + start)
                if since(g, 2):
                    v.wait_ge(summed, g - 1)
                    v.sem_inc(vtick, 1)
                for t in range(G):
                    last = nc.vector.tensor_scalar(hot[:, b, t, :], k.count[:], rec[:, bass.ds(g * G + t, 1), 1],
                                                   None, ALU.is_equal)
                last.then_inc(hot_made, 1)
                if since(g, 1):
                    add_up(g - 1, (s - 1) % SLOTS)
                if table is not None:
                    v.wait_ge(gathered[s], u * (16 * G) + (16 * G + base))
                    v.sem_inc(vtick, 1)
                if loads:
                    v.wait_ge(loaded[s], (u + 1) * 16 * loads)
                    v.sem_inc(vtick, 1)
                own = None
                if pair is not None:
                    v.wait_ge(owned, g + 1)
                    v.sem_inc(vtick, 1)
                    own = ps_own[:, b]

                def ask():
                    v.sem_inc(asked, 1)
                    v.wait_ge(raised, g + 1)
                    v.sem_inc(vtick, 1)

                weigh(v, c, msg[:, b], rows[:, s], attrs[:, s] if attributes else None, own,
                      rec[:, bass.ds(g * G, G), :], tmp[:, b], ask)
                assert c.n == steps, (name, c.n)
                v.sem_inc(weighed, 1)

            each_group(v, body)
            add_up(GROUPS - 1, SLOTS - 1)
            v.wait_ge(added, GROUPS * G + G)
        if table is not None:
            k.pool_dma_count += GROUPS // SLOTS * 16 * G


def over(a, n):
    return a.unsqueeze(3).broadcast_to([*a.shape, n])


def weigh_attention(nc):
    def weigh(v, c, msg, rows, attrs, own, rec, tmp, ask):
        score, e, ex = tmp[:, 2, :, 0:HEADS], tmp[:, 0, :, 0:HEADS], tmp[:, 1, :, 0:HEADS]
        exw = tmp[:, 3, :, 0:HEADS]
        c.step(nc.vector.tensor_add(score, rows[:, :, FEAT:R_GAT], own[:, :, 0:HEADS]))
        c.step(nc.vector.scalar_tensor_tensor(score, score, SLOPE, score, ALU.mult, ALU.max))
        c.step(nc.vector.tensor_sub(e, score, own[:, :, HEADS:2 * HEADS]))
        ask()
        c.step(nc.vector.tensor_mul(exw, ex, rec[:, :, 2:3].broadcast_to([P, G, HEADS])))
        c.did(nc.vector.tensor_mul(msg[:, :, 0:FEAT].rearrange("p g (h d) -> p g h d", h=HEADS),
                                   rows[:, :, 0:FEAT].rearrange("p g (h d) -> p g h d", h=HEADS), over(exw, DH)))
        c.step(nc.vector.tensor_copy(msg[:, :, FEAT:R_GAT], ex))
    return weigh, 6


def weigh_plain(nc, k, relations):
    def weigh(v, c, msg, rows, attrs, own, rec, tmp, ask):
        c.did(nc.vector.tensor_mul(msg[:, :, 0:FEAT], rows, rec[:, :, 2:3].broadcast_to([P, G, FEAT])))
        if relations:
            c.did(nc.vector.tensor_tensor(msg[:, :, FEAT:FEAT + RELS], rec[:, :, 3:4].broadcast_to([P, G, RELS]),
                                          k.count[:, 0:RELS].unsqueeze(1).broadcast_to([P, G, RELS]), ALU.is_equal))
        c.wait()
    return weigh, 1 + relations


def attention_end(nc, k, name, bias_in, out):
    with ExitStack() as ctx:
        m = Mem(nc, ctx, name)
        bias = m.sb("bias", [P, FEAT])
        inv = m.sb("inv", [P, WIN, HEADS])
        low = m.sb("low", [P, WIN, FEAT])
        landed, chain, asked, raised = (m.sem(x) for x in ("landed", "chain", "asked", "raised"))
        block = ctx.enter_context(nc.Block())

        @block.sync
        def _(sp):
            sp.dma_start(bias[:], bias_in.unsqueeze(0).broadcast_to([P, FEAT])).then_inc(landed, 16)
            sp.wait_ge(landed, 16)

        @block.scalar
        def _(act):
            act.wait_ge(asked, 1)
            nc.scalar.activation(low[:], low[:], ACT.Exp).then_inc(raised, 1)

        @block.vector
        def _(v):
            c = Chain(v, chain)
            v.wait_ge(landed, 16)
            c.step(nc.vector.tensor_scalar(k.per_dst[:], k.acc[:, :, R_GAT], 1.0, None, ALU.max))
            c.step(nc.vector.reciprocal(k.per_dst[:], k.per_dst[:]))
            c.step(nc.vector.tensor_scalar(inv[:], k.acc[:, :, FEAT:R_GAT], 1e-20, None, ALU.max))
            c.step(nc.vector.reciprocal(inv[:], inv[:]))
            heads = lambda a: a.rearrange("p w (h d) -> p w h d", h=HEADS)
            c.step(nc.vector.tensor_mul(heads(out[:]), heads(k.acc[:, :, 0:FEAT]), over(inv[:], DH)))
            c.step(nc.vector.tensor_add(out[:], out[:], bias[:].unsqueeze(1).broadcast_to([P, WIN, FEAT])))
            c.step(nc.vector.tensor_scalar(low[:], out[:], 0.0, None, ALU.min))
            v.sem_inc(asked, 1)
            v.wait_ge(raised, 1)
            c.step(nc.vector.tensor_scalar(low[:], low[:], -1.0, None, ALU.add))
            c.step(nc.vector.scalar_tensor_tensor(out[:], out[:], 0.0, low[:], ALU.max, ALU.add))


def weigh_normed(nc):
    def weigh(v, c, msg, rows, attrs, own, rec, tmp, ask):
        squares, inv = tmp[:, 0, :, 0:1], tmp[:, 2, :, 0:1]
        c.step(nc.vector.tensor_mul(msg[:, :, FEAT:FEAT + ATTR], attrs, attrs))
        c.step(nc.vector.tensor_reduce(tmp[:, 0, :, 0], msg[:, :, FEAT:FEAT + ATTR], AX, ALU.add))
        c.step(nc.vector.tensor_add(squares, squares, rows[:, :, FEAT:FEAT + 1]))
        ask()
        c.step(nc.vector.tensor_scalar(inv, tmp[:, 1, :, 0:1], 1e-12, None, ALU.max))
        c.step(nc.vector.reciprocal(inv, inv))
        c.did(nc.vector.tensor_mul(msg[:, :, 0:FEAT], rows[:, :, 0:FEAT], inv.broadcast_to([P, G, FEAT])))
        c.step(nc.vector.tensor_mul(msg[:, :, FEAT:FEAT + ATTR], attrs, inv.broadcast_to([P, G, ATTR])))
    return weigh, 7


def weigh_relation(nc, k):
    def weigh(v, c, msg, rows, attrs, own, rec, tmp, ask):
        c.step(nc.vector.tensor_tensor(tmp[:, 0], rec[:, :, 3:4].broadcast_to([P, G, RELS]),
                                       k.count[:, 0:RELS].unsqueeze(1).broadcast_to([P, G, RELS]), ALU.is_equal))
        c.step(nc.vector.tensor_mul(tmp[:, 1], tmp[:, 0], own))
        c.step(nc.vector.tensor_reduce(tmp[:, 2, :, 0], tmp[:, 1], AX, ALU.add))
        c.step(nc.vector.tensor_mul(msg, rows, tmp[:, 2, :, 0:1].broadcast_to([P, G, FEAT])))
    return weigh, 4


def index_first(nc, k, order):
    def index(v, c, out):
        c.step(nc.vector.tensor_copy(out[:], k.sorted[order][:, :, 0]))
    return index


def index_relation(nc, k):
    def index(v, c, out):
        rec = k.sorted["s"]
        c.step(nc.vector.scalar_tensor_tensor(out[:], rec[:, :, 3], float(ROWS), rec[:, :, 0], ALU.mult, ALU.add))
    return index


def store_nodes(nc, k, name, table, nodes, combine=None):
    with ExitStack() as ctx:
        m = Mem(nc, ctx, name)
        chain, ready, wrote = (m.sem(x) for x in ("chain", "ready", "wrote"))
        block = ctx.enter_context(nc.Block())

        @block.vector
        def _(v):
            if combine:
                combine(v, Chain(v, chain))
            v.sem_inc(ready, 1)

        @block.sync
        def _(sp):
            sp.wait_ge(ready, 1)
            sp.dma_start(table_view(table), nodes).then_inc(wrote, 16)
            sp.wait_ge(wrote, 16)


def turn_weights(nc, k, name, out, pieces):
    with ExitStack() as ctx:
        m = Mem(nc, ctx, name)
        raw = m.sb("raw", [P, len(pieces), P])
        ps = m.ps("ps", [P, 2, 512])
        landed, turned, copied = (m.sem(x) for x in ("landed", "turned", "copied"))
        block = ctx.enter_context(nc.Block())

        @block.sync
        def _(sp):
            for n, (a, _) in enumerate(pieces):
                sp.dma_start(raw[:, n, 0:a.shape[1]], a).then_inc(landed, 16)

        @block.tensor
        def _(pe):
            pe.wait_ge(landed, 16 * len(pieces))
            for n, (a, _) in enumerate(pieces):
                if n >= 2:
                    pe.wait_ge(copied, n - 1)
                nc.tensor.transpose(ps[0:a.shape[1], n % 2, 0:P], raw[:, n, 0:a.shape[1]], k.ident[:]
                                    ).then_inc(turned, 1)

        @block.vector
        def _(v):
            for n, (a, to) in enumerate(pieces):
                v.wait_ge(turned, n + 1)
                nc.vector.tensor_copy(to, ps[0:a.shape[1], n % 2, 0:P]).then_inc(copied, 1)
            v.wait_ge(copied, len(pieces))


def dense(nc, k, name, terms, out, biases):
    n_terms = len(terms)
    with ExitStack() as ctx:
        m = Mem(nc, ctx, name)
        turned = m.sb("turned", [P, 2, n_terms, P])
        bias = m.sb("bias", [P, len(biases), FEAT])
        ps_t = m.ps("ps_t", [P, 2, 4, P])
        ps_o = m.ps("ps_o", [P, 2, 512])
        landed, turn, copied, product, used, chain = (
            m.sem(x) for x in ("landed", "turn", "copied", "product", "used", "chain"))
        block = ctx.enter_context(nc.Block())

        @block.sync
        def _(sp):
            for n, a in enumerate(biases):
                sp.dma_start(bias[:, n, :], a.unsqueeze(0).broadcast_to([P, FEAT])).then_inc(landed, 16)

        @block.tensor
        def _(pe):
            for g in range(WIN + 1):
                if g < WIN:
                    if g >= 2:
                        pe.wait_ge(copied, g - 1)
                    for n, (nodes, w) in enumerate(terms):
                        last = nc.tensor.transpose(ps_t[0:nodes.shape[2], g % 2, n, :], nodes[:, g, :], k.ident[:])
                    last.then_inc(turn, 1)
                if g >= 1:
                    pe.wait_ge(copied, g)
                    if g >= 3:
                        pe.wait_ge(used, g - 2)
                    for n, (nodes, w) in enumerate(terms):
                        last = nc.tensor.matmul(ps_o[:, (g - 1) % 2, 0:FEAT],
                                                turned[0:nodes.shape[2], (g - 1) % 2, n, :], w,
                                                start=n == 0, stop=n == n_terms - 1)
                    last.then_inc(product, 1)

        @block.scalar
        def _(act):
            for g in range(WIN):
                act.wait_ge(turn, g + 1)
                if g >= 2:
                    act.wait_ge(product, g - 1)
                for n, (nodes, w) in enumerate(terms):
                    q = nodes.shape[2]
                    last = nc.scalar.copy(turned[0:q, g % 2, n, :], ps_t[0:q, g % 2, n, :])
                last.then_inc(copied, 1)

        @block.vector
        def _(v):
            c = Chain(v, chain)
            v.wait_ge(landed, 16 * len(biases))
            for n in range(1, len(biases)):
                c.step(nc.vector.tensor_add(bias[:, 0, :], bias[:, 0, :], bias[:, n, :]))
            for g in range(WIN):
                v.wait_ge(product, g + 1)
                nc.vector.tensor_add(out[:, g, :], ps_o[:, g % 2, 0:FEAT], bias[:, 0, :]).then_inc(used, 1)
            v.wait_ge(used, WIN)


def relation_rows(nc, k, name, weights, table):
    with ExitStack() as ctx:
        m = Mem(nc, ctx, name)
        turned = m.sb("turned", [P, 2, P])
        out = m.sb("out", [P, 2, RELS, FEAT])
        ps_t = m.ps("ps_t", [P, 2, 512])
        ps_o = m.ps("ps_o", [P, 2, 2, 512])
        turn, copied, product, used_a, used_v = (
            m.sem(x) for x in ("turn", "copied", "product", "used_a", "used_v"))
        wrote = [m.sem(f"wrote{b}") for b in range(2)]
        to = table.rearrange("(r w p) f -> p w r f", p=P, r=RELS)
        half = RELS // 2
        block = ctx.enter_context(nc.Block())

        @block.tensor
        def _(pe):
            for g in range(WIN + 1):
                if g < WIN:
                    if g >= 2:
                        pe.wait_ge(copied, g - 1)
                    nc.tensor.transpose(ps_t[:, g % 2, 0:P], k.x[:, g, :], k.ident[:]).then_inc(turn, 1)
                if g >= 1:
                    pe.wait_ge(copied, g)
                    if g >= 3:
                        pe.wait_ge(used_a, g - 2)
                        pe.wait_ge(used_v, g - 2)
                    for q in range(2):
                        last = nc.tensor.matmul(ps_o[:, (g - 1) % 2, q, :], turned[:, (g - 1) % 2, :],
                                                weights[:, half * q:half * (q + 1), :].rearrange("p r f -> p (r f)"),
                                                start=True, stop=True)
                    last.then_inc(product, 1)

        @block.scalar
        def _(act):
            for g in range(WIN + 1):
                if g < WIN:
                    act.wait_ge(turn, g + 1)
                    if g >= 2:
                        act.wait_ge(product, g - 1)
                    nc.scalar.copy(turned[:, g % 2, :], ps_t[:, g % 2, 0:P]).then_inc(copied, 1)
                if g >= 1:
                    b = (g - 1) % 2
                    act.wait_ge(product, g)
                    if g >= 3:
                        act.wait_ge(wrote[b], 16 * ((g - 1) // 2))
                    nc.scalar.copy(out[:, b, half:RELS, :].rearrange("p r f -> p (r f)"), ps_o[:, b, 1, :]
                                   ).then_inc(used_a, 1)

        @block.vector
        def _(v):
            for g in range(WIN):
                b = g % 2
                v.wait_ge(product, g + 1)
                if g >= 2:
                    v.wait_ge(wrote[b], 16 * (g // 2))
                nc.vector.tensor_copy(out[:, b, 0:half, :].rearrange("p r f -> p (r f)"), ps_o[:, b, 0, :]
                                      ).then_inc(used_v, 1)

        @block.sync
        def _(sp):
            for g in range(WIN):
                sp.wait_ge(used_a, g + 1)
                sp.wait_ge(used_v, g + 1)
                sp.dma_start(to[:, g], out[:, g % 2]).then_inc(wrote[g % 2], 16)
            for b in range(2):
                sp.wait_ge(wrote[b], 16 * (WIN // 2))


def residual_norm(nc, k, name, delta, before=None, result=None, normed=False):
    with ExitStack() as ctx:
        m = Mem(nc, ctx, name)
        squares = m.sb("squares", [P, WIN, FEAT])
        stat = m.sb("stat", [P, 3, WIN])
        chain, asked, raised, ready, wrote = (m.sem(x) for x in ("chain", "asked", "raised", "ready", "wrote"))
        block = ctx.enter_context(nc.Block())
        wide = lambda a: a.unsqueeze(2).broadcast_to([P, WIN, FEAT])

        @block.scalar
        def _(act):
            for n in range(1 + normed):
                act.wait_ge(asked, n + 1)
                nc.scalar.activation(stat[:, 2, :], stat[:, 1, :], ACT.Sqrt).then_inc(raised, 1)

        @block.vector
        def _(v):
            c = Chain(v, chain)
            if before:
                before(v, c)
            if normed:
                c.step(nc.vector.tensor_mul(squares[:], delta, delta))
                c.step(nc.vector.tensor_reduce(stat[:, 1, :], squares[:], AX, ALU.add))
                v.sem_inc(asked, 1)
                v.wait_ge(raised, 1)
                c.step(nc.vector.tensor_scalar(stat[:, 0, :], stat[:, 2, :], 1e-12, None, ALU.max))
                c.step(nc.vector.reciprocal(stat[:, 0, :], stat[:, 0, :]))
                c.step(nc.vector.tensor_mul(delta, delta, wide(stat[:, 0, :])))
            c.step(nc.vector.tensor_add(k.x[:], k.x[:], delta))
            c.step(nc.vector.tensor_reduce(stat[:, 0, :], k.x[:], AX, ALU.add))
            c.step(nc.vector.tensor_scalar(stat[:, 0, :], stat[:, 0, :], 1.0 / FEAT, None, ALU.mult))
            c.step(nc.vector.tensor_sub(k.x[:], k.x[:], wide(stat[:, 0, :])))
            c.step(nc.vector.tensor_mul(squares[:], k.x[:], k.x[:]))
            c.step(nc.vector.tensor_reduce(stat[:, 1, :], squares[:], AX, ALU.add))
            c.step(nc.vector.tensor_scalar(stat[:, 1, :], stat[:, 1, :], 1.0 / FEAT, 1e-5, ALU.mult, ALU.add))
            v.sem_inc(asked, 1)
            v.wait_ge(raised, 1 + normed)
            c.step(nc.vector.reciprocal(stat[:, 0, :], stat[:, 2, :]))
            c.step(nc.vector.tensor_mul(k.x[:], k.x[:], wide(stat[:, 0, :])))
            v.sem_inc(ready, 1)

        if result is not None:
            @block.sync
            def _(sp):
                sp.wait_ge(ready, 1)
                whole = (REAL_WIN - 1) * P
                sp.dma_start(result[0:whole, :].rearrange("(w p) f -> p w f", p=P),
                             k.x[:, 0:REAL_WIN - 1, :]).then_inc(wrote, 16)
                sp.dma_start(result[whole:NODES, :], k.x[0:LAST_ROWS, REAL_WIN - 1, :]).then_inc(wrote, 16)
                sp.wait_ge(wrote, 32)


def gnn_kernel(nc, x, src, dst, edge_attr_64, edge_type_8, edge_weight, L0_gnn_W0, L0_gnn_attn_l0, L0_gnn_attn_r0,
               L0_gnn_bias0, L0_gnn_W1, L0_gnn_attn_l1, L0_gnn_attn_r1, L0_gnn_bias1, L1_gnn_W1, L1_gnn_b1,
               L1_gnn_W2, L1_gnn_b2, L2_gnn_W, L2_gnn_b, L3_gnn_weights, out):
    k = Kept()
    k.pool_dma = [nc.alloc_semaphore(f"pool_dma{s}") for s in range(SLOTS)]
    k.pool_dma_count = 0

    def dram(name, shape, dt=F32):
        return nc.dram_tensor(name, shape, dt).ap()

    k.rec_d = dram("rec_d", [P, TILES, DREC])
    k.rec_s = dram("rec_s", [P, TILES, REC])
    k.tile_win = dram("tile_win", [2, TILES], I32)
    k.gat_rows = dram("gat_rows", [ROWS, R_GAT])
    k.gat_edges = dram("gat_edges", [P, TILES, R_GAT])
    nodes_1 = dram("nodes_1", [ROWS, FEAT])
    nodes_2 = dram("nodes_2", [ROWS, FEAT])
    nodes_3 = dram("nodes_3", [ROWS, FEAT + 1])
    nodes_4 = dram("nodes_4", [RELS * ROWS, FEAT])

    with ExitStack() as outer:
        top = Mem(nc, outer, "top")
        constants(nc, k, top)
        k.sorted = {w: top.sb(f"sorted_{w}", [P, TILES, REC]) for w in "ds"}
        k.pair = top.sb("pair", [P, WIN, 2 * HEADS])
        k.per_dst = top.sb("per_dst", [P, WIN])
        k.per_rel = top.sb("per_rel", [P, WIN, RELS])
        sort_edges(nc, k, src, dst, edge_type_8, edge_weight, edge_attr_64)
        load_edges(nc, k)
        k.x = top.sb("x", [P, WIN, FEAT])
        load_nodes(nc, k, x)

        with ExitStack() as ctx:
            m = Mem(nc, ctx, "attention")
            k.h = m.sb("h", [P, WIN, FEAT])
            for n, (w, left, right, bias) in enumerate((
                    (L0_gnn_W0, L0_gnn_attn_l0, L0_gnn_attn_r0, L0_gnn_bias0),
                    (L0_gnn_W1, L0_gnn_attn_l1, L0_gnn_attn_r1, L0_gnn_bias1))):
                attention_rows(nc, k, f"rows{n}", (k.h if n else k.x)[:], w, left, right)
                attention_maxima(nc, k, f"maxima{n}")
                with ExitStack() as sums:
                    k.acc = Mem(nc, sums, f"attend{n}").sb("acc", [P, WIN, R_GAT + 1])
                    weigh, steps = weigh_attention(nc)
                    edge_pass(nc, k, f"attend{n}", "d", R_GAT + 1, weigh, steps, stream=k.gat_edges,
                              row_width=R_GAT, pair=k.pair, func=ACT.Exp, words=HEADS, counts=True)
                    attention_end(nc, k, f"elu{n}", bias, k.h)
            residual_norm(nc, k, "norm0", k.h[:])

        with ExitStack() as ctx:
            m = Mem(nc, ctx, "bilinear")
            both = m.sb("both", [P, WIN, FEAT])
            store_nodes(nc, k, "store1", nodes_1, k.x[:])
            k.acc = m.sb("acc", [P, WIN, FEAT + RELS])
            weigh, steps = weigh_plain(nc, k, True)
            edge_pass(nc, k, "spread1", "s", FEAT + RELS, weigh, steps, table=nodes_1, index=index_first(nc, k, "s"))

            def interact(v, c):
                c.did(nc.vector.tensor_add(both[:], k.x[:], k.acc[:, :, 0:FEAT]))
                c.step(nc.vector.tensor_scalar(k.per_rel[:], k.acc[:, :, FEAT:FEAT + RELS], 1.0, None, ALU.max))
                c.did(nc.vector.reciprocal(k.per_rel[:], k.per_rel[:]))
                c.step(nc.vector.tensor_mul(k.acc[:, :, 0:FEAT], k.x[:], k.acc[:, :, 0:FEAT]))

            store_nodes(nc, k, "store2", nodes_2, k.acc[:, :, 0:FEAT], interact)
            weigh, steps = weigh_plain(nc, k, False)
            edge_pass(nc, k, "spread2", "s", FEAT, weigh, steps, table=nodes_2, index=index_first(nc, k, "s"))
            w12 = m.sb("w12", [P, 2, FEAT])
            load_weights(nc, k, "weights1", w12, (L1_gnn_W1, L1_gnn_W2))
            dense(nc, k, "dense1", [(both, w12[:, 0, :]), (k.acc[:, :, 0:FEAT], w12[:, 1, :])], both,
                  (L1_gnn_b1, L1_gnn_b2))
            residual_norm(nc, k, "norm1", both[:])

        with ExitStack() as ctx:
            m = Mem(nc, ctx, "mean")
            with ExitStack() as table:
                wide = Mem(nc, table, "store3").sb("wide", [P, WIN, FEAT + 1])
                square = Mem(nc, table, "square").sb("wide", [P, WIN, FEAT])

                def with_square(v, c):
                    c.did(nc.vector.tensor_copy(wide[:, :, 0:FEAT], k.x[:]))
                    c.step(nc.vector.tensor_mul(square[:], k.x[:], k.x[:]))
                    c.step(nc.vector.tensor_reduce(wide[:, :, FEAT], square[:], AX, ALU.add))

                store_nodes(nc, k, "store3", nodes_3, wide[:], with_square)
            k.acc = m.sb("acc", [P, WIN, FEAT + ATTR])
            weigh, steps = weigh_normed(nc)
            edge_pass(nc, k, "mean", "d", FEAT + ATTR, weigh, steps, table=nodes_3, index=index_first(nc, k, "d"),
                      row_width=FEAT + 1, attributes=True, func=ACT.Sqrt)
            wt = m.sb("wt", [P, 2, FEAT])
            turn_weights(nc, k, "weights2", wt, [(L2_gnn_W[:, 0:FEAT], wt[:, 0, :]),
                                                 (L2_gnn_W[:, FEAT:FEAT + ATTR], wt[0:ATTR, 1, :])])
            scale_means(nc, k, "means")
            delta = m.sb("delta", [P, WIN, FEAT])
            dense(nc, k, "dense2", [(k.acc[:, :, 0:FEAT], wt[:, 0, :]), (k.acc[:, :, FEAT:], wt[0:ATTR, 1, :])],
                  delta, (L2_gnn_b,))
            residual_norm(nc, k, "norm2", delta[:], normed=True)

        with ExitStack() as ctx:
            m = Mem(nc, ctx, "relations")
            with ExitStack() as table:
                wr = Mem(nc, table, "relations_w").sb("wr", [P, RELS, FEAT])
                turn_weights(nc, k, "weights3", wr, [(L3_gnn_weights[r], wr[:, r, :]) for r in range(RELS)])
                relation_rows(nc, k, "relation_rows", wr, nodes_4)
            k.acc = m.sb("acc", [P, WIN, FEAT])
            weigh, steps = weigh_relation(nc, k)
            edge_pass(nc, k, "relate", "s", FEAT, weigh, steps, table=nodes_4, index=index_relation(nc, k),
                      pair=k.per_rel)

            def relu(v, c):
                c.step(nc.vector.tensor_scalar(k.acc[:], k.acc[:], 0.0, None, ALU.max))

            residual_norm(nc, k, "norm3", k.acc[:], before=relu, result=out)


class Kept:
    pass


def load_weights(nc, k, name, to, weights):
    with ExitStack() as ctx:
        landed = Mem(nc, ctx, name).sem("landed")
        block = ctx.enter_context(nc.Block())

        @block.sync
        def _(sp):
            for n, w in enumerate(weights):
                sp.dma_start(to[:, n, :], w).then_inc(landed, 16)
            sp.wait_ge(landed, 16 * len(weights))


def scale_means(nc, k, name):
    with ExitStack() as ctx:
        chain = Mem(nc, ctx, name).sem("chain")
        block = ctx.enter_context(nc.Block())

        @block.vector
        def _(v):
            c = Chain(v, chain)
            c.step(nc.vector.tensor_mul(k.acc[:], k.acc[:],
                                        k.per_dst[:].unsqueeze(2).broadcast_to([P, WIN, FEAT + ATTR])))


_INS = ["x", "src", "dst", "edge_attr_64", "edge_type_8", "edge_weight", "L0_gnn_W0", "L0_gnn_attn_l0",
        "L0_gnn_attn_r0", "L0_gnn_bias0", "L0_gnn_W1", "L0_gnn_attn_l1", "L0_gnn_attn_r1", "L0_gnn_bias1",
        "L1_gnn_W1", "L1_gnn_b1", "L1_gnn_W2", "L1_gnn_b2", "L2_gnn_W", "L2_gnn_b", "L3_gnn_weights"]


def kernel(**inputs):
    import numpy as np
    from concourse import bacc
    from concourse.bass_utils import run_bass_kernel_spmd

    nc = bacc.Bacc("TRN2", target_bir_lowering=False, num_devices=1)
    arrays, args = {}, []
    for name in _INS:
        a = np.ascontiguousarray(inputs[name])
        arrays[f"in_{name}"] = a
        args.append(nc.dram_tensor(f"in_{name}", a.shape, mybir.dt.from_np(a.dtype), kind="ExternalInput").ap())
    out = nc.dram_tensor("out", (NODES, FEAT), F32, kind="ExternalOutput").ap()
    gnn_kernel(nc, *args, out)
    r = run_bass_kernel_spmd(nc, [arrays], core_ids=[0])
    return r.results[0]["out"]
```

```python
from contextlib import ExitStack

import concourse.bass as bass
from concourse import mybir

F32 = mybir.dt.float32
BF16 = mybir.dt.bfloat16
I32 = mybir.dt.int32
ALU = mybir.AluOpType
ACT = mybir.ActivationFunctionType
AX = mybir.AxisListType.X
At = bass.IndirectOffsetOnAxis

P = 128
NODES, FEAT, HEADS, RELS, ATTR = 6250, 128, 4, 8, 64
DH = FEAT // HEADS
EDGES = 206250

REAL_WIN = -(-NODES // P)
WIN = REAL_WIN + 1
ROWS = WIN * P
PAD_NODE = REAL_WIN * P
LAST_ROWS = NODES - (REAL_WIN - 1) * P

COLS_REAL = -(-EDGES // P)
LAST_COLS = EDGES - (P - 1) * COLS_REAL
SG = 4
COLS = -(-COLS_REAL // SG) * SG + SG
SCAT = COLS // SG

PADS = COLS * P - EDGES
PAIR = 2 * P
G = 8
SLOTS = 4
PAIRS = (EDGES + REAL_WIN * (PAIR - 1)) // PAIR + -(-PADS // PAIR)
GROUPS = -(-PAIRS * 2 // (G * SLOTS)) * SLOTS
TILES = GROUPS * G
GP = G // 2
NOWHERE = 200.0
PCOLS = -(-TILES // 2 // P)

REC = 4
DREC = REC + ATTR
BIG = 1e30
SLOPE = 0.2
R_GAT = FEAT + HEADS


def since(g, n):
    return not isinstance(g, int) or g >= n


def ahead(g, n):
    return not isinstance(g, int) or g + n < GROUPS


def each_group(eng, body, groups=GROUPS):
    rounds = groups // SLOTS
    for g in range(SLOTS):
        body(g, g, 0)
    with eng.Fori(1, rounds - 1) as i:
        for s in range(SLOTS):
            body(i * SLOTS + s, s, i)
    for s in range(groups - groups // SLOTS * SLOTS + SLOTS):
        g = (rounds - 1) * SLOTS + s
        body(g, g % SLOTS, g // SLOTS)


class Chain:

    def __init__(self, eng, sem):
        self.eng, self.sem, self.base, self.n = eng, sem, 0, 0

    def begin(self, base):
        self.base, self.n = base, 0

    def did(self, ins):
        ins.then_inc(self.sem, 1)
        self.n += 1
        return ins

    def wait(self):
        self.eng.wait_ge(self.sem, self.base + self.n)

    def step(self, ins):
        self.did(ins)
        self.wait()


class Mem:

    def __init__(self, nc, ctx, tag):
        self.nc, self.ctx, self.tag, self.sems = nc, ctx, tag, []

    def sb(self, name, shape, dt=F32):
        return self.ctx.enter_context(self.nc.sbuf_tensor(f"{self.tag}_{name}", shape, dt))

    def ps(self, name, shape, dt=F32):
        return self.ctx.enter_context(self.nc.psum_tensor(f"{self.tag}_{name}", shape, dt))

    def sem(self, name):
        if not self.sems:
            self.ctx.callback(self.zero)
        self.sems.append(self.nc.alloc_semaphore(f"{self.tag}_{name}"))
        return self.sems[-1]

    def zero(self):
        with self.nc.Block() as block:
            @block.gpsimd
            def _(pool):
                for s in self.sems:
                    pool.sem_clear(s)
        for s in self.sems:
            self.nc.release_semaphore(s)


def constants(nc, k, top):
    k.ident = top.sb("ident", [P, P])
    k.ident16 = top.sb("ident16", [P, P], BF16)
    k.count = top.sb("count", [P, P])
    k.before = top.sb("before", [P, P])
    k.ones = top.sb("ones", [P, P])
    k.pick = top.sb("pick", [3 * HEADS, HEADS, P], BF16)
    with ExitStack() as ctx:
        m = Mem(nc, ctx, "const")
        made = m.sem("made")
        block = ctx.enter_context(nc.Block())

        @block.gpsimd
        def _(pool):
            c = Chain(pool, made)
            c.step(nc.gpsimd.memset(k.ident[:], 0.0))
            c.step(nc.gpsimd.memset(k.ones[:], 1.0))
            c.step(nc.gpsimd.memset(k.pick[:], 0.0))
            c.step(nc.gpsimd.affine_select(out=k.ident[:], in_=k.ident[:], compare_op=ALU.not_equal, fill=1.0,
                                           base=0, pattern=[[-1, P]], channel_multiplier=1))
            c.step(nc.gpsimd.iota(k.count[:], pattern=[[1, P]], base=0, channel_multiplier=0,
                                  allow_small_or_imprecise_dtypes=True))
            c.step(nc.gpsimd.affine_select(out=k.before[:], in_=k.ones[:], compare_op=ALU.is_gt, fill=0.0,
                                           base=0, pattern=[[1, P]], channel_multiplier=-1))
            for part in range(3):
                c.step(nc.gpsimd.affine_select(out=k.pick[:], in_=k.pick[:], compare_op=ALU.not_equal, fill=1.0,
                                               base=-HEADS * part, pattern=[[-1, HEADS], [0, P]],
                                               channel_multiplier=1))
            c.step(nc.gpsimd.tensor_copy(k.ident16[:], k.ident[:]))


def sort_edges(nc, k, src, dst, etype, ew, attr):
    with ExitStack() as ctx:
        m = Mem(nc, ctx, "sort")
        t = Kept()
        t.win = {w: m.sb(f"win_{w}", [P, COLS]) for w in "ds"}
        t.row_d = m.sb("row_d", [P, COLS], I32)
        t.hit = m.sb("hit", [P, COLS], I32)
        t.high = m.sb("high", [P, COLS], I32)
        t.run = m.sb("run", [P, COLS])
        t.place = m.sb("place", [P, COLS])
        t.total = m.sb("total", [P, WIN])
        t.pairs = m.sb("pairs", [P, WIN])
        t.pairsi = m.sb("pairsi", [P, WIN], I32)
        t.pend = m.sb("pend", [P, WIN])
        t.pstart = m.sb("pstart", [P, WIN])
        t.base = m.sb("base", [P, WIN])
        t.zero = m.sb("zero", [P, WIN])
        t.pair_no = m.sb("pair_no", [P, PCOLS])
        t.le = m.sb("le", [P, PCOLS, WIN])
        t.pw = m.sb("pw", [P, PCOLS])
        t.pwi = m.sb("pwi", [P, 2, PCOLS], I32)
        t.sums = m.ps("sums", [P, 2, 512])
        read_edges(nc, k, t, src, dst, etype, ew)
        scatter_by_dst(nc, k, t, attr)


def rank_sums(nc, k, t, pe, counted, summed):
    pe.wait_ge(counted, 1)
    nc.tensor.matmul(t.sums[:, 0, 0:WIN], k.before[:], t.total[:], start=True, stop=True)
    nc.tensor.matmul(t.sums[:, 1, 0:WIN], k.ones[:], t.total[:], start=True, stop=True).then_inc(summed, 1)


def rank(nc, k, t, v, c, n, rows, chain, counted, summed, tiled, tick):
    win = t.win["ds"[n]]
    start = c.base + c.n
    with v.Fori(0, WIN) as i:
        nc.vector.tensor_scalar(t.run[:], win[:], k.count[:, bass.ds(i, 1)], 0.0, ALU.is_equal, ALU.add,
                                accum_out=t.total[:, bass.ds(i, 1)]).then_inc(chain, 1)
        v.wait_ge(chain, i + (start + 1))
    v.sem_inc(counted, 1)
    c.begin(start + WIN)
    v.wait_ge(summed, 1)
    c.step(nc.vector.tensor_scalar(t.pairsi[:], t.sums[:, 1, 0:WIN], float(PAIR - 1), None, ALU.add))
    c.step(nc.vector.tensor_scalar(t.pairsi[:], t.pairsi[:], 8, None, ALU.arith_shift_right))
    c.step(nc.vector.tensor_copy(t.pairs[:], t.pairsi[:]))
    c.step(nc.vector.tensor_tensor_scan(t.pend[:], t.pairs[:], t.zero[:], 0.0, ALU.add, ALU.add))
    c.step(nc.vector.tensor_sub(t.pstart[:], t.pend[:], t.pairs[:]))
    c.step(nc.vector.scalar_tensor_tensor(t.base[:], t.pstart[:], float(PAIR), t.sums[:, 0, 0:WIN],
                                          ALU.mult, ALU.add))
    c.step(nc.vector.tensor_tensor(t.le[:], t.pstart[:].unsqueeze(1).broadcast_to([P, PCOLS, WIN]),
                                   t.pair_no[:].unsqueeze(2).broadcast_to([P, PCOLS, WIN]), ALU.is_le))
    c.step(nc.vector.tensor_reduce(t.pw[:], t.le[:], AX, ALU.add))
    c.step(nc.vector.tensor_scalar(t.pwi[:, n, :], t.pw[:], -1.0, None, ALU.add))
    v.sem_inc(tiled, 1)
    c.step(nc.vector.memset(t.place[:], 0.0))
    start = c.base + c.n
    with v.Fori(0, WIN) as i:
        done = i * 3 + start
        nc.vector.tensor_scalar(t.hit[:], win[:], k.count[:, bass.ds(i, 1)], None, ALU.is_equal).then_inc(chain, 1)
        v.wait_ge(chain, done + 1)
        nc.vector.tensor_tensor_scan(t.run[:], t.hit[:], t.hit[:], t.base[:, bass.ds(i, 1)],
                                     ALU.add, ALU.max).then_inc(chain, 1)
        v.wait_ge(chain, done + 2)
        v.sem_inc(tick, 1)
        nc.vector.copy_predicated(t.place[:], t.hit[:], t.run[:]).then_inc(chain, 1)
        v.wait_ge(chain, done + 3)
        v.sem_inc(tick, 1)
    c.begin(start + 3 * WIN)
    c.step(nc.vector.tensor_scalar(t.hit[:], t.place[:], -1.0, None, ALU.add))
    c.step(nc.vector.tensor_scalar(t.high[:], t.hit[:], 7, None, ALU.arith_shift_right))
    c.step(nc.vector.tensor_scalar(t.hit[:], t.hit[:], P - 1, None, ALU.bitwise_and))
    c.step(nc.vector.tensor_copy(t.run[:], t.high[:]))
    c.step(nc.vector.tensor_copy(t.place[:], t.hit[:]))
    c.step(nc.vector.scalar_tensor_tensor(rows, t.place[:], float(TILES), t.run[:], ALU.mult, ALU.add))


def read_edges(nc, k, t, src, dst, etype, ew):
    with ExitStack() as ctx:
        m = Mem(nc, ctx, "read")
        raw = {w: m.sb(f"raw_{w}", [P, COLS], I32) for w in ("src", "dst", "rel")}
        weight = m.sb("weight", [P, COLS])
        fill = m.sb("fill", [P, TILES // 64, DREC])
        fill_s = m.sb("fill_s", [P, TILES // 8, REC])
        padded, landed, filled = m.sem("padded"), m.sem("landed"), m.sem("filled")
        counted, summed, tiled, cleared, made, chain, tick = (
            m.sem(x) for x in ("counted", "summed", "tiled", "cleared", "made", "chain", "tick"))
        block = ctx.enter_context(nc.Block())

        @block.sync
        def _(sp):
            sp.wait_ge(padded, 1)
            for name, a in {"dst": dst, "src": src, "rel": etype, "ew": ew}.items():
                to = weight if name == "ew" else raw[name]
                flat = (P - 1) * COLS_REAL
                sp.dma_start(to[0:P - 1, 0:COLS_REAL],
                             a[0:flat].rearrange("(p c) -> p c", p=P - 1)).then_inc(landed, 16)
                sp.dma_start(to[P - 1:P, 0:LAST_COLS],
                             a[flat:EDGES].rearrange("(p c) -> p c", p=1)).then_inc(landed, 16)
            sp.wait_ge(made, 1)
            for j in range(64):
                sp.dma_start(k.rec_d[:, bass.ts(j, TILES // 64), :], fill[:]).then_inc(filled, 16)
            for j in range(8):
                sp.dma_start(k.rec_s[:, bass.ts(j, TILES // 8), :], fill_s[:]).then_inc(filled, 16)
            sp.wait_ge(filled, 16 * (64 + 8))
            sp.wait_ge(landed, 16 * 8)

        @block.tensor
        def _(pe):
            rank_sums(nc, k, t, pe, counted, summed)

        @block.gpsimd
        def _(pool):
            nc.gpsimd.iota(t.pair_no[:], pattern=[[1, PCOLS]], base=0, channel_multiplier=PCOLS,
                           allow_small_or_imprecise_dtypes=True)
            nc.gpsimd.memset(fill_s[:], 0.0)
            nc.gpsimd.memset(fill[:], 0.0).then_inc(cleared, 1)
            pool.wait_ge(cleared, 1)
            nc.gpsimd.memset(fill_s[:, :, 1:2], NOWHERE)
            nc.gpsimd.memset(fill[:, :, 1:2], NOWHERE).then_inc(made, 1)

        @block.vector
        def _(v):
            c = Chain(v, chain)
            for a in (raw["src"], raw["dst"]):
                nc.vector.memset(a[:, COLS_REAL:COLS], PAD_NODE)
                nc.vector.memset(a[P - 32:P, LAST_COLS:COLS_REAL], PAD_NODE)
            for a in (raw["rel"], weight):
                nc.vector.memset(a[:, COLS_REAL:COLS], 0)
                nc.vector.memset(a[P - 32:P, LAST_COLS:COLS_REAL], 0)
            c.did(nc.vector.memset(t.zero[:], 0.0))
            c.wait()
            v.sem_inc(padded, 1)
            v.wait_ge(landed, 16 * 8)
            for w, key, other in (("d", "dst", "src"), ("s", "src", "dst")):
                rec = k.sorted[w]
                c.step(nc.vector.tensor_scalar(t.high[:], raw[key][:], 7, None, ALU.arith_shift_right))
                c.did(nc.vector.tensor_copy(t.run[:], raw[key][:]))
                c.step(nc.vector.tensor_copy(t.win[w][:], t.high[:]))
                c.did(nc.vector.scalar_tensor_tensor(rec[:, 0:COLS, 1], t.win[w][:], -float(P), t.run[:],
                                                     ALU.mult, ALU.add))
                c.did(nc.vector.tensor_copy(rec[:, 0:COLS, 0], raw[other][:]))
                c.did(nc.vector.tensor_copy(rec[:, 0:COLS, 2], weight[:]))
                c.step(nc.vector.tensor_copy(rec[:, 0:COLS, 3], raw["rel"][:]))
            v.wait_ge(made, 1)
            rank(nc, k, t, v, c, 0, t.row_d[:], chain, counted, summed, tiled, tick)


def scatter_by_dst(nc, k, t, attr):
    with ExitStack() as ctx:
        m = Mem(nc, ctx, "scatter")
        out = m.sb("out", [P, SLOTS, SG, DREC])
        where = m.sb("where", [P, SLOTS, SG], I32)
        attr_in = [m.sem(f"attr_in{s}") for s in range(SLOTS)]
        counted, summed, tiled, chain, tick, staged, ptick, wrote = (
            m.sem(x) for x in ("counted", "summed", "tiled", "chain", "tick", "staged", "ptick", "wrote"))
        sent, base = k.pool_dma, k.pool_dma_count
        whole = (P - 1) * COLS_REAL
        attr_a = attr[0:whole, :].rearrange("(p c) f -> p c f", p=P - 1)
        attr_b = attr[whole:EDGES, :].rearrange("(p c) f -> p c f", p=1)
        per_slot = SG * 16
        full = LAST_COLS // SG
        block = ctx.enter_context(nc.Block())

        @block.sync
        def _(sp):
            def body(g, s, u):
                if since(g, SLOTS):
                    sp.wait_ge(sent[s], u * per_slot + base)
                sp.dma_start(out[0:P - 1, s, :, REC:], attr_a[:, bass.ds(g * SG, SG), :]).then_inc(attr_in[s], 16)
                sp.dma_start(out[P - 1:P, s, :, REC:], attr_b[:, bass.ds(g * SG, SG), :]).then_inc(attr_in[s], 16)

            each_group(sp, body, full)
            for g in range(full, SCAT):
                s, u = g % SLOTS, g // SLOTS
                sp.wait_ge(sent[s], u * per_slot + base)
                c0 = g * SG
                for rows, a, n in ((slice(0, P - 1), attr_a, min(SG, COLS_REAL - c0)),
                                   (slice(P - 1, P), attr_b, min(SG, LAST_COLS - c0))):
                    if n > 0:
                        sp.dma_start(out[rows, s, 0:n, REC:], a[:, c0:c0 + n, :]).then_inc(attr_in[s], 16)
                    else:
                        sp.sem_inc(attr_in[s], 16)
            sp.wait_ge(tiled, 1)
            for n in range(2):
                sp.dma_start(k.pair_win[n].rearrange("(p c) -> p c", p=P), t.pwi[:, n, :]).then_inc(wrote, 16)
            sp.wait_ge(wrote, 32)

        @block.gpsimd
        def _(pool):
            def body(g, s, u):
                pool.wait_ge(attr_in[s], (u + 1) * 32)
                pool.sem_inc(ptick, 1)
                nc.gpsimd.tensor_copy(out[:, s, :, 0:REC], k.sorted["d"][:, bass.ds(g * SG, SG), :])
                nc.gpsimd.tensor_copy(where[:, s, :], t.row_d[:, bass.ds(g * SG, SG)]).then_inc(staged, 1)
                pool.wait_ge(staged, g + 1)
                pool.sem_inc(ptick, 1)
                for j in range(SG):
                    nc.gpsimd.indirect_dma_start(k.rec_d.rearrange("p t r -> (p t) r"), At(where[:, s, j:j + 1], 0),
                                                 out[:, s, j, :], None).then_inc(sent[s], 16)

            each_group(pool, body, SCAT)
            for s in range(SLOTS):
                pool.wait_ge(sent[s], SCAT // SLOTS * per_slot + base)

        @block.tensor
        def _(pe):
            rank_sums(nc, k, t, pe, counted, summed)

        @block.vector
        def _(v):
            rank(nc, k, t, v, Chain(v, chain), 1, k.index[:, 0:COLS], chain, counted, summed, tiled, tick)

        k.pool_dma_count += SCAT // SLOTS * per_slot


def scatter_by_src(nc, k, pool, m, first, rounds):
    out = m.sb("scatter_out", [P, SLOTS, SG, REC])
    where = m.sb("scatter_where", [P, SLOTS, SG], I32)
    staged, ptick = m.scatter_sems
    sent, base = k.pool_dma, k.pool_dma_count
    per_slot = SG * 16

    def body(g, s, u):
        if since(g, SLOTS):
            pool.wait_ge(sent[s], u * per_slot + base)
            pool.sem_inc(ptick, 1)
        nc.gpsimd.tensor_copy(out[:, s], k.sorted["s"][:, bass.ds((g + first) * SG, SG), :])
        nc.gpsimd.tensor_copy(where[:, s, :], k.index[:, bass.ds((g + first) * SG, SG)]).then_inc(staged, 1)
        pool.wait_ge(staged, g + 1)
        pool.sem_inc(ptick, 1)
        for j in range(SG):
            nc.gpsimd.indirect_dma_start(k.rec_s.rearrange("p t r -> (p t) r"), At(where[:, s, j:j + 1], 0),
                                         out[:, s, j, :], None).then_inc(sent[s], 16)

    each_group(pool, body, rounds * SLOTS)
    for s in range(SLOTS):
        pool.wait_ge(sent[s], rounds * per_slot + base)
    k.pool_dma_count += rounds * per_slot


def load_edges(nc, k, order):
    table = k.rec_d if order == "d" else k.rec_s
    with ExitStack() as ctx:
        m = Mem(nc, ctx, f"edges_{order}")
        landed = m.sem("landed")
        block = ctx.enter_context(nc.Block())

        @block.sync
        def _(sp):
            for j in range(8):
                part = bass.ts(j, TILES // 8)
                sp.dma_start(k.sorted[order][:, part, :], table[:, part, 0:REC]).then_inc(landed, 16)
            sp.wait_ge(landed, 16 * 8)


def load_nodes(nc, k, x_in):
    with ExitStack() as ctx:
        m = Mem(nc, ctx, "nodes")
        zeroed, landed = m.sem("zeroed"), m.sem("landed")
        block = ctx.enter_context(nc.Block())

        @block.vector
        def _(v):
            nc.vector.memset(k.x[:, REAL_WIN - 1:WIN, :], 0.0).then_inc(zeroed, 1)

        @block.sync
        def _(sp):
            whole = (REAL_WIN - 1) * P
            sp.wait_ge(zeroed, 1)
            sp.dma_start(k.x[:, 0:REAL_WIN - 1, :],
                         x_in[0:whole, :].rearrange("(w p) f -> p w f", p=P)).then_inc(landed, 16)
            sp.dma_start(k.x[0:LAST_ROWS, REAL_WIN - 1, :], x_in[whole:NODES, :]).then_inc(landed, 16)
            sp.wait_ge(landed, 32)


def table_view(table):
    return table.rearrange("(w p) f -> p w f", p=P)


def attention_rows(nc, k, name, nodes, weight, left, right):
    with ExitStack() as ctx:
        m = Mem(nc, ctx, name)
        w = m.sb("w", [P, FEAT])
        sides = m.sb("sides", [P, 2, FEAT])
        turned = m.sb("turned", [P, 2, P])
        out = m.sb("out", [P, WIN, R_GAT])
        prod = m.sb("prod", [P, 2, 2, FEAT])
        ps_t = m.ps("ps_t", [P, 2, 512])
        ps_f = m.ps("ps_f", [P, 2, 512])
        landed, turn, copied, product, used, chain, wrote = (
            m.sem(x) for x in ("landed", "turn", "copied", "product", "used", "chain", "wrote"))
        block = ctx.enter_context(nc.Block())

        @block.sync
        def _(sp):
            sp.dma_start(w[:], weight).then_inc(landed, 16)
            for n, a in enumerate((left, right)):
                sp.dma_start(sides[:, n, :], a.rearrange("h d -> (h d)").unsqueeze(0).broadcast_to([P, FEAT])
                             ).then_inc(landed, 16)
            sp.wait_ge(used, WIN)
            sp.dma_start(table_view(k.gat_rows), out[:]).then_inc(wrote, 16)
            sp.wait_ge(wrote, 16)

        @block.tensor
        def _(pe):
            pe.wait_ge(landed, 48)
            for g in range(WIN + 1):
                if g < WIN:
                    if g >= 2:
                        pe.wait_ge(copied, g - 1)
                    nc.tensor.transpose(ps_t[:, g % 2, 0:P], nodes[:, g, :], k.ident[:]).then_inc(turn, 1)
                if g >= 1:
                    pe.wait_ge(copied, g)
                    if g >= 3:
                        pe.wait_ge(used, g - 2)
                    nc.tensor.matmul(ps_f[:, (g - 1) % 2, 0:FEAT], turned[:, (g - 1) % 2, :], w[:],
                                     start=True, stop=True).then_inc(product, 1)

        @block.scalar
        def _(act):
            for g in range(WIN):
                act.wait_ge(turn, g + 1)
                if g >= 2:
                    act.wait_ge(product, g - 1)
                nc.scalar.copy(turned[:, g % 2, :], ps_t[:, g % 2, 0:P]).then_inc(copied, 1)

        @block.vector
        def _(v):
            c = Chain(v, chain)
            v.wait_ge(landed, 48)
            for g in range(WIN):
                b = g % 2
                f = ps_f[:, b, 0:FEAT]
                v.wait_ge(product, g + 1)
                for n in range(2):
                    c.did(nc.vector.tensor_mul(prod[:, b, n, :], f, sides[:, n, :]))
                c.wait()
                heads = prod[:, b].rearrange("p n (h d) -> p n h d", h=HEADS)
                nc.vector.tensor_reduce(out[:, g, FEAT:R_GAT], heads[:, 0], AX, ALU.add)
                nc.vector.tensor_reduce(k.pair[:, g, 0:HEADS], heads[:, 1], AX, ALU.add)
                nc.vector.tensor_copy(out[:, g, 0:FEAT], f).then_inc(used, 1)


def attention_maxima(nc, k, name):
    with ExitStack() as ctx:
        m = Mem(nc, ctx, name)
        index = m.sb("index", [P, TILES], I32)
        wins = m.sb("wins", [1, TILES // 2], I32)
        slot_index = m.sb("slot_index", [P, SLOTS, G], I32)
        rows = m.sb("rows", [P, SLOTS, G, R_GAT])
        parts = m.sb("parts", [P, 2, G, 3 * HEADS], BF16)
        rest = m.sb("rest", [P, 2, 2, G, HEADS])
        hide = m.sb("hide", [P, 2, G, P], BF16)
        scores = m.sb("scores", [3 * HEADS, 2, G * P], BF16)
        best = m.sb("best", [P, WIN, HEADS])
        tile_best = m.sb("tile_best", [P, 2, GP, 2, HEADS])
        pair_best = m.sb("pair_best", [P, 2, GP, HEADS])
        z = m.sb("z", [P, WIN, HEADS])
        ps_s = m.ps("ps_s", [P, 2, 512])
        ps_z = m.ps("ps_z", [P, 4, HEADS, P])
        made, landed, chain, tick, bested = (m.sem(x) for x in ("made", "landed", "chain", "tick", "bested"))
        indexed = [m.sem(f"indexed{s}") for s in range(SLOTS)]
        gathered, base = k.pool_dma, k.pool_dma_count
        stored = [m.sem(f"stored{s}") for s in range(SLOTS)]
        split, hidden, turned, copied, masked, reduced = (
            m.sem(x) for x in ("split", "hidden", "turned", "copied", "masked", "reduced"))
        ptick, atick, etick, stick = (m.sem(x) for x in ("ptick", "atick", "etick", "stick"))
        regs = [nc.vector.alloc_register(f"{name}_w{q}") for q in range(GP)]
        rec = k.sorted["d"]
        block = ctx.enter_context(nc.Block())

        @block.sync
        def _(sp):
            sp.dma_start(wins[:], k.pair_win[0][0:TILES // 2].unsqueeze(0)).then_inc(landed, 16)
            sp.wait_ge(made, 1)

            def body(g, s, u):
                if since(g, SLOTS):
                    sp.wait_ge(split, g - (SLOTS - 1))
                    sp.sem_inc(stick, 1)
                    sp.wait_ge(stored[s], u * 16)
                    sp.sem_inc(stick, 1)
                sp.dma_start(slot_index[:, s, :], index[:, bass.ds(g * G, G)]).then_inc(indexed[s], 16)

            each_group(sp, body)
            sp.wait_ge(landed, 16)

        @block.gpsimd
        def _(pool):
            def body(g, s, u):
                pool.wait_ge(indexed[s], (u + 1) * 16)
                pool.sem_inc(ptick, 1)
                for t in range(G):
                    nc.gpsimd.indirect_dma_start(rows[:, s, t, :], None, k.gat_rows,
                                                 At(slot_index[:, s, t:t + 1], 0)).then_inc(gathered[s], 16)

            each_group(pool, body)

        @block.scalar
        def _(act):
            def body(g, s, u):
                act.wait_ge(gathered[s], u * (16 * G) + (16 * G + base))
                act.sem_inc(atick, 1)
                act.dma_start(k.gat_edges[:, bass.ds(g * G, G), :], rows[:, s]).then_inc(stored[s], 16)
                if since(g, 2):
                    act.wait_ge(masked, g * G - G)
                    act.sem_inc(atick, 1)
                act.wait_ge(turned, g + 1)
                act.sem_inc(atick, 1)
                nc.scalar.copy(scores[:, s % 2, :], ps_s[0:3 * HEADS].rearrange("p a b -> p (a b)")
                               ).then_inc(copied, 1)

            each_group(act, body)
            for s in range(SLOTS):
                act.wait_ge(stored[s], GROUPS // SLOTS * 16)

        @block.tensor
        def _(pe):
            def body(g, s, u):
                b = s % 2
                pe.wait_ge(split, g + 1)
                pe.sem_inc(etick, 1)
                if since(g, 1):
                    pe.wait_ge(copied, g)
                    pe.sem_inc(etick, 1)
                for t in range(G):
                    last = nc.tensor.matmul(ps_s[0:3 * HEADS, t // 4, bass.ts(t % 4, P)], parts[:, b, t, :],
                                            k.ident16[:], start=True, stop=True)
                last.then_inc(turned, 1)
                pe.wait_ge(hidden, g + 1)
                pe.sem_inc(etick, 1)
                pe.wait_ge(copied, g + 1)
                pe.sem_inc(etick, 1)
                for t in range(G):
                    if since(g, 1) or t >= 4:
                        pe.wait_ge(reduced, g * G + (t - 3))
                        pe.sem_inc(etick, 1)
                    nc.tensor.matmul(ps_z[:, t % 4], hide[:, b, t, :],
                                     k.ident16[:].unsqueeze(1).broadcast_to([P, HEADS, P]), start=True, stop=False)
                    for h in range(HEADS):
                        last = nc.tensor.matmul(ps_z[:, t % 4, h, :], k.pick[:, h, :], scores[:, b, bass.ts(t, P)],
                                                start=False, stop=h == HEADS - 1)
                    last.then_inc(masked, 1)

            each_group(pe, body)

        @block.vector
        def _(v):
            c = Chain(v, chain)
            c.did(nc.vector.memset(best[:], -BIG))
            nc.vector.tensor_copy(index[:], rec[:, :, 0]).then_inc(made, 1)
            v.wait_ge(landed, 16)
            c.wait()
            start, per = c.n, 4

            def reduce(g, s, t):
                v.wait_ge(masked, g * G + (t + 1))
                nc.vector.tensor_reduce(tile_best[:, s % 2, t // 2, t % 2, :], ps_z[:, t % 4], AX,
                                        ALU.max).then_inc(reduced, 1)

            def update(g, s, win):
                b = s % 2
                v.wait_ge(reduced, g * G + G)
                nc.vector.tensor_tensor(pair_best[:, b], tile_best[:, b, :, 0], tile_best[:, b, :, 1],
                                        ALU.max).then_inc(bested, 1)
                for q in range(GP):
                    v.wait_ge(bested, g * (GP + 1) + (q + 1))
                    at = best[:, bass.ds(win[q], 1), :]
                    nc.vector.tensor_tensor(at, at, pair_best[:, b, q:q + 1, :], ALU.max).then_inc(bested, 1)

            def windows(g):
                v.reg_load(regs, wins[0:1, bass.ds(g * GP, GP)])
                return [v.snap(r, min_val=0, max_val=WIN - 1) for r in regs]

            def body(g, s, u):
                b = s % 2
                c.begin(g * per + start)
                if since(g, 1):
                    win = windows(g - 1)
                if since(g, 2):
                    v.wait_ge(masked, g * G - G)
                    v.sem_inc(tick, 1)
                v.wait_ge(gathered[s], u * (16 * G) + (16 * G + base))
                score, r1, r2 = rows[:, s, :, FEAT:R_GAT], rest[:, b, 0], rest[:, b, 1]
                hi, mid, lo = (parts[:, b, :, bass.ts(q, HEADS)] for q in range(3))
                c.step(nc.vector.tensor_copy(hi, score))
                c.step(nc.vector.tensor_sub(r1, score, hi))
                c.step(nc.vector.tensor_copy(mid, r1))
                c.step(nc.vector.tensor_sub(r2, r1, mid))
                nc.vector.tensor_copy(lo, r2).then_inc(split, 1)
                group = rec[:, bass.ds(g * G, G), :]
                for t in range(G):
                    last = nc.vector.tensor_scalar(hide[:, b, t, :], k.count[:], group[:, t, 1:2], -BIG,
                                                   ALU.not_equal, ALU.mult)
                    if t == G - 1:
                        last.then_inc(hidden, 1)
                    if since(g, 1):
                        reduce(g - 1, s - 1, t)
                if since(g, 1):
                    update(g - 1, s - 1, win)

            each_group(v, body)
            g = GROUPS - 1
            for t in range(G):
                reduce(g, g % SLOTS, t)
            update(g, g % SLOTS, windows(g))
            c.begin(GROUPS * per + start)
            v.wait_ge(bested, GROUPS * (GP + 1))
            c.step(nc.vector.tensor_add(z[:], best[:], k.pair[:, :, 0:HEADS]))
            c.step(nc.vector.scalar_tensor_tensor(k.pair[:, :, HEADS:2 * HEADS], z[:], SLOPE, z[:],
                                                  ALU.mult, ALU.max))
        k.pool_dma_count += GROUPS // SLOTS * 16 * G


def edge_pass(nc, k, name, order, width, weigh, steps, *, index=None, table=None, stream=None, row_width=FEAT,
              attributes=False, pair=None, func=None, words=1, counts=False, scatter=None):
    with ExitStack() as ctx:
        m = Mem(nc, ctx, name)
        n_win = 0 if order == "d" else 1
        rec = k.sorted[order]
        wins = m.sb("wins", [1, TILES // 2], I32)
        rows = m.sb("rows", [P, SLOTS, G, row_width])
        hot = m.sb("hot", [P, SLOTS, G, P])
        msg = m.sb("msg", [P, 2, G, width])
        if table is not None:
            slot_index = m.sb("slot_index", [P, SLOTS, G], I32)
        if attributes:
            attrs = m.sb("attrs", [P, SLOTS, G, ATTR])
        if pair is not None:
            hot_t = m.sb("hot_t", [P, 2, G, P], BF16)
            parts = m.sb("parts", [P, WIN, 3, 8], BF16)
            rest = m.sb("rest", [P, 2, WIN, 8])
            own_sum = m.sb("own_sum", [P, 2, G, 8])
            ps_t = m.ps("ps_t", [P, 2, 4, P])
            ps_own = m.ps("ps_own", [P, 2, 512])
        tmp = m.sb("tmp", [P, 2, 4, G, 8])
        per_bank = 512 // width
        banks = -(-GP // per_bank)
        ps_sum = m.ps("ps_sum", [P, 2, banks, 512])
        gathered, base = k.pool_dma, k.pool_dma_count
        loaded = [m.sem(f"loaded{s}") for s in range(SLOTS)]
        loads = (table is None) + attributes
        indexed = [m.sem(f"indexed{s}") for s in range(SLOTS)]
        made, landed, chain = m.sem("made"), m.sem("landed"), m.sem("chain")
        hot_made, turned, copied, owned, asked, raised, weighed, summed, added = (
            m.sem(x) for x in ("hot_made", "turned", "copied", "owned", "asked", "raised", "weighed", "summed",
                               "added"))
        vtick, ptick, atick, etick, stick = (m.sem(x) for x in ("vtick", "ptick", "atick", "etick", "stick"))
        m.scatter_sems = m.sem("staged"), m.sem("scatter_tick")
        vregs = [nc.vector.alloc_register(f"{name}_v{q}") for q in range(GP)]
        block = ctx.enter_context(nc.Block())

        def sums(b, q):
            at = q % per_bank * width
            return ps_sum[:, b, q // per_bank, at:at + width]

        @block.sync
        def _(sp):
            sp.dma_start(wins[:], k.pair_win[n_win][0:TILES // 2].unsqueeze(0)).then_inc(landed, 16)
            sp.wait_ge(made, 1)

            def body(g, s, u):
                if since(g, SLOTS):
                    sp.wait_ge(weighed, g - (SLOTS - 1))
                    sp.sem_inc(stick, 1)
                if table is not None:
                    sp.dma_start(slot_index[:, s, :], k.index[:, bass.ds(g * G, G)]).then_inc(indexed[s], 16)
                else:
                    sp.dma_start(rows[:, s], stream[:, bass.ds(g * G, G), :]).then_inc(loaded[s], 16)
                if attributes:
                    sp.dma_start(attrs[:, s], k.rec_d[:, bass.ds(g * G, G), REC:DREC]).then_inc(loaded[s], 16)

            each_group(sp, body)
            sp.wait_ge(landed, 16)

        if table is not None:
            @block.gpsimd
            def _(pool):
                def body(g, s, u):
                    pool.wait_ge(indexed[s], (u + 1) * 16)
                    pool.sem_inc(ptick, 1)
                    for t in range(G):
                        nc.gpsimd.indirect_dma_start(rows[:, s, t, :], None, table,
                                                     At(slot_index[:, s, t:t + 1], 0)).then_inc(gathered[s], 16)

                each_group(pool, body)
        elif scatter:
            @block.gpsimd
            def _(pool):
                scatter_by_src(nc, k, pool, m, *scatter)

        if pair is not None or func is not None:
            @block.scalar
            def _(act):
                def copy_out(g, b):
                    for half in range(2):
                        act.wait_ge(turned, g * 2 + (half + 1))
                        act.sem_inc(atick, 1)
                        nc.scalar.copy(hot_t[:, b, bass.ts(half, 4), :], ps_t[:, half]).then_inc(copied, 1)

                def body(g, s, u):
                    if pair is not None and not since(g, 1):
                        copy_out(0, 0)
                        copy_out(1, 1)
                    if func is not None:
                        act.wait_ge(asked, g + 1)
                        act.sem_inc(atick, 1)
                        nc.scalar.activation(tmp[:, s % 2, 1, :, 0:words], tmp[:, s % 2, 0, :, 0:words],
                                             func).then_inc(raised, 1)
                    if pair is not None and ahead(g, 2):
                        copy_out(g + 2, s % 2)

                each_group(act, body)

        @block.tensor
        def _(pe):
            pregs = [nc.tensor.alloc_register(f"{name}_p{q}") for q in range(GP)] if pair is not None else None
            pe.wait_ge(landed, 16)

            def turn(g, b):
                pe.wait_ge(hot_made, g + 1)
                pe.sem_inc(etick, 1)
                for half in range(2):
                    if since(g, 1):
                        pe.wait_ge(copied, g * 2 + (half - 1))
                        pe.sem_inc(etick, 1)
                    for t in range(4):
                        last = nc.tensor.transpose(ps_t[:, half, t, :], hot[:, b, 4 * half + t, :], k.ident[:])
                    last.then_inc(turned, 1)

            def look_up(g, b):
                pe.reg_load(pregs, wins[0:1, bass.ds(g * GP, GP)])
                win = [pe.snap(r, min_val=0, max_val=WIN - 1) for r in pregs]
                pe.wait_ge(copied, g * 2 + 2)
                pe.sem_inc(etick, 1)
                for t in range(G):
                    last = nc.tensor.matmul(ps_own[:, b, bass.ts(t, 24)], hot_t[:, b, t, :],
                                            parts[:, bass.ds(win[t // 2], 1), :, :].rearrange("p a c w -> p (a c w)"),
                                            start=True, stop=True)
                last.then_inc(owned, 1)

            def body(g, s, u):
                b = s % 2
                if pair is not None:
                    if not since(g, 1):
                        turn(0, 0)
                        turn(1, 1)
                        look_up(0, 0)
                    if ahead(g, 2):
                        turn(g + 2, (s + 2) % SLOTS)
                    if ahead(g, 1):
                        look_up(g + 1, (s + 1) % 2)
                else:
                    pe.wait_ge(hot_made, g + 1)
                    pe.sem_inc(etick, 1)
                pe.wait_ge(weighed, g + 1)
                pe.sem_inc(etick, 1)
                if since(g, 2):
                    pe.wait_ge(added, g * GP)
                    pe.sem_inc(etick, 1)
                for t in range(G):
                    last = nc.tensor.matmul(sums(b, t // 2), hot[:, s, t, :], msg[:, b, t, :],
                                            start=t % 2 == 0, stop=t % 2 == 1)
                last.then_inc(summed, 1)

            each_group(pe, body)

        @block.vector
        def _(v):
            c = Chain(v, chain)
            nc.vector.memset(k.acc[:, :, 0:width], 0.0).then_inc(added, GP)
            if table is not None:
                index(v, c)
            if counts:
                c.step(nc.vector.memset(msg[:, :, :, width - 1:width], 1.0))
            v.sem_inc(made, 1)
            v.wait_ge(landed, 16)
            v.wait_ge(added, GP)
            if pair is not None:
                for q in range(3):
                    c.step(nc.vector.tensor_copy(parts[:, :, q, :], pair[:] if q == 0 else rest[:, q - 1]))
                    if q < 2:
                        c.step(nc.vector.tensor_sub(rest[:, q], pair[:] if q == 0 else rest[:, 0],
                                                    parts[:, :, q, :]))
            start = c.n

            def windows(g):
                v.reg_load(vregs, wins[0:1, bass.ds(g * GP, GP)])
                return [v.snap(r, min_val=0, max_val=WIN - 1) for r in vregs]

            def add(g, s, q, win):
                at = k.acc[:, bass.ds(win[q], 1), 0:width].rearrange("p a w -> p (a w)")
                v.wait_ge(added, g * GP + (q + GP))
                nc.vector.tensor_add(at, at, sums(s % 2, q)).then_inc(added, 1)

            def mark(g, b, t):
                last = nc.vector.tensor_scalar(hot[:, b, t, :], k.count[:], rec[:, bass.ds(g * G, G), :][:, t, 1:2],
                                               None, ALU.is_equal)
                if t == G - 1:
                    last.then_inc(hot_made, 1)

            own_steps = 1 if pair is not None else 0

            def body(g, s, u):
                b = s % 2
                c.begin(g * (steps + own_steps) + start)
                if not since(g, 1):
                    for t in range(2 * G):
                        mark(t // G, t // G, t % G)
                if since(g, 2):
                    win = windows(g - 2)
                own = None
                if pair is not None:
                    v.wait_ge(owned, g + 1)
                    own = own_sum[:, b]
                    c.step(nc.vector.tensor_reduce(own, ps_own[:, b, 0:24 * G].rearrange(
                        "p (g c w) -> p g w c", c=3, w=8), AX, ALU.add))
                if table is not None:
                    v.wait_ge(gathered[s], u * (16 * G) + (16 * G + base))
                    v.sem_inc(vtick, 1)
                if loads:
                    v.wait_ge(loaded[s], (u + 1) * 16 * loads)
                    v.sem_inc(vtick, 1)

                given = (v, c, msg[:, b], rows[:, s], attrs[:, s] if attributes else None, own,
                         rec[:, bass.ds(g * G, G), :], tmp[:, b])
                if since(g, 2):
                    v.wait_ge(summed, g - 1)
                    v.sem_inc(vtick, 1)
                weigh(0, *given)
                if func is not None:
                    v.sem_inc(asked, 1)
                for t in range(G):
                    if ahead(g, 2):
                        mark(g + 2, (s + 2) % SLOTS, t)
                    if since(g, 2) and t % 2:
                        add(g - 2, s, t // 2, win)
                if func is not None:
                    v.wait_ge(raised, g + 1)
                    v.sem_inc(vtick, 1)
                weigh(1, *given)
                assert c.n == steps + own_steps, (name, c.n)
                v.sem_inc(weighed, 1)

            each_group(v, body)
            for g in (GROUPS - 2, GROUPS - 1):
                win = windows(g)
                v.wait_ge(summed, g + 1)
                v.sem_inc(vtick, 1)
                for q in range(GP):
                    add(g, g % SLOTS, q, win)
            v.wait_ge(added, GROUPS * GP + GP)
        if table is not None:
            k.pool_dma_count += GROUPS // SLOTS * 16 * G


def over(a, n):
    return a.unsqueeze(3).broadcast_to([*a.shape, n])


def weigh_attention(nc):
    def weigh(stage, v, c, msg, rows, attrs, own, rec, tmp):
        score, e, ex = tmp[:, 2, :, 0:HEADS], tmp[:, 0, :, 0:HEADS], tmp[:, 1, :, 0:HEADS]
        exw = tmp[:, 3, :, 0:HEADS]
        if stage == 0:
            c.step(nc.vector.tensor_add(score, rows[:, :, FEAT:R_GAT], own[:, :, 0:HEADS]))
            c.step(nc.vector.scalar_tensor_tensor(score, score, SLOPE, score, ALU.mult, ALU.max))
            c.step(nc.vector.tensor_sub(e, score, own[:, :, HEADS:2 * HEADS]))
            return
        c.step(nc.vector.tensor_mul(exw, ex, rec[:, :, 2:3].broadcast_to([P, G, HEADS])))
        c.did(nc.vector.tensor_mul(msg[:, :, 0:FEAT].rearrange("p g (h d) -> p g h d", h=HEADS),
                                   rows[:, :, 0:FEAT].rearrange("p g (h d) -> p g h d", h=HEADS), over(exw, DH)))
        c.step(nc.vector.tensor_copy(msg[:, :, FEAT:R_GAT], ex))
    return weigh, 6


def weigh_plain(nc, k, relations):
    def weigh(stage, v, c, msg, rows, attrs, own, rec, tmp):
        if stage == 0:
            return
        c.did(nc.vector.tensor_mul(msg[:, :, 0:FEAT], rows, rec[:, :, 2:3].broadcast_to([P, G, FEAT])))
        if relations:
            c.did(nc.vector.tensor_tensor(msg[:, :, FEAT:FEAT + RELS], rec[:, :, 3:4].broadcast_to([P, G, RELS]),
                                          k.count[:, 0:RELS].unsqueeze(1).broadcast_to([P, G, RELS]), ALU.is_equal))
        c.wait()
    return weigh, 1 + relations


def attention_end(nc, k, name, bias_in, out):
    with ExitStack() as ctx:
        m = Mem(nc, ctx, name)
        bias = m.sb("bias", [P, FEAT])
        inv = m.sb("inv", [P, WIN, HEADS])
        low = m.sb("low", [P, WIN, FEAT])
        landed, chain, asked, raised = (m.sem(x) for x in ("landed", "chain", "asked", "raised"))
        block = ctx.enter_context(nc.Block())

        @block.sync
        def _(sp):
            sp.dma_start(bias[:], bias_in.unsqueeze(0).broadcast_to([P, FEAT])).then_inc(landed, 16)
            sp.wait_ge(landed, 16)

        @block.scalar
        def _(act):
            act.wait_ge(asked, 1)
            nc.scalar.activation(low[:], low[:], ACT.Exp).then_inc(raised, 1)

        @block.vector
        def _(v):
            c = Chain(v, chain)
            v.wait_ge(landed, 16)
            c.step(nc.vector.tensor_scalar(k.per_dst[:], k.acc[:, :, R_GAT], 1.0, None, ALU.max))
            c.step(nc.vector.reciprocal(k.per_dst[:], k.per_dst[:]))
            c.step(nc.vector.tensor_scalar(inv[:], k.acc[:, :, FEAT:R_GAT], 1e-20, None, ALU.max))
            c.step(nc.vector.reciprocal(inv[:], inv[:]))
            heads = lambda a: a.rearrange("p w (h d) -> p w h d", h=HEADS)
            c.step(nc.vector.tensor_mul(heads(out[:]), heads(k.acc[:, :, 0:FEAT]), over(inv[:], DH)))
            c.step(nc.vector.tensor_add(out[:], out[:], bias[:].unsqueeze(1).broadcast_to([P, WIN, FEAT])))
            c.step(nc.vector.tensor_scalar(low[:], out[:], 0.0, None, ALU.min))
            v.sem_inc(asked, 1)
            v.wait_ge(raised, 1)
            c.step(nc.vector.tensor_scalar(low[:], low[:], -1.0, None, ALU.add))
            c.step(nc.vector.scalar_tensor_tensor(out[:], out[:], 0.0, low[:], ALU.max, ALU.add))


def weigh_normed(nc):
    def weigh(stage, v, c, msg, rows, attrs, own, rec, tmp):
        squares, inv = tmp[:, 0, :, 0:1], tmp[:, 2, :, 0:1]
        if stage == 0:
            c.step(nc.vector.tensor_mul(msg[:, :, FEAT:FEAT + ATTR], attrs, attrs))
            c.step(nc.vector.tensor_reduce(tmp[:, 0, :, 0], msg[:, :, FEAT:FEAT + ATTR], AX, ALU.add))
            c.step(nc.vector.tensor_add(squares, squares, rows[:, :, FEAT:FEAT + 1]))
            return
        c.step(nc.vector.tensor_scalar(inv, tmp[:, 1, :, 0:1], 1e-12, None, ALU.max))
        c.step(nc.vector.reciprocal(inv, inv))
        c.did(nc.vector.tensor_mul(msg[:, :, 0:FEAT], rows[:, :, 0:FEAT], inv.broadcast_to([P, G, FEAT])))
        c.step(nc.vector.tensor_mul(msg[:, :, FEAT:FEAT + ATTR], attrs, inv.broadcast_to([P, G, ATTR])))
    return weigh, 7


def weigh_relation(nc, k):
    def weigh(stage, v, c, msg, rows, attrs, own, rec, tmp):
        if stage == 0:
            return
        c.step(nc.vector.tensor_tensor(tmp[:, 0], rec[:, :, 3:4].broadcast_to([P, G, RELS]),
                                       k.count[:, 0:RELS].unsqueeze(1).broadcast_to([P, G, RELS]), ALU.is_equal))
        c.step(nc.vector.tensor_mul(tmp[:, 1], tmp[:, 0], own))
        c.step(nc.vector.tensor_reduce(tmp[:, 2, :, 0], tmp[:, 1], AX, ALU.add))
        c.step(nc.vector.tensor_mul(msg, rows, tmp[:, 2, :, 0:1].broadcast_to([P, G, FEAT])))
    return weigh, 4


def index_first(nc, k, order):
    def index(v, c):
        c.step(nc.vector.tensor_copy(k.index[:], k.sorted[order][:, :, 0]))
    return index


def index_relation(nc, k):
    def index(v, c):
        rec = k.sorted["s"]
        c.step(nc.vector.scalar_tensor_tensor(k.index[:], rec[:, :, 3], float(ROWS), rec[:, :, 0], ALU.mult, ALU.add))
    return index


def store_nodes(nc, k, name, table, nodes, combine=None):
    with ExitStack() as ctx:
        m = Mem(nc, ctx, name)
        chain, ready, wrote = (m.sem(x) for x in ("chain", "ready", "wrote"))
        block = ctx.enter_context(nc.Block())

        @block.vector
        def _(v):
            if combine:
                combine(v, Chain(v, chain))
            v.sem_inc(ready, 1)

        @block.sync
        def _(sp):
            sp.wait_ge(ready, 1)
            sp.dma_start(table_view(table), nodes).then_inc(wrote, 16)
            sp.wait_ge(wrote, 16)


def turn_weights(nc, k, name, out, pieces):
    with ExitStack() as ctx:
        m = Mem(nc, ctx, name)
        raw = m.sb("raw", [P, len(pieces), P])
        ps = m.ps("ps", [P, 2, 512])
        landed, turned, copied = (m.sem(x) for x in ("landed", "turned", "copied"))
        block = ctx.enter_context(nc.Block())

        @block.sync
        def _(sp):
            for n, (a, _) in enumerate(pieces):
                sp.dma_start(raw[:, n, 0:a.shape[1]], a).then_inc(landed, 16)

        @block.tensor
        def _(pe):
            pe.wait_ge(landed, 16 * len(pieces))
            for n, (a, _) in enumerate(pieces):
                if n >= 2:
                    pe.wait_ge(copied, n - 1)
                nc.tensor.transpose(ps[0:a.shape[1], n % 2, 0:P], raw[:, n, 0:a.shape[1]], k.ident[:]
                                    ).then_inc(turned, 1)

        @block.vector
        def _(v):
            for n, (a, to) in enumerate(pieces):
                v.wait_ge(turned, n + 1)
                nc.vector.tensor_copy(to, ps[0:a.shape[1], n % 2, 0:P]).then_inc(copied, 1)
            v.wait_ge(copied, len(pieces))


def dense(nc, k, name, terms, out, biases):
    n_terms = len(terms)
    with ExitStack() as ctx:
        m = Mem(nc, ctx, name)
        turned = m.sb("turned", [P, 2, n_terms, P])
        bias = m.sb("bias", [P, len(biases), FEAT])
        ps_t = m.ps("ps_t", [P, 2, 4, P])
        ps_o = m.ps("ps_o", [P, 2, 512])
        landed, turn, copied, product, used, chain = (
            m.sem(x) for x in ("landed", "turn", "copied", "product", "used", "chain"))
        block = ctx.enter_context(nc.Block())

        @block.sync
        def _(sp):
            for n, a in enumerate(biases):
                sp.dma_start(bias[:, n, :], a.unsqueeze(0).broadcast_to([P, FEAT])).then_inc(landed, 16)

        @block.tensor
        def _(pe):
            for g in range(WIN + 1):
                if g < WIN:
                    if g >= 2:
                        pe.wait_ge(copied, g - 1)
                    for n, (nodes, w) in enumerate(terms):
                        last = nc.tensor.transpose(ps_t[0:nodes.shape[2], g % 2, n, :], nodes[:, g, :], k.ident[:])
                    last.then_inc(turn, 1)
                if g >= 1:
                    pe.wait_ge(copied, g)
                    if g >= 3:
                        pe.wait_ge(used, g - 2)
                    for n, (nodes, w) in enumerate(terms):
                        last = nc.tensor.matmul(ps_o[:, (g - 1) % 2, 0:FEAT],
                                                turned[0:nodes.shape[2], (g - 1) % 2, n, :], w,
                                                start=n == 0, stop=n == n_terms - 1)
                    last.then_inc(product, 1)

        @block.scalar
        def _(act):
            for g in range(WIN):
                act.wait_ge(turn, g + 1)
                if g >= 2:
                    act.wait_ge(product, g - 1)
                for n, (nodes, w) in enumerate(terms):
                    q = nodes.shape[2]
                    last = nc.scalar.copy(turned[0:q, g % 2, n, :], ps_t[0:q, g % 2, n, :])
                last.then_inc(copied, 1)

        @block.vector
        def _(v):
            c = Chain(v, chain)
            v.wait_ge(landed, 16 * len(biases))
            for n in range(1, len(biases)):
                c.step(nc.vector.tensor_add(bias[:, 0, :], bias[:, 0, :], bias[:, n, :]))
            for g in range(WIN):
                v.wait_ge(product, g + 1)
                nc.vector.tensor_add(out[:, g, :], ps_o[:, g % 2, 0:FEAT], bias[:, 0, :]).then_inc(used, 1)
            v.wait_ge(used, WIN)


def relation_rows(nc, k, name, weights, table):
    with ExitStack() as ctx:
        m = Mem(nc, ctx, name)
        turned = m.sb("turned", [P, 2, P])
        out = m.sb("out", [P, 2, RELS, FEAT])
        ps_t = m.ps("ps_t", [P, 2, 512])
        ps_o = m.ps("ps_o", [P, 2, 2, 512])
        turn, copied, product, used_a, used_v = (
            m.sem(x) for x in ("turn", "copied", "product", "used_a", "used_v"))
        wrote = [m.sem(f"wrote{b}") for b in range(2)]
        to = table.rearrange("(r w p) f -> p w r f", p=P, r=RELS)
        half = RELS // 2
        block = ctx.enter_context(nc.Block())

        @block.tensor
        def _(pe):
            for g in range(WIN + 1):
                if g < WIN:
                    if g >= 2:
                        pe.wait_ge(copied, g - 1)
                    nc.tensor.transpose(ps_t[:, g % 2, 0:P], k.x[:, g, :], k.ident[:]).then_inc(turn, 1)
                if g >= 1:
                    pe.wait_ge(copied, g)
                    if g >= 3:
                        pe.wait_ge(used_a, g - 2)
                        pe.wait_ge(used_v, g - 2)
                    for q in range(2):
                        last = nc.tensor.matmul(ps_o[:, (g - 1) % 2, q, :], turned[:, (g - 1) % 2, :],
                                                weights[:, half * q:half * (q + 1), :].rearrange("p r f -> p (r f)"),
                                                start=True, stop=True)
                    last.then_inc(product, 1)

        @block.scalar
        def _(act):
            for g in range(WIN + 1):
                if g < WIN:
                    act.wait_ge(turn, g + 1)
                    if g >= 2:
                        act.wait_ge(product, g - 1)
                    nc.scalar.copy(turned[:, g % 2, :], ps_t[:, g % 2, 0:P]).then_inc(copied, 1)
                if g >= 1:
                    b = (g - 1) % 2
                    act.wait_ge(product, g)
                    if g >= 3:
                        act.wait_ge(wrote[b], 16 * ((g - 1) // 2))
                    nc.scalar.copy(out[:, b, half:RELS, :].rearrange("p r f -> p (r f)"), ps_o[:, b, 1, :]
                                   ).then_inc(used_a, 1)

        @block.vector
        def _(v):
            for g in range(WIN):
                b = g % 2
                v.wait_ge(product, g + 1)
                if g >= 2:
                    v.wait_ge(wrote[b], 16 * (g // 2))
                nc.vector.tensor_copy(out[:, b, 0:half, :].rearrange("p r f -> p (r f)"), ps_o[:, b, 0, :]
                                      ).then_inc(used_v, 1)

        @block.sync
        def _(sp):
            for g in range(WIN):
                sp.wait_ge(used_a, g + 1)
                sp.wait_ge(used_v, g + 1)
                sp.dma_start(to[:, g], out[:, g % 2]).then_inc(wrote[g % 2], 16)
            for b in range(2):
                sp.wait_ge(wrote[b], 16 * (WIN // 2))


def residual_norm(nc, k, name, delta, before=None, result=None, normed=False):
    with ExitStack() as ctx:
        m = Mem(nc, ctx, name)
        squares = m.sb("squares", [P, WIN, FEAT])
        stat = m.sb("stat", [P, 3, WIN])
        chain, asked, raised, ready, wrote = (m.sem(x) for x in ("chain", "asked", "raised", "ready", "wrote"))
        block = ctx.enter_context(nc.Block())
        wide = lambda a: a.unsqueeze(2).broadcast_to([P, WIN, FEAT])

        @block.scalar
        def _(act):
            for n in range(1 + normed):
                act.wait_ge(asked, n + 1)
                nc.scalar.activation(stat[:, 2, :], stat[:, 1, :], ACT.Sqrt).then_inc(raised, 1)

        @block.vector
        def _(v):
            c = Chain(v, chain)
            if before:
                before(v, c)
            if normed:
                c.step(nc.vector.tensor_mul(squares[:], delta, delta))
                c.step(nc.vector.tensor_reduce(stat[:, 1, :], squares[:], AX, ALU.add))
                v.sem_inc(asked, 1)
                v.wait_ge(raised, 1)
                c.step(nc.vector.tensor_scalar(stat[:, 0, :], stat[:, 2, :], 1e-12, None, ALU.max))
                c.step(nc.vector.reciprocal(stat[:, 0, :], stat[:, 0, :]))
                c.step(nc.vector.tensor_mul(delta, delta, wide(stat[:, 0, :])))
            c.step(nc.vector.tensor_add(k.x[:], k.x[:], delta))
            c.step(nc.vector.tensor_reduce(stat[:, 0, :], k.x[:], AX, ALU.add))
            c.step(nc.vector.tensor_scalar(stat[:, 0, :], stat[:, 0, :], 1.0 / FEAT, None, ALU.mult))
            c.step(nc.vector.tensor_sub(k.x[:], k.x[:], wide(stat[:, 0, :])))
            c.step(nc.vector.tensor_mul(squares[:], k.x[:], k.x[:]))
            c.step(nc.vector.tensor_reduce(stat[:, 1, :], squares[:], AX, ALU.add))
            c.step(nc.vector.tensor_scalar(stat[:, 1, :], stat[:, 1, :], 1.0 / FEAT, 1e-5, ALU.mult, ALU.add))
            v.sem_inc(asked, 1)
            v.wait_ge(raised, 1 + normed)
            c.step(nc.vector.reciprocal(stat[:, 0, :], stat[:, 2, :]))
            c.step(nc.vector.tensor_mul(k.x[:], k.x[:], wide(stat[:, 0, :])))
            v.sem_inc(ready, 1)

        if result is not None:
            @block.sync
            def _(sp):
                sp.wait_ge(ready, 1)
                whole = (REAL_WIN - 1) * P
                sp.dma_start(result[0:whole, :].rearrange("(w p) f -> p w f", p=P),
                             k.x[:, 0:REAL_WIN - 1, :]).then_inc(wrote, 16)
                sp.dma_start(result[whole:NODES, :], k.x[0:LAST_ROWS, REAL_WIN - 1, :]).then_inc(wrote, 16)
                sp.wait_ge(wrote, 32)


def gnn_kernel(nc, x, src, dst, edge_attr_64, edge_type_8, edge_weight, L0_gnn_W0, L0_gnn_attn_l0, L0_gnn_attn_r0,
               L0_gnn_bias0, L0_gnn_W1, L0_gnn_attn_l1, L0_gnn_attn_r1, L0_gnn_bias1, L1_gnn_W1, L1_gnn_b1,
               L1_gnn_W2, L1_gnn_b2, L2_gnn_W, L2_gnn_b, L3_gnn_weights, out):
    k = Kept()
    k.pool_dma = [nc.alloc_semaphore(f"pool_dma{s}") for s in range(SLOTS)]
    k.pool_dma_count = 0

    def dram(name, shape, dt=F32):
        return nc.dram_tensor(name, shape, dt).ap()

    k.rec_d = dram("rec_d", [P, TILES, DREC])
    k.rec_s = dram("rec_s", [P, TILES, REC])
    k.pair_win = dram("pair_win", [2, P * PCOLS], I32)
    k.gat_rows = dram("gat_rows", [ROWS, R_GAT])
    k.gat_edges = dram("gat_edges", [P, TILES, R_GAT])
    nodes_1 = dram("nodes_1", [ROWS, FEAT])
    nodes_2 = dram("nodes_2", [ROWS, FEAT])
    nodes_3 = dram("nodes_3", [ROWS, FEAT + 1])
    nodes_4 = dram("nodes_4", [RELS * ROWS, FEAT])

    with ExitStack() as outer:
        top = Mem(nc, outer, "top")
        constants(nc, k, top)
        k.sorted = {w: top.sb(f"sorted_{w}", [P, TILES, REC]) for w in "ds"}
        k.pair = top.sb("pair", [P, WIN, 2 * HEADS])
        k.per_dst = top.sb("per_dst", [P, WIN])
        k.per_rel = top.sb("per_rel", [P, WIN, RELS])
        k.index = top.sb("index", [P, TILES], I32)
        sort_edges(nc, k, src, dst, edge_type_8, edge_weight, edge_attr_64)
        load_edges(nc, k, "d")
        k.x = top.sb("x", [P, WIN, FEAT])
        load_nodes(nc, k, x)

        with ExitStack() as ctx:
            m = Mem(nc, ctx, "attention")
            k.h = m.sb("h", [P, WIN, FEAT])
            half = -(-SCAT // SLOTS // 2)
            for n, (w, left, right, bias) in enumerate((
                    (L0_gnn_W0, L0_gnn_attn_l0, L0_gnn_attn_r0, L0_gnn_bias0),
                    (L0_gnn_W1, L0_gnn_attn_l1, L0_gnn_attn_r1, L0_gnn_bias1))):
                attention_rows(nc, k, f"rows{n}", (k.h if n else k.x)[:], w, left, right)
                attention_maxima(nc, k, f"maxima{n}")
                with ExitStack() as sums:
                    k.acc = Mem(nc, sums, f"attend{n}").sb("acc", [P, WIN, R_GAT + 1])
                    weigh, steps = weigh_attention(nc)
                    edge_pass(nc, k, f"attend{n}", "d", R_GAT + 1, weigh, steps, stream=k.gat_edges,
                              row_width=R_GAT, pair=k.pair, func=ACT.Exp, words=HEADS, counts=True,
                              scatter=[(0, half), (half * SLOTS, SCAT // SLOTS - half)][n])
                    attention_end(nc, k, f"elu{n}", bias, k.h)
            load_edges(nc, k, "s")
            residual_norm(nc, k, "norm0", k.h[:])

        with ExitStack() as ctx:
            m = Mem(nc, ctx, "bilinear")
            both = m.sb("both", [P, WIN, FEAT])
            store_nodes(nc, k, "store1", nodes_1, k.x[:])
            k.acc = m.sb("acc", [P, WIN, FEAT + RELS])
            weigh, steps = weigh_plain(nc, k, True)
            edge_pass(nc, k, "spread1", "s", FEAT + RELS, weigh, steps, table=nodes_1, index=index_first(nc, k, "s"))

            def interact(v, c):
                c.did(nc.vector.tensor_add(both[:], k.x[:], k.acc[:, :, 0:FEAT]))
                c.step(nc.vector.tensor_scalar(k.per_rel[:], k.acc[:, :, FEAT:FEAT + RELS], 1.0, None, ALU.max))
                c.did(nc.vector.reciprocal(k.per_rel[:], k.per_rel[:]))
                c.step(nc.vector.tensor_mul(k.acc[:, :, 0:FEAT], k.x[:], k.acc[:, :, 0:FEAT]))

            store_nodes(nc, k, "store2", nodes_2, k.acc[:, :, 0:FEAT], interact)
            weigh, steps = weigh_plain(nc, k, False)
            edge_pass(nc, k, "spread2", "s", FEAT, weigh, steps, table=nodes_2, index=index_first(nc, k, "s"))
            w12 = m.sb("w12", [P, 2, FEAT])
            load_weights(nc, k, "weights1", w12, (L1_gnn_W1, L1_gnn_W2))
            dense(nc, k, "dense1", [(both, w12[:, 0, :]), (k.acc[:, :, 0:FEAT], w12[:, 1, :])], both,
                  (L1_gnn_b1, L1_gnn_b2))
            residual_norm(nc, k, "norm1", both[:])

        with ExitStack() as ctx:
            m = Mem(nc, ctx, "mean")
            with ExitStack() as table:
                wide = Mem(nc, table, "store3").sb("wide", [P, WIN, FEAT + 1])
                square = Mem(nc, table, "square").sb("wide", [P, WIN, FEAT])

                def with_square(v, c):
                    c.did(nc.vector.tensor_copy(wide[:, :, 0:FEAT], k.x[:]))
                    c.step(nc.vector.tensor_mul(square[:], k.x[:], k.x[:]))
                    c.step(nc.vector.tensor_reduce(wide[:, :, FEAT], square[:], AX, ALU.add))

                store_nodes(nc, k, "store3", nodes_3, wide[:], with_square)
            k.acc = m.sb("acc", [P, WIN, FEAT + ATTR])
            weigh, steps = weigh_normed(nc)
            edge_pass(nc, k, "mean", "d", FEAT + ATTR, weigh, steps, table=nodes_3, index=index_first(nc, k, "d"),
                      row_width=FEAT + 1, attributes=True, func=ACT.Sqrt)
            wt = m.sb("wt", [P, 2, FEAT])
            turn_weights(nc, k, "weights2", wt, [(L2_gnn_W[:, 0:FEAT], wt[:, 0, :]),
                                                 (L2_gnn_W[:, FEAT:FEAT + ATTR], wt[0:ATTR, 1, :])])
            scale_means(nc, k, "means")
            delta = m.sb("delta", [P, WIN, FEAT])
            dense(nc, k, "dense2", [(k.acc[:, :, 0:FEAT], wt[:, 0, :]), (k.acc[:, :, FEAT:], wt[0:ATTR, 1, :])],
                  delta, (L2_gnn_b,))
            residual_norm(nc, k, "norm2", delta[:], normed=True)

        with ExitStack() as ctx:
            m = Mem(nc, ctx, "relations")
            with ExitStack() as table:
                wr = Mem(nc, table, "relations_w").sb("wr", [P, RELS, FEAT])
                turn_weights(nc, k, "weights3", wr, [(L3_gnn_weights[r], wr[:, r, :]) for r in range(RELS)])
                relation_rows(nc, k, "relation_rows", wr, nodes_4)
            k.acc = m.sb("acc", [P, WIN, FEAT])
            weigh, steps = weigh_relation(nc, k)
            edge_pass(nc, k, "relate", "s", FEAT, weigh, steps, table=nodes_4, index=index_relation(nc, k),
                      pair=k.per_rel)

            def relu(v, c):
                c.step(nc.vector.tensor_scalar(k.acc[:], k.acc[:], 0.0, None, ALU.max))

            residual_norm(nc, k, "norm3", k.acc[:], before=relu, result=out)


class Kept:
    pass


def load_weights(nc, k, name, to, weights):
    with ExitStack() as ctx:
        landed = Mem(nc, ctx, name).sem("landed")
        block = ctx.enter_context(nc.Block())

        @block.sync
        def _(sp):
            for n, w in enumerate(weights):
                sp.dma_start(to[:, n, :], w).then_inc(landed, 16)
            sp.wait_ge(landed, 16 * len(weights))


def scale_means(nc, k, name):
    with ExitStack() as ctx:
        chain = Mem(nc, ctx, name).sem("chain")
        block = ctx.enter_context(nc.Block())

        @block.vector
        def _(v):
            c = Chain(v, chain)
            c.step(nc.vector.tensor_mul(k.acc[:], k.acc[:],
                                        k.per_dst[:].unsqueeze(2).broadcast_to([P, WIN, FEAT + ATTR])))


_INS = ["x", "src", "dst", "edge_attr_64", "edge_type_8", "edge_weight", "L0_gnn_W0", "L0_gnn_attn_l0",
        "L0_gnn_attn_r0", "L0_gnn_bias0", "L0_gnn_W1", "L0_gnn_attn_l1", "L0_gnn_attn_r1", "L0_gnn_bias1",
        "L1_gnn_W1", "L1_gnn_b1", "L1_gnn_W2", "L1_gnn_b2", "L2_gnn_W", "L2_gnn_b", "L3_gnn_weights"]


def kernel(**inputs):
    import numpy as np
    from concourse import bacc
    from concourse.bass_utils import run_bass_kernel_spmd

    nc = bacc.Bacc("TRN2", target_bir_lowering=False, num_devices=1)
    arrays, args = {}, []
    for name in _INS:
        a = np.ascontiguousarray(inputs[name])
        arrays[f"in_{name}"] = a
        args.append(nc.dram_tensor(f"in_{name}", a.shape, mybir.dt.from_np(a.dtype), kind="ExternalInput").ap())
    out = nc.dram_tensor("out", (NODES, FEAT), F32, kind="ExternalOutput").ap()
    gnn_kernel(nc, *args, out)
    r = run_bass_kernel_spmd(nc, [arrays], core_ids=[0])
    return r.results[0]["out"]
```

```python
from contextlib import ExitStack

import concourse.bass as bass
from concourse import mybir

F32 = mybir.dt.float32
BF16 = mybir.dt.bfloat16
I32 = mybir.dt.int32
ALU = mybir.AluOpType
ACT = mybir.ActivationFunctionType
AX = mybir.AxisListType.X
At = bass.IndirectOffsetOnAxis

P = 128
NODES, FEAT, HEADS, RELS, ATTR = 6250, 128, 4, 8, 64
DH = FEAT // HEADS
EDGES = 206250

REAL_WIN = -(-NODES // P)
WIN = REAL_WIN + 1
ROWS = WIN * P
PAD_NODE = REAL_WIN * P
LAST_ROWS = NODES - (REAL_WIN - 1) * P

COLS_REAL = -(-EDGES // P)
LAST_COLS = EDGES - (P - 1) * COLS_REAL
SG = 4
COLS = -(-COLS_REAL // SG) * SG + SG
SCAT = COLS // SG

PADS = COLS * P - EDGES
PAIR = 2 * P
G = 8
SLOTS = 4
PAIRS = (EDGES + REAL_WIN * (PAIR - 1)) // PAIR + -(-PADS // PAIR)
GROUPS = -(-PAIRS * 2 // (G * SLOTS)) * SLOTS
TILES = GROUPS * G
GP = G // 2
SHARES = (0, GROUPS * 7 // 20, GROUPS * 14 // 20, GROUPS)
NOWHERE = 200.0
PAIRS_ALL = TILES // 2
PCOLS = -(-PAIRS_ALL // P)

REC = 4
DREC = REC + ATTR
BIG = 1e30
SLOPE = 0.2
R_GAT = FEAT + HEADS


def since(g, n):
    return not isinstance(g, int) or g >= n


def ahead(g, n):
    return not isinstance(g, int) or g + n < GROUPS


def each_group(eng, body, groups=GROUPS, before=None):
    rounds = groups // SLOTS
    before = before or (lambda g: None)
    before(0)
    for g in range(SLOTS):
        body(g, g, 0)
    with eng.Fori(1, rounds - 1) as i:
        before(i * SLOTS)
        for s in range(SLOTS):
            body(i * SLOTS + s, s, i)
    before((rounds - 1) * SLOTS)
    for s in range(groups - groups // SLOTS * SLOTS + SLOTS):
        g = (rounds - 1) * SLOTS + s
        body(g, g % SLOTS, g // SLOTS)


class Windows:

    PADS = SLOTS * GP

    def __init__(self, eng, wins, name, shift):
        self.eng, self.wins, self.shift = eng, wins, shift
        self.regs = [eng.alloc_register(f"{name}{q}") for q in range(GP * SLOTS)]

    @staticmethod
    def load(nc, m, sp, wins, table, landed, padded):
        sp.wait_ge(padded, 1)
        sp.dma_start(wins[:, Windows.PADS:Windows.PADS + TILES // 2], table[0:TILES // 2].unsqueeze(0)
                     ).then_inc(landed, 16)

    def take(self, g):
        self.eng.reg_load(self.regs, self.wins[0:1, bass.ds(g * GP + (self.PADS + self.shift * GP), GP * SLOTS)])
        self.at = [self.eng.snap(r, min_val=0, max_val=WIN - 1) for r in self.regs]

    def of(self, s):
        return self.at[s * GP:(s + 1) * GP]


class Chain:

    def __init__(self, eng, sem):
        self.eng, self.sem, self.base, self.n = eng, sem, 0, 0

    def begin(self, base):
        self.base, self.n = base, 0

    def did(self, ins):
        ins.then_inc(self.sem, 1)
        self.n += 1
        return ins

    def wait(self):
        self.eng.wait_ge(self.sem, self.base + self.n)

    def step(self, ins, between=None):
        self.did(ins)
        if between:
            between()
        self.wait()


class Mem:

    def __init__(self, nc, ctx, tag):
        self.nc, self.ctx, self.tag, self.sems = nc, ctx, tag, []

    def sb(self, name, shape, dt=F32):
        return self.ctx.enter_context(self.nc.sbuf_tensor(f"{self.tag}_{name}", shape, dt))

    def ps(self, name, shape, dt=F32):
        return self.ctx.enter_context(self.nc.psum_tensor(f"{self.tag}_{name}", shape, dt))

    def sem(self, name):
        if not self.sems:
            self.ctx.callback(self.zero)
        self.sems.append(self.nc.alloc_semaphore(f"{self.tag}_{name}"))
        return self.sems[-1]

    def zero(self):
        with self.nc.Block() as block:
            @block.gpsimd
            def _(pool):
                for s in self.sems:
                    pool.sem_clear(s)
        for s in self.sems:
            self.nc.release_semaphore(s)


def constants(nc, k, top):
    k.ident = top.sb("ident", [P, P])
    k.ident16 = top.sb("ident16", [P, P], BF16)
    k.count = top.sb("count", [P, P])
    k.before = top.sb("before", [P, P])
    k.ones = top.sb("ones", [P, P])
    k.pick = top.sb("pick", [3 * HEADS, HEADS, P], BF16)
    with ExitStack() as ctx:
        m = Mem(nc, ctx, "const")
        made = m.sem("made")
        block = ctx.enter_context(nc.Block())

        @block.gpsimd
        def _(pool):
            c = Chain(pool, made)
            c.step(nc.gpsimd.memset(k.ident[:], 0.0))
            c.step(nc.gpsimd.memset(k.ones[:], 1.0))
            c.step(nc.gpsimd.memset(k.pick[:], 0.0))
            c.step(nc.gpsimd.affine_select(out=k.ident[:], in_=k.ident[:], compare_op=ALU.not_equal, fill=1.0,
                                           base=0, pattern=[[-1, P]], channel_multiplier=1))
            c.step(nc.gpsimd.iota(k.count[:], pattern=[[1, P]], base=0, channel_multiplier=0,
                                  allow_small_or_imprecise_dtypes=True))
            c.step(nc.gpsimd.affine_select(out=k.before[:], in_=k.ones[:], compare_op=ALU.is_gt, fill=0.0,
                                           base=0, pattern=[[1, P]], channel_multiplier=-1))
            for part in range(3):
                c.step(nc.gpsimd.affine_select(out=k.pick[:], in_=k.pick[:], compare_op=ALU.not_equal, fill=1.0,
                                               base=-HEADS * part, pattern=[[-1, HEADS], [0, P]],
                                               channel_multiplier=1))
            c.step(nc.gpsimd.tensor_copy(k.ident16[:], k.ident[:]))


def sort_edges(nc, k, src, dst, etype, ew, attr):
    with ExitStack() as ctx:
        m = Mem(nc, ctx, "sort")
        t = Kept()
        t.win = {w: m.sb(f"win_{w}", [P, COLS]) for w in "ds"}
        t.row_d = m.sb("row_d", [P, COLS], I32)
        t.hit = m.sb("hit", [P, COLS], I32)
        t.high = m.sb("high", [P, COLS], I32)
        t.run = m.sb("run", [P, COLS])
        t.run_b = m.sb("run_b", [P, COLS])
        t.place = m.sb("place", [P, COLS])
        t.total = m.sb("total", [P, WIN])
        t.pairs = m.sb("pairs", [P, WIN])
        t.pairsi = m.sb("pairsi", [P, WIN], I32)
        t.pend = m.sb("pend", [P, WIN])
        t.pstart = m.sb("pstart", [P, WIN])
        t.base = m.sb("base", [P, WIN])
        t.zero = m.sb("zero", [P, WIN])
        t.pair_no = m.sb("pair_no", [P, PCOLS])
        t.first = m.sb("first", [P, PCOLS])
        t.tables = m.sb("tables", [P, 2, PCOLS], I32)
        t.le = m.sb("le", [P, PCOLS, WIN])
        t.pw = m.sb("pw", [P, PCOLS])
        t.pwi = m.sb("pwi", [P, 2, PCOLS], I32)
        t.sums = m.ps("sums", [P, 2, 512])
        read_edges(nc, k, t, src, dst, etype, ew)
        scatter_by_dst(nc, k, t, attr)


def rank_sums(nc, k, t, pe, counted, summed):
    pe.wait_ge(counted, 1)
    nc.tensor.matmul(t.sums[:, 0, 0:WIN], k.before[:], t.total[:], start=True, stop=True)
    nc.tensor.matmul(t.sums[:, 1, 0:WIN], k.ones[:], t.total[:], start=True, stop=True).then_inc(summed, 1)


def rank_windows(nc, k, t, v, c, n, chain, counted, summed, tiled):
    win = t.win["ds"[n]]
    start = c.base + c.n
    with v.Fori(0, WIN) as i:
        nc.vector.tensor_scalar(t.run[:], win[:], k.count[:, bass.ds(i, 1)], 0.0, ALU.is_equal, ALU.add,
                                accum_out=t.total[:, bass.ds(i, 1)]).then_inc(chain, 1)
        v.wait_ge(chain, i + (start + 1))
    v.sem_inc(counted, 1)
    c.begin(start + WIN)
    v.wait_ge(summed, 1)
    c.step(nc.vector.tensor_scalar(t.pairsi[:], t.sums[:, 1, 0:WIN], float(PAIR - 1), None, ALU.add))
    c.step(nc.vector.tensor_scalar(t.pairsi[:], t.pairsi[:], 8, None, ALU.arith_shift_right))
    c.step(nc.vector.tensor_copy(t.pairs[:], t.pairsi[:]))
    c.step(nc.vector.tensor_tensor_scan(t.pend[:], t.pairs[:], t.zero[:], 0.0, ALU.add, ALU.add))
    c.step(nc.vector.tensor_sub(t.pstart[:], t.pend[:], t.pairs[:]))
    c.step(nc.vector.scalar_tensor_tensor(t.base[:], t.pstart[:], float(PAIR), t.sums[:, 0, 0:WIN],
                                          ALU.mult, ALU.add))
    c.step(nc.vector.tensor_tensor(t.le[:], t.pstart[:].unsqueeze(1).broadcast_to([P, PCOLS, WIN]),
                                   t.pair_no[:].unsqueeze(2).broadcast_to([P, PCOLS, WIN]), ALU.is_le))
    c.step(nc.vector.tensor_reduce(t.pw[:], t.le[:], AX, ALU.add))
    c.step(nc.vector.tensor_scalar(t.pwi[:, n, :], t.pw[:], -1.0, None, ALU.add))
    v.sem_inc(tiled, 1)


def rank_edges(nc, k, t, v, c, n, rows, chain, tick):
    win = t.win["ds"[n]]
    c.step(nc.vector.memset(t.place[:], 0.0))
    start = c.base + c.n
    two = ((t.hit, t.run), (t.high, t.run_b))
    with v.Fori(0, WIN // 2) as i:
        done = i * 6 + start
        for n, (hit, run) in enumerate(two):
            nc.vector.tensor_scalar(hit[:], win[:], k.count[:, bass.ds(i * 2 + n, 1)], None, ALU.is_equal
                                    ).then_inc(chain, 1)
        for n, (hit, run) in enumerate(two):
            v.wait_ge(chain, done + (n + 1))
            nc.vector.tensor_tensor_scan(run[:], hit[:], hit[:], t.base[:, bass.ds(i * 2 + n, 1)],
                                         ALU.add, ALU.max).then_inc(chain, 1)
        for n, (hit, run) in enumerate(two):
            v.wait_ge(chain, done + (n + 3))
            v.sem_inc(tick, 1)
            if n:
                v.wait_ge(chain, done + 5)
                v.sem_inc(tick, 1)
            nc.vector.copy_predicated(t.place[:], hit[:], run[:]).then_inc(chain, 1)
        v.wait_ge(chain, done + 6)
        v.sem_inc(tick, 1)
    c.begin(start + 3 * WIN)
    c.step(nc.vector.tensor_scalar(t.hit[:], t.place[:], -1.0, None, ALU.add))
    c.step(nc.vector.tensor_scalar(t.high[:], t.hit[:], 7, None, ALU.arith_shift_right))
    c.step(nc.vector.tensor_scalar(t.hit[:], t.hit[:], P - 1, None, ALU.bitwise_and))
    c.step(nc.vector.tensor_copy(t.run[:], t.high[:]))
    c.step(nc.vector.tensor_copy(t.place[:], t.hit[:]))
    c.step(nc.vector.scalar_tensor_tensor(rows, t.place[:], float(TILES), t.run[:], ALU.mult, ALU.add))


def read_edges(nc, k, t, src, dst, etype, ew):
    with ExitStack() as ctx:
        m = Mem(nc, ctx, "read")
        raw = {w: m.sb(f"raw_{w}", [P, COLS], I32) for w in ("src", "dst", "rel")}
        weight = m.sb("weight", [P, COLS])
        fill = m.sb("fill", [P, TILES // 64, DREC])
        fill_s = m.sb("fill_s", [P, TILES // 8, REC])
        falls = m.sb("falls", [P, 2])
        moved = m.sb("moved", [P, 3, WIN])
        compared, passed, decided = m.sem("compared"), m.sem("passed"), m.sem("decided")
        padded, landed, filled = m.sem("padded"), m.sem("landed"), m.sem("filled")
        counted, summed, tiled, cleared, made, chain, tick = (
            m.sem(x) for x in ("counted", "summed", "tiled", "cleared", "made", "chain", "tick"))
        block = ctx.enter_context(nc.Block())

        @block.sync
        def _(sp):
            sp.wait_ge(padded, 1)
            for name, a in {"dst": dst, "src": src, "rel": etype, "ew": ew}.items():
                to = weight if name == "ew" else raw[name]
                flat = (P - 1) * COLS_REAL
                sp.dma_start(to[0:P - 1, 0:COLS_REAL],
                             a[0:flat].rearrange("(p c) -> p c", p=P - 1)).then_inc(landed, 16)
                sp.dma_start(to[P - 1:P, 0:LAST_COLS],
                             a[flat:EDGES].rearrange("(p c) -> p c", p=1)).then_inc(landed, 16)
            sp.wait_ge(made, 1)
            for j in range(8):
                sp.dma_start(k.rec_s[:, bass.ts(j, TILES // 8), :], fill_s[:]).then_inc(filled, 16)
            sp.wait_ge(filled, 16 * 8)
            sp.wait_ge(landed, 16 * 8)
            sp.wait_ge(decided, 1)
            with sp.If(in_order(nc.sync, k, "read_sp")):
                sp.wait_ge(decided, 1)
            with sp.Else():
                for j in range(64):
                    sp.dma_start(k.rec_d[:, bass.ts(j, TILES // 64), :], fill[:]).then_inc(filled, 16)
                sp.wait_ge(filled, 16 * (64 + 8))
            sp.end_ifs()

        @block.tensor
        def _(pe):
            rank_sums(nc, k, t, pe, counted, summed)
            pe.wait_ge(compared, 1)
            nc.tensor.matmul(t.sums[0:P - 1, 0, 64:65], k.ident[:, 1:P], t.win["d"][:, 0:1],
                             start=True, stop=True).then_inc(passed, 1)
            pe.wait_ge(compared, 2)
            nc.tensor.matmul(t.sums[0:1, 1, 64:65], falls[:, 0:1], k.ones[:, 0:1],
                             start=True, stop=True).then_inc(passed, 1)

        @block.gpsimd
        def _(pool):
            nc.gpsimd.iota(t.pair_no[:], pattern=[[1, PCOLS]], base=0, channel_multiplier=PCOLS,
                           allow_small_or_imprecise_dtypes=True)
            nc.gpsimd.memset(fill_s[:], 0.0)
            nc.gpsimd.memset(fill[:], 0.0).then_inc(cleared, 1)
            pool.wait_ge(cleared, 1)
            nc.gpsimd.memset(fill_s[:, :, 1:2], NOWHERE)
            nc.gpsimd.memset(fill[:, :, 1:2], NOWHERE).then_inc(made, 1)

        @block.vector
        def _(v):
            c = Chain(v, chain)
            for a in (raw["src"], raw["dst"]):
                nc.vector.memset(a[:, COLS_REAL:COLS], PAD_NODE)
                nc.vector.memset(a[P - 32:P, LAST_COLS:COLS_REAL], PAD_NODE)
            for a in (raw["rel"], weight):
                nc.vector.memset(a[:, COLS_REAL:COLS], 0)
                nc.vector.memset(a[P - 32:P, LAST_COLS:COLS_REAL], 0)
            c.did(nc.vector.memset(t.zero[:], 0.0))
            c.wait()
            v.sem_inc(padded, 1)
            v.wait_ge(landed, 16 * 8)
            for w, key, other in (("d", "dst", "src"), ("s", "src", "dst")):
                rec = k.sorted[w]
                c.step(nc.vector.tensor_scalar(t.high[:], raw[key][:], 7, None, ALU.arith_shift_right))
                c.did(nc.vector.tensor_copy(t.run[:], raw[key][:]))
                c.step(nc.vector.tensor_copy(t.win[w][:], t.high[:]))
                c.did(nc.vector.scalar_tensor_tensor(rec[:, 0:COLS, 1], t.win[w][:], -float(P), t.run[:],
                                                     ALU.mult, ALU.add))
                c.did(nc.vector.tensor_copy(rec[:, 0:COLS, 0], raw[other][:]))
                c.did(nc.vector.tensor_copy(rec[:, 0:COLS, 2], weight[:]))
                c.step(nc.vector.tensor_copy(rec[:, 0:COLS, 3], raw["rel" if w == "s" else "dst"][:]))
            v.wait_ge(made, 1)
            rank_windows(nc, k, t, v, c, 0, chain, counted, summed, tiled)
            win = t.win["d"]
            c.step(nc.vector.tensor_tensor(t.run[:, 0:COLS_REAL - 1], win[:, 0:COLS_REAL - 1], win[:, 1:COLS_REAL],
                                           ALU.is_gt))
            c.step(nc.vector.tensor_reduce(falls[:, 0:1], t.run[:, 0:COLS_REAL - 1], AX, ALU.add))
            v.sem_inc(compared, 1)
            v.wait_ge(passed, 1)
            c.step(nc.vector.tensor_tensor(falls[0:P - 1, 1:2], win[0:P - 1, COLS_REAL - 1:COLS_REAL],
                                           t.sums[0:P - 1, 0, 64:65], ALU.is_gt))
            c.step(nc.vector.tensor_add(falls[0:P - 1, 0:1], falls[0:P - 1, 0:1], falls[0:P - 1, 1:2]))
            v.sem_inc(compared, 1)
            v.wait_ge(passed, 2)
            c.step(nc.vector.tensor_scalar(k.in_order[:], t.sums[0:1, 1, 64:65], 0.0, None, ALU.is_equal))
            v.sem_inc(decided, 1)
            ends, shift, rise = (moved[:, n, :] for n in range(3))
            c.step(nc.vector.tensor_tensor_scan(ends, t.sums[:, 1, 0:WIN], t.zero[:], 0.0, ALU.add, ALU.add))
            c.step(nc.vector.tensor_sub(ends, ends, t.sums[:, 1, 0:WIN]))
            c.step(nc.vector.scalar_tensor_tensor(shift, t.pstart[:], -float(PAIR), ends, ALU.mult, ALU.add))
            c.did(nc.vector.tensor_copy(rise[:, 0:1], shift[:, 0:1]))
            c.step(nc.vector.tensor_sub(rise[:, 1:WIN], shift[:, 1:WIN], shift[:, 0:WIN - 1]))
            c.step(nc.vector.tensor_mul(t.le[:], t.le[:], rise.unsqueeze(1).broadcast_to([P, PCOLS, WIN])))
            c.step(nc.vector.tensor_reduce(t.pw[:], t.le[:], AX, ALU.add))
            c.step(nc.vector.scalar_tensor_tensor(t.first[:], t.pair_no[:], float(PAIR), t.pw[:], ALU.mult, ALU.add))
            c.step(nc.vector.tensor_scalar(t.pw[:], t.first[:], float(EDGES - PAIR), None, ALU.min))
            c.did(nc.vector.tensor_copy(t.tables[:, 0, :], t.pw[:]))
            c.step(nc.vector.tensor_sub(t.tables[:, 1, :], t.first[:], t.pw[:]))
            with v.If(in_order(nc.vector, k, "read_v")):
                v.wait_ge(decided, 1)
            with v.Else():
                rank_edges(nc, k, t, v, c, 0, t.row_d[:], chain, tick)
            v.end_ifs()


def in_order(eng, k, name):
    reg = eng.alloc_register(f"in_order_{name}")
    eng.reg_load([reg], k.in_order[:])
    return eng.snap(reg, min_val=0, max_val=1)


def scatter_by_dst(nc, k, t, attr):
    with ExitStack() as ctx:
        m = Mem(nc, ctx, "scatter")
        out = m.sb("out", [P, SLOTS, SG, DREC])
        where = m.sb("where", [P, SLOTS, SG], I32)
        attr_in = [m.sem(f"attr_in{s}") for s in range(SLOTS)]
        counted, summed, tiled, chain, tick, staged, ptick, wrote = (
            m.sem(x) for x in ("counted", "summed", "tiled", "chain", "tick", "staged", "ptick", "wrote"))
        sent = [nc.alloc_semaphore(f"scattered{s}") for s in range(SLOTS)]
        firsts = m.sb("firsts", [1, PAIRS_ALL], I32)
        kept, known, paired_sp, paired_act = (m.sem(x) for x in ("kept", "known", "paired_sp", "paired_act"))
        paired_pool = nc.alloc_semaphore("paired_pool")
        first_regs = {e: [eng.alloc_register(f"first_{e}{q}") for q in range(GP)]
                      for e, eng in (("sp", nc.sync), ("act", nc.scalar), ("pool", nc.gpsimd))}
        whole = (P - 1) * COLS_REAL
        attr_a = attr[0:whole, :].rearrange("(p c) f -> p c f", p=P - 1)
        attr_b = attr[whole:EDGES, :].rearrange("(p c) f -> p c f", p=1)
        per_slot = SG * 16
        full = LAST_COLS // SG
        block = ctx.enter_context(nc.Block())

        def load_pairs(eng, regs, share, done):
            groups = SHARES[share + 1] - SHARES[share]
            with eng.Fori(0, groups) as i:
                at = i * GP + SHARES[share] * GP
                eng.reg_load(regs, firsts[0:1, bass.ds(at, GP)])
                for q in range(GP):
                    first = eng.snap(regs[q], min_val=0, max_val=EDGES - PAIR)
                    eng.dma_start(k.sorted["d"][:, bass.ds((at + q) * 2, 2), :].rearrange("p j w -> p (j w)"),
                                  k.natural[bass.ds(first, PAIR), :].rearrange("(p j) w -> p (j w)", p=P)
                                  ).then_inc(done, 16)
            eng.wait_ge(done, 16 * GP * groups)

        @block.scalar
        def _(act):
            act.wait_ge(known, 1)
            with act.If(in_order(nc.scalar, k, "scatter_act")):
                load_pairs(act, first_regs["act"], 1, paired_act)
            act.end_ifs()

        @block.sync
        def _(sp):
            table = lambda n: t.tables[:, n, :]
            for to, a in ((k.pair_win[0], t.pwi[:, 0, :]), (k.pair_first, table(0)), (k.pair_skip, table(1))):
                sp.dma_start(to.rearrange("(p c) -> p c", p=P), a).then_inc(wrote, 16)
            rec = k.sorted["d"]
            sp.dma_start(k.natural[0:whole, :].rearrange("(p c) w -> p c w", p=P - 1),
                         rec[0:P - 1, 0:COLS_REAL, :]).then_inc(wrote, 16)
            sp.dma_start(k.natural[whole:EDGES, :].rearrange("(p c) w -> p c w", p=1),
                         rec[P - 1:P, 0:LAST_COLS, :]).then_inc(wrote, 16)
            sp.wait_ge(wrote, 16 * 5)
            sp.dma_start(firsts[:], k.pair_first[0:PAIRS_ALL].unsqueeze(0)).then_inc(kept, 16)
            sp.wait_ge(kept, 16)
            sp.sem_inc(known, 1)

            def body(g, s, u):
                if since(g, SLOTS):
                    sp.wait_ge(sent[s], u * per_slot)
                sp.dma_start(out[0:P - 1, s, :, REC:], attr_a[:, bass.ds(g * SG, SG), :]).then_inc(attr_in[s], 16)
                sp.dma_start(out[P - 1:P, s, :, REC:], attr_b[:, bass.ds(g * SG, SG), :]).then_inc(attr_in[s], 16)

            with sp.If(in_order(nc.sync, k, "scatter_sp")):
                load_pairs(sp, first_regs["sp"], 0, paired_sp)
            with sp.Else():
                each_group(sp, body, full)
                for g in range(full, SCAT):
                    s, u = g % SLOTS, g // SLOTS
                    sp.wait_ge(sent[s], u * per_slot)
                    c0 = g * SG
                    for rows, a, n in ((slice(0, P - 1), attr_a, min(SG, COLS_REAL - c0)),
                                       (slice(P - 1, P), attr_b, min(SG, LAST_COLS - c0))):
                        if n > 0:
                            sp.dma_start(out[rows, s, 0:n, REC:], a[:, c0:c0 + n, :]).then_inc(attr_in[s], 16)
                        else:
                            sp.sem_inc(attr_in[s], 16)
            sp.end_ifs()
            sp.wait_ge(tiled, 1)
            sp.dma_start(k.pair_win[1].rearrange("(p c) -> p c", p=P), t.pwi[:, 1, :]).then_inc(wrote, 16)
            sp.wait_ge(wrote, 16 * 6)

        @block.gpsimd
        def _(pool):
            def body(g, s, u):
                pool.wait_ge(attr_in[s], (u + 1) * 32)
                pool.sem_inc(ptick, 1)
                nc.gpsimd.tensor_copy(out[:, s, :, 0:REC], k.sorted["d"][:, bass.ds(g * SG, SG), :])
                nc.gpsimd.tensor_copy(where[:, s, :], t.row_d[:, bass.ds(g * SG, SG)]).then_inc(staged, 1)
                pool.wait_ge(staged, g + 1)
                pool.sem_inc(ptick, 1)
                for j in range(SG):
                    nc.gpsimd.indirect_dma_start(k.rec_d.rearrange("p t r -> (p t) r"), At(where[:, s, j:j + 1], 0),
                                                 out[:, s, j, :], None).then_inc(sent[s], 16)

            pool.wait_ge(known, 1)
            with pool.If(in_order(nc.gpsimd, k, "scatter_pool")):
                load_pairs(pool, first_regs["pool"], 2, paired_pool)
            with pool.Else():
                each_group(pool, body, SCAT)
                for s in range(SLOTS):
                    pool.wait_ge(sent[s], SCAT // SLOTS * per_slot)
            pool.end_ifs()

        @block.tensor
        def _(pe):
            rank_sums(nc, k, t, pe, counted, summed)

        @block.vector
        def _(v):
            c = Chain(v, chain)
            rank_windows(nc, k, t, v, c, 1, chain, counted, summed, tiled)
            rank_edges(nc, k, t, v, c, 1, k.index[:, 0:COLS], chain, tick)


def scatter_by_src(nc, k, pool, m, first, rounds):
    out = m.sb("scatter_out", [P, SLOTS, SG, REC])
    where = m.sb("scatter_where", [P, SLOTS, SG], I32)
    staged, ptick = m.scatter_sems
    sent, base = k.pool_dma, k.pool_dma_count
    per_slot = SG * 16

    def body(g, s, u):
        if since(g, SLOTS):
            pool.wait_ge(sent[s], u * per_slot + base)
            pool.sem_inc(ptick, 1)
        nc.gpsimd.tensor_copy(out[:, s], k.sorted["s"][:, bass.ds((g + first) * SG, SG), :])
        nc.gpsimd.tensor_copy(where[:, s, :], k.index[:, bass.ds((g + first) * SG, SG)]).then_inc(staged, 1)
        pool.wait_ge(staged, g + 1)
        pool.sem_inc(ptick, 1)
        for j in range(SG):
            nc.gpsimd.indirect_dma_start(k.rec_s.rearrange("p t r -> (p t) r"), At(where[:, s, j:j + 1], 0),
                                         out[:, s, j, :], None).then_inc(sent[s], 16)

    each_group(pool, body, rounds * SLOTS)
    for s in range(SLOTS):
        pool.wait_ge(sent[s], rounds * per_slot + base)
    k.pool_dma_count += rounds * per_slot


def load_edges(nc, k, order):
    table = k.rec_d if order == "d" else k.rec_s
    by_dst = order == "d"
    with ExitStack() as ctx:
        m = Mem(nc, ctx, f"edges_{order}")
        landed = m.sem("landed")
        if by_dst:
            of_pair = m.sb("of_pair", [P, 2, PAIRS_ALL], I32)
            row = m.sb("row", [P, 2])
            skipped = m.sb("skipped", [P, PAIRS_ALL, 2])
            told, placed, chain = m.sem("told"), m.sem("placed"), m.sem("chain")
        block = ctx.enter_context(nc.Block())

        def load(sp):
            for j in range(8):
                part = bass.ts(j, TILES // 8)
                sp.dma_start(k.sorted[order][:, part, :], table[:, part, 0:REC]).then_inc(landed, 16)
            sp.wait_ge(landed, 16 * 8)

        if by_dst:
            @block.gpsimd
            def _(pool):
                nc.gpsimd.iota(row[:], pattern=[[1, 2]], base=0, channel_multiplier=2,
                               allow_small_or_imprecise_dtypes=True).then_inc(placed, 1)

            @block.vector
            def _(v):
                c = Chain(v, chain)
                rec = k.sorted["d"].rearrange("p (q j) w -> p q j w", j=2)
                wide = lambda a: a.unsqueeze(2).broadcast_to([P, PAIRS_ALL, 2])
                v.wait_ge(told, 32)
                v.wait_ge(placed, 1)
                with v.If(in_order(nc.vector, k, "edges_v")):
                    c.step(nc.vector.tensor_tensor(skipped[:], wide(of_pair[:, 1, :]),
                                                   row[:].unsqueeze(1).broadcast_to([P, PAIRS_ALL, 2]), ALU.is_gt))
                    c.step(nc.vector.scalar_tensor_tensor(skipped[:], skipped[:], float(ROWS), rec[:, :, :, 3],
                                                          ALU.mult, ALU.add))
                    c.step(nc.vector.scalar_tensor_tensor(rec[:, :, :, 1], wide(of_pair[:, 0, :]), -float(P),
                                                          skipped[:], ALU.mult, ALU.add))
                v.end_ifs()

            @block.sync
            def _(sp):
                for n, a in enumerate((k.pair_win[0], k.pair_skip)):
                    sp.dma_start(of_pair[:, n, :], a[0:PAIRS_ALL].unsqueeze(0).broadcast_to([P, PAIRS_ALL])
                                 ).then_inc(told, 16)
                sp.wait_ge(told, 32)
                with sp.If(in_order(nc.sync, k, "edges_sp")):
                    sp.wait_ge(told, 32)
                with sp.Else():
                    load(sp)
                sp.end_ifs()
        else:
            @block.sync
            def _(sp):
                load(sp)


def load_nodes(nc, k, x_in):
    with ExitStack() as ctx:
        m = Mem(nc, ctx, "nodes")
        zeroed, landed = m.sem("zeroed"), m.sem("landed")
        block = ctx.enter_context(nc.Block())

        @block.vector
        def _(v):
            nc.vector.memset(k.x[:, REAL_WIN - 1:WIN, :], 0.0).then_inc(zeroed, 1)

        @block.sync
        def _(sp):
            whole = (REAL_WIN - 1) * P
            sp.wait_ge(zeroed, 1)
            sp.dma_start(k.x[:, 0:REAL_WIN - 1, :],
                         x_in[0:whole, :].rearrange("(w p) f -> p w f", p=P)).then_inc(landed, 16)
            sp.dma_start(k.x[0:LAST_ROWS, REAL_WIN - 1, :], x_in[whole:NODES, :]).then_inc(landed, 16)
            sp.wait_ge(landed, 32)


def table_view(table):
    return table.rearrange("(w p) f -> p w f", p=P)


def attention_rows(nc, k, name, nodes, weight, left, right):
    with ExitStack() as ctx:
        m = Mem(nc, ctx, name)
        w = m.sb("w", [P, FEAT])
        sides = m.sb("sides", [P, 2, FEAT])
        turned = m.sb("turned", [P, 2, P])
        out = m.sb("out", [P, WIN, R_GAT])
        prod = m.sb("prod", [P, 2, 2, FEAT])
        ps_t = m.ps("ps_t", [P, 2, 512])
        ps_f = m.ps("ps_f", [P, 2, 512])
        landed, turn, copied, product, used, chain, wrote = (
            m.sem(x) for x in ("landed", "turn", "copied", "product", "used", "chain", "wrote"))
        block = ctx.enter_context(nc.Block())

        @block.sync
        def _(sp):
            sp.dma_start(w[:], weight).then_inc(landed, 16)
            for n, a in enumerate((left, right)):
                sp.dma_start(sides[:, n, :], a.rearrange("h d -> (h d)").unsqueeze(0).broadcast_to([P, FEAT])
                             ).then_inc(landed, 16)
            sp.wait_ge(used, WIN)
            sp.dma_start(table_view(k.gat_rows), out[:]).then_inc(wrote, 16)
            sp.wait_ge(wrote, 16)

        @block.tensor
        def _(pe):
            pe.wait_ge(landed, 48)
            for g in range(WIN + 1):
                if g < WIN:
                    if g >= 2:
                        pe.wait_ge(copied, g - 1)
                    nc.tensor.transpose(ps_t[:, g % 2, 0:P], nodes[:, g, :], k.ident[:]).then_inc(turn, 1)
                if g >= 1:
                    pe.wait_ge(copied, g)
                    if g >= 3:
                        pe.wait_ge(used, g - 2)
                    nc.tensor.matmul(ps_f[:, (g - 1) % 2, 0:FEAT], turned[:, (g - 1) % 2, :], w[:],
                                     start=True, stop=True).then_inc(product, 1)

        @block.scalar
        def _(act):
            for g in range(WIN):
                act.wait_ge(turn, g + 1)
                if g >= 2:
                    act.wait_ge(product, g - 1)
                nc.scalar.copy(turned[:, g % 2, :], ps_t[:, g % 2, 0:P]).then_inc(copied, 1)

        @block.vector
        def _(v):
            c = Chain(v, chain)
            v.wait_ge(landed, 48)
            for g in range(WIN):
                b = g % 2
                f = ps_f[:, b, 0:FEAT]
                v.wait_ge(product, g + 1)
                for n in range(2):
                    c.did(nc.vector.tensor_mul(prod[:, b, n, :], f, sides[:, n, :]))
                c.wait()
                heads = prod[:, b].rearrange("p n (h d) -> p n h d", h=HEADS)
                nc.vector.tensor_reduce(out[:, g, FEAT:R_GAT], heads[:, 0], AX, ALU.add)
                nc.vector.tensor_reduce(k.pair[:, g, 0:HEADS], heads[:, 1], AX, ALU.add)
                nc.vector.tensor_copy(out[:, g, 0:FEAT], f).then_inc(used, 1)


def attention_maxima(nc, k, name):
    with ExitStack() as ctx:
        m = Mem(nc, ctx, name)
        index = m.sb("index", [P, TILES], I32)
        wins = m.sb("wins", [1, TILES // 2 + 2 * Windows.PADS], I32)
        slot_index = m.sb("slot_index", [P, SLOTS, G], I32)
        rows = m.sb("rows", [P, SLOTS, G, R_GAT])
        parts = m.sb("parts", [P, 2, G, 3 * HEADS], BF16)
        rest = m.sb("rest", [P, 2, 2, G, HEADS])
        hide = m.sb("hide", [P, 2, G, P], BF16)
        scores = m.sb("scores", [3 * HEADS, 2, G * P], BF16)
        best = m.sb("best", [P, WIN, HEADS])
        tile_best = m.sb("tile_best", [P, 2, GP, 2, HEADS])
        pair_best = m.sb("pair_best", [P, 2, GP, HEADS])
        z = m.sb("z", [P, WIN, HEADS])
        ps_s = m.ps("ps_s", [P, 2, 512])
        ps_z = m.ps("ps_z", [P, 4, HEADS, P])
        made, padded, landed, chain, tick, bested = (m.sem(x) for x in ("made", "padded", "landed", "chain", "tick", "bested"))
        indexed = [m.sem(f"indexed{s}") for s in range(SLOTS)]
        gathered, base = k.pool_dma, k.pool_dma_count
        stored = [m.sem(f"stored{s}") for s in range(SLOTS)]
        split, hidden, turned, copied, masked, reduced = (
            m.sem(x) for x in ("split", "hidden", "turned", "copied", "masked", "reduced"))
        ptick, atick, etick, stick = (m.sem(x) for x in ("ptick", "atick", "etick", "stick"))
        window = Windows(nc.vector, wins, f"{name}_w", -2)
        rec = k.sorted["d"]
        block = ctx.enter_context(nc.Block())

        @block.sync
        def _(sp):
            Windows.load(nc, m, sp, wins, k.pair_win[0], landed, padded)
            sp.wait_ge(made, 1)

            def load_index(g, s, u):
                if since(g, SLOTS):
                    sp.wait_ge(gathered[s], u * (16 * G) + base)
                    sp.sem_inc(stick, 1)
                sp.dma_start(slot_index[:, s, :], index[:, bass.ds(g * G, G)]).then_inc(indexed[s], 16)

            def body(g, s, u):
                if not since(g, 1):
                    for n in range(2):
                        load_index(n, n, 0)
                if ahead(g, 2):
                    load_index(g + 2, (s + 2) % SLOTS, u + (s + 2) // SLOTS)
                sp.wait_ge(gathered[s], u * (16 * G) + (16 * G + base))
                sp.sem_inc(stick, 1)
                sp.dma_start(k.gat_edges[:, bass.ds(g * G, G), :], rows[:, s]).then_inc(stored[s], 16)

            each_group(sp, body)
            sp.wait_ge(landed, 16)
            for s in range(SLOTS):
                sp.wait_ge(stored[s], GROUPS // SLOTS * 16)

        @block.gpsimd
        def _(pool):
            def body(g, s, u):
                if since(g, SLOTS):
                    pool.wait_ge(split, g - (SLOTS - 1))
                    pool.sem_inc(ptick, 1)
                    pool.wait_ge(stored[s], u * 16)
                    pool.sem_inc(ptick, 1)
                pool.wait_ge(indexed[s], (u + 1) * 16)
                pool.sem_inc(ptick, 1)
                for t in range(G):
                    nc.gpsimd.indirect_dma_start(rows[:, s, t, :], None, k.gat_rows,
                                                 At(slot_index[:, s, t:t + 1], 0)).then_inc(gathered[s], 16)

            each_group(pool, body)

        @block.scalar
        def _(act):
            def body(g, s, u):
                if since(g, 2):
                    act.wait_ge(masked, g * G - G)
                    act.sem_inc(atick, 1)
                act.wait_ge(turned, g + 1)
                act.sem_inc(atick, 1)
                nc.scalar.copy(scores[:, s % 2, :], ps_s[0:3 * HEADS].rearrange("p a b -> p (a b)")
                               ).then_inc(copied, 1)

            each_group(act, body)

        @block.tensor
        def _(pe):
            def turn(g, b):
                pe.wait_ge(split, g + 1)
                pe.sem_inc(etick, 1)
                if since(g, 1):
                    pe.wait_ge(copied, g)
                    pe.sem_inc(etick, 1)
                for t in range(G):
                    last = nc.tensor.matmul(ps_s[0:3 * HEADS, t // 4, bass.ts(t % 4, P)], parts[:, b, t, :],
                                            k.ident16[:], start=True, stop=True)
                last.then_inc(turned, 1)

            def body(g, s, u):
                b = s % 2
                if not since(g, 1):
                    turn(0, 0)
                if ahead(g, 1):
                    turn(g + 1, (s + 1) % 2)
                pe.wait_ge(hidden, g + 1)
                pe.sem_inc(etick, 1)
                pe.wait_ge(copied, g + 1)
                pe.sem_inc(etick, 1)
                for t in range(G):
                    if since(g, 1) or t >= 4:
                        pe.wait_ge(reduced, g * G + (t - 3))
                        pe.sem_inc(etick, 1)
                    nc.tensor.matmul(ps_z[:, t % 4], hide[:, b, t, :],
                                     k.ident16[:].unsqueeze(1).broadcast_to([P, HEADS, P]), start=True, stop=False)
                    for h in range(HEADS):
                        last = nc.tensor.matmul(ps_z[:, t % 4, h, :], k.pick[:, h, :], scores[:, b, bass.ts(t, P)],
                                                start=False, stop=h == HEADS - 1)
                    last.then_inc(masked, 1)

            each_group(pe, body)

        @block.vector
        def _(v):
            c = Chain(v, chain)
            nc.vector.memset(wins[:], 0).then_inc(padded, 1)
            c.did(nc.vector.memset(best[:], -BIG))
            nc.vector.tensor_copy(index[:], rec[:, :, 0]).then_inc(made, 1)
            v.wait_ge(landed, 16)
            c.wait()
            start, per = c.n, 4

            def reduce(g, s, t):
                v.wait_ge(masked, g * G + (t + 1))
                nc.vector.tensor_reduce(tile_best[:, s % 2, t // 2, t % 2, :], ps_z[:, t % 4], AX,
                                        ALU.max).then_inc(reduced, 1)

            def combine(g, b):
                v.wait_ge(reduced, g * G + G)
                nc.vector.tensor_tensor(pair_best[:, b], tile_best[:, b, :, 0], tile_best[:, b, :, 1],
                                        ALU.max).then_inc(bested, 1)

            def update(g, b, q, win):
                v.wait_ge(bested, g * (GP + 1) + (q + 1))
                at = best[:, bass.ds(win[q], 1), :]
                nc.vector.tensor_tensor(at, at, pair_best[:, b, q:q + 1, :], ALU.max).then_inc(bested, 1)

            def split_part(s, n):
                b = s % 2
                score, r1, r2 = rows[:, s, :, FEAT:R_GAT], rest[:, b, 0], rest[:, b, 1]
                hi, mid, lo = (parts[:, b, :, bass.ts(q, HEADS)] for q in range(3))
                if n > 0:
                    c.wait()
                if n % 2:
                    c.did(nc.vector.tensor_sub(*((r1, score, hi), (r2, r1, mid))[n // 2]))
                elif n < 4:
                    c.did(nc.vector.tensor_copy(*((hi, score), (mid, r1))[n // 2]))
                else:
                    nc.vector.tensor_copy(lo, r2).then_inc(split, 1)

            def body(g, s, u):
                b = s % 2
                if not since(g, 1):
                    c.begin(start)
                    v.wait_ge(gathered[0], 16 * G + base)
                    for n in range(5):
                        split_part(0, n)
                c.begin((g + 1) * per + start)
                if since(g, 2):
                    v.wait_ge(masked, g * G - G)
                    v.sem_inc(tick, 1)
                group = rec[:, bass.ds(g * G, G), :]
                for t in range(G):
                    last = nc.vector.tensor_scalar(hide[:, b, t, :], k.count[:], group[:, t, 1:2], -BIG,
                                                   ALU.not_equal, ALU.mult)
                    if t == G - 1:
                        last.then_inc(hidden, 1)
                    if ahead(g, 1) and t < 5:
                        if t == 0:
                            s1, u1 = (s + 1) % SLOTS, u + (s + 1) // SLOTS
                            if since(g, 1):
                                v.wait_ge(turned, g)
                                v.sem_inc(tick, 1)
                            v.wait_ge(gathered[s1], u1 * (16 * G) + (16 * G + base))
                        split_part(s1, t)
                    if since(g, 2) and t == 0:
                        combine(g - 2, b)
                    if since(g, 1):
                        reduce(g - 1, s - 1, t)
                    if since(g, 2) and t % 2:
                        update(g - 2, b, t // 2, window.of(s))

            each_group(v, body, before=window.take)
            window.take(GROUPS)
            for t in range(G):
                reduce(GROUPS - 1, GROUPS - 1, t)
            for g in (GROUPS - 2, GROUPS - 1):
                combine(g, g % 2)
                for q in range(GP):
                    update(g, g % 2, q, window.of(g + 2 - GROUPS))
            c.begin(GROUPS * per + start)
            v.wait_ge(bested, GROUPS * (GP + 1))
            c.step(nc.vector.tensor_add(z[:], best[:], k.pair[:, :, 0:HEADS]))
            c.step(nc.vector.scalar_tensor_tensor(k.pair[:, :, HEADS:2 * HEADS], z[:], SLOPE, z[:],
                                                  ALU.mult, ALU.max))
        k.pool_dma_count += GROUPS // SLOTS * 16 * G


def edge_pass(nc, k, name, order, width, weigh, steps, *, index=None, table=None, stream=None, row_width=FEAT,
              attributes=None, pair=None, func=None, words=1, counts=False, scatter=None):
    with ExitStack() as ctx:
        m = Mem(nc, ctx, name)
        n_win = 0 if order == "d" else 1
        rec = k.sorted[order]
        wins = m.sb("wins", [1, TILES // 2 + 2 * Windows.PADS], I32)
        rows = m.sb("rows", [P, SLOTS, G, row_width])
        hot = m.sb("hot", [P, SLOTS, G, P])
        msg = m.sb("msg", [P, 2, G, width])
        if table is not None:
            slot_index = m.sb("slot_index", [P, SLOTS, G], I32)
        if attributes is not None:
            firsts = m.sb("firsts", [1, PAIRS_ALL], I32)
            first_regs = [nc.sync.alloc_register(f"{name}_f{q}") for q in range(GP)]
            attrs = m.sb("attrs", [P, SLOTS, G, ATTR])
        if pair is not None:
            hot_t = m.sb("hot_t", [P, 2, G, P], BF16)
            parts = m.sb("parts", [P, WIN, 3, 8], BF16)
            rest = m.sb("rest", [P, 2, WIN, 8])
            own_sum = m.sb("own_sum", [P, 2, G, 8])
            ps_t = m.ps("ps_t", [P, 2, 4, P])
            ps_own = m.ps("ps_own", [P, 2, 512])
        tmp = m.sb("tmp", [P, 2, 4, G, 8])
        per_bank = 512 // width
        banks = -(-GP // per_bank)
        ps_sum = m.ps("ps_sum", [P, 2, banks, 512])
        gathered, base = k.pool_dma, k.pool_dma_count
        loaded = [m.sem(f"loaded{s}") for s in range(SLOTS)]
        loads = GP if attributes is not None else int(table is None)
        indexed = [m.sem(f"indexed{s}") for s in range(SLOTS)]
        made, padded, landed, chain = (m.sem(x) for x in ("made", "padded", "landed", "chain"))
        hot_made, turned, copied, owned, asked, raised, weighed, summed, added = (
            m.sem(x) for x in ("hot_made", "turned", "copied", "owned", "asked", "raised", "weighed", "summed",
                               "added"))
        told = m.sem("told")
        vtick, ptick, atick, etick, stick = (m.sem(x) for x in ("vtick", "ptick", "atick", "etick", "stick"))
        m.scatter_sems = m.sem("staged"), m.sem("scatter_tick")
        add_to = Windows(nc.vector, wins, f"{name}_v", -2)
        look_at = Windows(nc.tensor, wins, f"{name}_p", 1) if pair is not None else None
        block = ctx.enter_context(nc.Block())

        def sums(b, q):
            at = q % per_bank * width
            return ps_sum[:, b, q // per_bank, at:at + width]

        @block.sync
        def _(sp):
            Windows.load(nc, m, sp, wins, k.pair_win[n_win], landed, padded)
            sp.wait_ge(made, 1)

            def body(g, s, u):
                if since(g, SLOTS):
                    sp.wait_ge(weighed, g - (SLOTS - 1))
                    sp.sem_inc(stick, 1)
                if table is not None:
                    sp.dma_start(slot_index[:, s, :], k.index[:, bass.ds(g * G, G)]).then_inc(indexed[s], 16)
                else:
                    sp.dma_start(rows[:, s], stream[:, bass.ds(g * G, G), :]).then_inc(loaded[s], 16)

            def from_records(g, s, u):
                body(g, s, u)
                for q in range(GP):
                    sp.dma_start(attrs[:, s, 2 * q:2 * q + 2, :],
                                 k.rec_d[:, bass.ds(g * G + 2 * q, 2), REC:DREC]).then_inc(loaded[s], 16)

            def from_input(g, s, u):
                body(g, s, u)
                sp.reg_load(first_regs, firsts[0:1, bass.ds(g * GP, GP)])
                for q in range(GP):
                    first = sp.snap(first_regs[q], min_val=0, max_val=EDGES - PAIR)
                    sp.dma_start(attrs[:, s, 2 * q:2 * q + 2, :].rearrange("p j f -> p (j f)"),
                                 attributes[bass.ds(first, PAIR), :].rearrange("(p j) f -> p (j f)", p=P)
                                 ).then_inc(loaded[s], 16)

            if attributes is None:
                each_group(sp, body)
            else:
                sp.dma_start(firsts[:], k.pair_first[0:PAIRS_ALL].unsqueeze(0)).then_inc(told, 16)
                sp.wait_ge(told, 16)
                with sp.If(in_order(nc.sync, k, name)):
                    each_group(sp, from_input)
                with sp.Else():
                    each_group(sp, from_records)
                sp.end_ifs()
            sp.wait_ge(landed, 16)

        if table is not None:
            @block.gpsimd
            def _(pool):
                def body(g, s, u):
                    pool.wait_ge(indexed[s], (u + 1) * 16)
                    pool.sem_inc(ptick, 1)
                    for t in range(G):
                        nc.gpsimd.indirect_dma_start(rows[:, s, t, :], None, table,
                                                     At(slot_index[:, s, t:t + 1], 0)).then_inc(gathered[s], 16)

                each_group(pool, body)
        elif scatter:
            @block.gpsimd
            def _(pool):
                scatter_by_src(nc, k, pool, m, *scatter)

        if pair is not None or func is not None:
            @block.scalar
            def _(act):
                def copy_out(g, b):
                    for half in range(2):
                        act.wait_ge(turned, g * 2 + (half + 1))
                        act.sem_inc(atick, 1)
                        nc.scalar.copy(hot_t[:, b, bass.ts(half, 4), :], ps_t[:, half]).then_inc(copied, 1)

                def body(g, s, u):
                    if pair is not None and not since(g, 1):
                        copy_out(0, 0)
                        copy_out(1, 1)
                    if func is not None:
                        act.wait_ge(asked, g + 1)
                        act.sem_inc(atick, 1)
                        nc.scalar.activation(tmp[:, s % 2, 1, :, 0:words], tmp[:, s % 2, 0, :, 0:words],
                                             func).then_inc(raised, 1)
                    if pair is not None and ahead(g, 2):
                        copy_out(g + 2, s % 2)

                each_group(act, body)

        @block.tensor
        def _(pe):
            pe.wait_ge(landed, 16)

            def turn(g, b):
                pe.wait_ge(hot_made, g + 1)
                pe.sem_inc(etick, 1)
                for half in range(2):
                    if since(g, 1):
                        pe.wait_ge(copied, g * 2 + (half - 1))
                        pe.sem_inc(etick, 1)
                    for t in range(4):
                        last = nc.tensor.transpose(ps_t[:, half, t, :], hot[:, b, 4 * half + t, :], k.ident[:])
                    last.then_inc(turned, 1)

            def look_up(g, b, win):
                pe.wait_ge(copied, g * 2 + 2)
                pe.sem_inc(etick, 1)
                for t in range(G):
                    last = nc.tensor.matmul(ps_own[:, b, bass.ts(t, 24)], hot_t[:, b, t, :],
                                            parts[:, bass.ds(win[t // 2], 1), :, :].rearrange("p a c w -> p (a c w)"),
                                            start=True, stop=True)
                last.then_inc(owned, 1)

            def body(g, s, u):
                b = s % 2
                if pair is not None:
                    if not since(g, 1):
                        turn(0, 0)
                        turn(1, 1)
                        look_at.take(-1)
                        look_up(0, 0, look_at.of(0))
                        look_at.take(0)
                    if ahead(g, 2):
                        turn(g + 2, (s + 2) % SLOTS)
                    if ahead(g, 1):
                        look_up(g + 1, (s + 1) % 2, look_at.of(s))
                else:
                    pe.wait_ge(hot_made, g + 1)
                    pe.sem_inc(etick, 1)
                pe.wait_ge(weighed, g + 1)
                pe.sem_inc(etick, 1)
                if since(g, 2):
                    pe.wait_ge(added, g * GP)
                    pe.sem_inc(etick, 1)
                for t in range(G):
                    last = nc.tensor.matmul(sums(b, t // 2), hot[:, s, t, :], msg[:, b, t, :],
                                            start=t % 2 == 0, stop=t % 2 == 1)
                last.then_inc(summed, 1)

            each_group(pe, body, before=look_at and look_at.take)

        @block.vector
        def _(v):
            c = Chain(v, chain)
            nc.vector.memset(wins[:], 0).then_inc(padded, 1)
            nc.vector.memset(k.acc[:, :, 0:width], 0.0).then_inc(added, GP)
            if table is not None:
                index(v, c)
            if counts:
                c.step(nc.vector.memset(msg[:, :, :, width - 1:width], 1.0))
            v.sem_inc(made, 1)
            v.wait_ge(landed, 16)
            v.wait_ge(added, GP)
            if pair is not None:
                for q in range(3):
                    c.step(nc.vector.tensor_copy(parts[:, :, q, :], pair[:] if q == 0 else rest[:, q - 1]))
                    if q < 2:
                        c.step(nc.vector.tensor_sub(rest[:, q], pair[:] if q == 0 else rest[:, 0],
                                                    parts[:, :, q, :]))
            start = c.n

            def add(g, s, q, win):
                at = k.acc[:, bass.ds(win[q], 1), 0:width].rearrange("p a w -> p (a w)")
                v.wait_ge(added, g * GP + (q + GP))
                nc.vector.tensor_add(at, at, sums(s % 2, q)).then_inc(added, 1)

            def mark(g, b):
                nc.vector.tensor_tensor(hot[:, b], k.count[:].unsqueeze(1).broadcast_to([P, G, P]),
                                        rec[:, bass.ds(g * G, G), 1:2].broadcast_to([P, G, P]),
                                        ALU.is_equal).then_inc(hot_made, 1)

            own_steps = 1 if pair is not None else 0

            def body(g, s, u):
                b = s % 2
                c.begin(g * (steps + own_steps) + start)
                if not since(g, 1):
                    mark(0, 0)
                    mark(1, 1)
                pairs = iter(range(GP if since(g, 2) else 0))

                def add_next():
                    for q in pairs:
                        add(g - 2, s, q, add_to.of(s))
                        break

                if since(g, 2):
                    v.wait_ge(summed, g - 1)
                    v.sem_inc(vtick, 1)
                own = None
                if pair is not None:
                    v.wait_ge(owned, g + 1)
                    own = own_sum[:, b]
                    c.step(nc.vector.tensor_reduce(own, ps_own[:, b, 0:24 * G].rearrange(
                        "p (g c w) -> p g w c", c=3, w=8), AX, ALU.add), add_next)
                if table is not None:
                    v.wait_ge(gathered[s], u * (16 * G) + (16 * G + base))
                    v.sem_inc(vtick, 1)
                if loads:
                    v.wait_ge(loaded[s], (u + 1) * 16 * loads)
                    v.sem_inc(vtick, 1)

                given = (v, c, add_next, msg[:, b], rows[:, s], attrs[:, s] if attributes is not None else None, own,
                         rec[:, bass.ds(g * G, G), :], tmp[:, b])
                prepared = weigh(0, *given)
                if func is not None:
                    prepared.then_inc(asked, 1)
                if ahead(g, 2):
                    mark(g + 2, (s + 2) % SLOTS)
                for q in range(GP):
                    add_next()
                if func is not None:
                    v.wait_ge(raised, g + 1)
                    v.sem_inc(vtick, 1)
                weigh(1, *given).then_inc(weighed, 1)
                assert c.n == steps + own_steps, (name, c.n)

            each_group(v, body, before=add_to.take)
            add_to.take(GROUPS)
            for g in (GROUPS - 2, GROUPS - 1):
                win = add_to.of(g + 2 - GROUPS)
                v.wait_ge(summed, g + 1)
                v.sem_inc(vtick, 1)
                for q in range(GP):
                    add(g, g % SLOTS, q, win)
            v.wait_ge(added, GROUPS * GP + GP)
        if table is not None:
            k.pool_dma_count += GROUPS // SLOTS * 16 * G


def over(a, n):
    return a.unsqueeze(3).broadcast_to([*a.shape, n])


def weigh_attention(nc):
    def weigh(stage, v, c, add, msg, rows, attrs, own, rec, tmp):
        score, e, ex = tmp[:, 2, :, 0:HEADS], tmp[:, 0, :, 0:HEADS], tmp[:, 1, :, 0:HEADS]
        exw = tmp[:, 3, :, 0:HEADS]
        if stage == 0:
            c.step(nc.vector.tensor_add(score, rows[:, :, FEAT:R_GAT], own[:, :, 0:HEADS]), add)
            c.step(nc.vector.scalar_tensor_tensor(score, score, SLOPE, score, ALU.mult, ALU.max), add)
            c.step(nc.vector.tensor_sub(e, score, own[:, :, HEADS:2 * HEADS]), add)
            return nc.vector.tensor_scalar(e, e, 0.0, None, ALU.min)
        c.did(nc.vector.tensor_mul(exw, ex, rec[:, :, 2:3].broadcast_to([P, G, HEADS])))
        c.step(nc.vector.tensor_copy(msg[:, :, FEAT:R_GAT], ex))
        return nc.vector.tensor_mul(msg[:, :, 0:FEAT].rearrange("p g (h d) -> p g h d", h=HEADS),
                                    rows[:, :, 0:FEAT].rearrange("p g (h d) -> p g h d", h=HEADS), over(exw, DH))
    return weigh, 5


def weigh_plain(nc, k, relations):
    def weigh(stage, v, c, add, msg, rows, attrs, own, rec, tmp):
        if stage == 0:
            return None
        last = nc.vector.tensor_mul(msg[:, :, 0:FEAT], rows, rec[:, :, 2:3].broadcast_to([P, G, FEAT]))
        if relations:
            last = nc.vector.tensor_tensor(msg[:, :, FEAT:FEAT + RELS], rec[:, :, 3:4].broadcast_to([P, G, RELS]),
                                           k.count[:, 0:RELS].unsqueeze(1).broadcast_to([P, G, RELS]),
                                           ALU.is_equal)
        return last
    return weigh, 0


def attention_end(nc, k, name, bias_in, out):
    with ExitStack() as ctx:
        m = Mem(nc, ctx, name)
        bias = m.sb("bias", [P, FEAT])
        inv = m.sb("inv", [P, WIN, HEADS])
        low = m.sb("low", [P, WIN, FEAT])
        landed, chain, asked, raised = (m.sem(x) for x in ("landed", "chain", "asked", "raised"))
        block = ctx.enter_context(nc.Block())

        @block.sync
        def _(sp):
            sp.dma_start(bias[:], bias_in.unsqueeze(0).broadcast_to([P, FEAT])).then_inc(landed, 16)
            sp.wait_ge(landed, 16)

        @block.scalar
        def _(act):
            act.wait_ge(asked, 1)
            nc.scalar.activation(low[:], low[:], ACT.Exp).then_inc(raised, 1)

        @block.vector
        def _(v):
            c = Chain(v, chain)
            v.wait_ge(landed, 16)
            c.step(nc.vector.tensor_scalar(k.per_dst[:], k.acc[:, :, R_GAT], 1.0, None, ALU.max))
            c.step(nc.vector.reciprocal(k.per_dst[:], k.per_dst[:]))
            c.step(nc.vector.tensor_scalar(inv[:], k.acc[:, :, FEAT:R_GAT], 1e-20, None, ALU.max))
            c.step(nc.vector.reciprocal(inv[:], inv[:]))
            heads = lambda a: a.rearrange("p w (h d) -> p w h d", h=HEADS)
            c.step(nc.vector.tensor_mul(heads(out[:]), heads(k.acc[:, :, 0:FEAT]), over(inv[:], DH)))
            c.step(nc.vector.tensor_add(out[:], out[:], bias[:].unsqueeze(1).broadcast_to([P, WIN, FEAT])))
            c.step(nc.vector.tensor_scalar(low[:], out[:], 0.0, None, ALU.min))
            v.sem_inc(asked, 1)
            v.wait_ge(raised, 1)
            c.step(nc.vector.tensor_scalar(low[:], low[:], -1.0, None, ALU.add))
            c.step(nc.vector.scalar_tensor_tensor(out[:], out[:], 0.0, low[:], ALU.max, ALU.add))


def weigh_normed(nc):
    def weigh(stage, v, c, add, msg, rows, attrs, own, rec, tmp):
        squares, inv = tmp[:, 0, :, 0:1], tmp[:, 2, :, 0:1]
        if stage == 0:
            c.step(nc.vector.tensor_mul(msg[:, :, FEAT:FEAT + ATTR], attrs, attrs), add)
            c.step(nc.vector.tensor_reduce(tmp[:, 0, :, 0], msg[:, :, FEAT:FEAT + ATTR], AX, ALU.add), add)
            return nc.vector.tensor_add(squares, squares, rows[:, :, FEAT:FEAT + 1])
        c.step(nc.vector.tensor_scalar(inv, tmp[:, 1, :, 0:1], 1e-12, None, ALU.max))
        c.step(nc.vector.reciprocal(inv, inv))
        nc.vector.tensor_mul(msg[:, :, 0:FEAT], rows[:, :, 0:FEAT], inv.broadcast_to([P, G, FEAT]))
        return nc.vector.tensor_mul(msg[:, :, FEAT:FEAT + ATTR], attrs, inv.broadcast_to([P, G, ATTR]))
    return weigh, 4


def weigh_relation(nc, k):
    def weigh(stage, v, c, add, msg, rows, attrs, own, rec, tmp):
        if stage == 0:
            return None
        c.step(nc.vector.tensor_tensor(tmp[:, 0], rec[:, :, 3:4].broadcast_to([P, G, RELS]),
                                       k.count[:, 0:RELS].unsqueeze(1).broadcast_to([P, G, RELS]), ALU.is_equal))
        c.step(nc.vector.tensor_mul(tmp[:, 1], tmp[:, 0], own))
        c.step(nc.vector.tensor_reduce(tmp[:, 2, :, 0], tmp[:, 1], AX, ALU.add))
        return nc.vector.tensor_mul(msg, rows, tmp[:, 2, :, 0:1].broadcast_to([P, G, FEAT]))
    return weigh, 3


def index_first(nc, k, order):
    def index(v, c):
        c.step(nc.vector.tensor_copy(k.index[:], k.sorted[order][:, :, 0]))
    return index


def index_relation(nc, k):
    def index(v, c):
        rec = k.sorted["s"]
        c.step(nc.vector.scalar_tensor_tensor(k.index[:], rec[:, :, 3], float(ROWS), rec[:, :, 0], ALU.mult, ALU.add))
    return index


def store_nodes(nc, k, name, table, nodes, combine=None):
    with ExitStack() as ctx:
        m = Mem(nc, ctx, name)
        chain, ready, wrote = (m.sem(x) for x in ("chain", "ready", "wrote"))
        block = ctx.enter_context(nc.Block())

        @block.vector
        def _(v):
            if combine:
                combine(v, Chain(v, chain))
            v.sem_inc(ready, 1)

        @block.sync
        def _(sp):
            sp.wait_ge(ready, 1)
            sp.dma_start(table_view(table), nodes).then_inc(wrote, 16)
            sp.wait_ge(wrote, 16)


def turn_weights(nc, k, name, out, pieces):
    with ExitStack() as ctx:
        m = Mem(nc, ctx, name)
        raw = m.sb("raw", [P, len(pieces), P])
        ps = m.ps("ps", [P, 2, 512])
        landed, turned, copied = (m.sem(x) for x in ("landed", "turned", "copied"))
        block = ctx.enter_context(nc.Block())

        @block.sync
        def _(sp):
            for n, (a, _) in enumerate(pieces):
                sp.dma_start(raw[:, n, 0:a.shape[1]], a).then_inc(landed, 16)

        @block.tensor
        def _(pe):
            pe.wait_ge(landed, 16 * len(pieces))
            for n, (a, _) in enumerate(pieces):
                if n >= 2:
                    pe.wait_ge(copied, n - 1)
                nc.tensor.transpose(ps[0:a.shape[1], n % 2, 0:P], raw[:, n, 0:a.shape[1]], k.ident[:]
                                    ).then_inc(turned, 1)

        @block.vector
        def _(v):
            for n, (a, to) in enumerate(pieces):
                v.wait_ge(turned, n + 1)
                nc.vector.tensor_copy(to, ps[0:a.shape[1], n % 2, 0:P]).then_inc(copied, 1)
            v.wait_ge(copied, len(pieces))


def dense(nc, k, name, terms, out, biases):
    n_terms = len(terms)
    with ExitStack() as ctx:
        m = Mem(nc, ctx, name)
        turned = m.sb("turned", [P, 2, n_terms, P])
        bias = m.sb("bias", [P, len(biases), FEAT])
        ps_t = m.ps("ps_t", [P, 2, 4, P])
        ps_o = m.ps("ps_o", [P, 2, 512])
        landed, turn, copied, product, used, chain = (
            m.sem(x) for x in ("landed", "turn", "copied", "product", "used", "chain"))
        block = ctx.enter_context(nc.Block())

        @block.sync
        def _(sp):
            for n, a in enumerate(biases):
                sp.dma_start(bias[:, n, :], a.unsqueeze(0).broadcast_to([P, FEAT])).then_inc(landed, 16)

        @block.tensor
        def _(pe):
            for g in range(WIN + 1):
                if g < WIN:
                    if g >= 2:
                        pe.wait_ge(copied, g - 1)
                    for n, (nodes, w) in enumerate(terms):
                        last = nc.tensor.transpose(ps_t[0:nodes.shape[2], g % 2, n, :], nodes[:, g, :], k.ident[:])
                    last.then_inc(turn, 1)
                if g >= 1:
                    pe.wait_ge(copied, g)
                    if g >= 3:
                        pe.wait_ge(used, g - 2)
                    for n, (nodes, w) in enumerate(terms):
                        last = nc.tensor.matmul(ps_o[:, (g - 1) % 2, 0:FEAT],
                                                turned[0:nodes.shape[2], (g - 1) % 2, n, :], w,
                                                start=n == 0, stop=n == n_terms - 1)
                    last.then_inc(product, 1)

        @block.scalar
        def _(act):
            for g in range(WIN):
                act.wait_ge(turn, g + 1)
                if g >= 2:
                    act.wait_ge(product, g - 1)
                for n, (nodes, w) in enumerate(terms):
                    q = nodes.shape[2]
                    last = nc.scalar.copy(turned[0:q, g % 2, n, :], ps_t[0:q, g % 2, n, :])
                last.then_inc(copied, 1)

        @block.vector
        def _(v):
            c = Chain(v, chain)
            v.wait_ge(landed, 16 * len(biases))
            for n in range(1, len(biases)):
                c.step(nc.vector.tensor_add(bias[:, 0, :], bias[:, 0, :], bias[:, n, :]))
            for g in range(WIN):
                v.wait_ge(product, g + 1)
                nc.vector.tensor_add(out[:, g, :], ps_o[:, g % 2, 0:FEAT], bias[:, 0, :]).then_inc(used, 1)
            v.wait_ge(used, WIN)


def relation_rows(nc, k, name, weights, table):
    with ExitStack() as ctx:
        m = Mem(nc, ctx, name)
        turned = m.sb("turned", [P, 2, P])
        out = m.sb("out", [P, 2, RELS, FEAT])
        ps_t = m.ps("ps_t", [P, 2, 512])
        ps_o = m.ps("ps_o", [P, 2, 2, 512])
        turn, copied, product, used_a, used_v = (
            m.sem(x) for x in ("turn", "copied", "product", "used_a", "used_v"))
        wrote = [m.sem(f"wrote{b}") for b in range(2)]
        to = table.rearrange("(r w p) f -> p w r f", p=P, r=RELS)
        half = RELS // 2
        block = ctx.enter_context(nc.Block())

        @block.tensor
        def _(pe):
            for g in range(WIN + 1):
                if g < WIN:
                    if g >= 2:
                        pe.wait_ge(copied, g - 1)
                    nc.tensor.transpose(ps_t[:, g % 2, 0:P], k.x[:, g, :], k.ident[:]).then_inc(turn, 1)
                if g >= 1:
                    pe.wait_ge(copied, g)
                    if g >= 3:
                        pe.wait_ge(used_a, g - 2)
                        pe.wait_ge(used_v, g - 2)
                    for q in range(2):
                        last = nc.tensor.matmul(ps_o[:, (g - 1) % 2, q, :], turned[:, (g - 1) % 2, :],
                                                weights[:, half * q:half * (q + 1), :].rearrange("p r f -> p (r f)"),
                                                start=True, stop=True)
                    last.then_inc(product, 1)

        @block.scalar
        def _(act):
            for g in range(WIN + 1):
                if g < WIN:
                    act.wait_ge(turn, g + 1)
                    if g >= 2:
                        act.wait_ge(product, g - 1)
                    nc.scalar.copy(turned[:, g % 2, :], ps_t[:, g % 2, 0:P]).then_inc(copied, 1)
                if g >= 1:
                    b = (g - 1) % 2
                    act.wait_ge(product, g)
                    if g >= 3:
                        act.wait_ge(wrote[b], 16 * ((g - 1) // 2))
                    nc.scalar.copy(out[:, b, half:RELS, :].rearrange("p r f -> p (r f)"), ps_o[:, b, 1, :]
                                   ).then_inc(used_a, 1)

        @block.vector
        def _(v):
            for g in range(WIN):
                b = g % 2
                v.wait_ge(product, g + 1)
                if g >= 2:
                    v.wait_ge(wrote[b], 16 * (g // 2))
                nc.vector.tensor_copy(out[:, b, 0:half, :].rearrange("p r f -> p (r f)"), ps_o[:, b, 0, :]
                                      ).then_inc(used_v, 1)

        @block.sync
        def _(sp):
            for g in range(WIN):
                sp.wait_ge(used_a, g + 1)
                sp.wait_ge(used_v, g + 1)
                sp.dma_start(to[:, g], out[:, g % 2]).then_inc(wrote[g % 2], 16)
            for b in range(2):
                sp.wait_ge(wrote[b], 16 * (WIN // 2))


def residual_norm(nc, k, name, delta, before=None, result=None, normed=False):
    with ExitStack() as ctx:
        m = Mem(nc, ctx, name)
        squares = m.sb("squares", [P, WIN, FEAT])
        stat = m.sb("stat", [P, 3, WIN])
        chain, asked, raised, ready, wrote = (m.sem(x) for x in ("chain", "asked", "raised", "ready", "wrote"))
        block = ctx.enter_context(nc.Block())
        wide = lambda a: a.unsqueeze(2).broadcast_to([P, WIN, FEAT])

        @block.scalar
        def _(act):
            for n in range(1 + normed):
                act.wait_ge(asked, n + 1)
                nc.scalar.activation(stat[:, 2, :], stat[:, 1, :], ACT.Sqrt).then_inc(raised, 1)

        @block.vector
        def _(v):
            c = Chain(v, chain)
            if before:
                before(v, c)
            if normed:
                c.step(nc.vector.tensor_mul(squares[:], delta, delta))
                c.step(nc.vector.tensor_reduce(stat[:, 1, :], squares[:], AX, ALU.add))
                v.sem_inc(asked, 1)
                v.wait_ge(raised, 1)
                c.step(nc.vector.tensor_scalar(stat[:, 0, :], stat[:, 2, :], 1e-12, None, ALU.max))
                c.step(nc.vector.reciprocal(stat[:, 0, :], stat[:, 0, :]))
                c.step(nc.vector.tensor_mul(delta, delta, wide(stat[:, 0, :])))
            c.step(nc.vector.tensor_add(k.x[:], k.x[:], delta))
            c.step(nc.vector.tensor_reduce(stat[:, 0, :], k.x[:], AX, ALU.add))
            c.step(nc.vector.tensor_scalar(stat[:, 0, :], stat[:, 0, :], 1.0 / FEAT, None, ALU.mult))
            c.step(nc.vector.tensor_sub(k.x[:], k.x[:], wide(stat[:, 0, :])))
            c.step(nc.vector.tensor_mul(squares[:], k.x[:], k.x[:]))
            c.step(nc.vector.tensor_reduce(stat[:, 1, :], squares[:], AX, ALU.add))
            c.step(nc.vector.tensor_scalar(stat[:, 1, :], stat[:, 1, :], 1.0 / FEAT, 1e-5, ALU.mult, ALU.add))
            v.sem_inc(asked, 1)
            v.wait_ge(raised, 1 + normed)
            c.step(nc.vector.reciprocal(stat[:, 0, :], stat[:, 2, :]))
            c.step(nc.vector.tensor_mul(k.x[:], k.x[:], wide(stat[:, 0, :])))
            v.sem_inc(ready, 1)

        if result is not None:
            @block.sync
            def _(sp):
                sp.wait_ge(ready, 1)
                whole = (REAL_WIN - 1) * P
                sp.dma_start(result[0:whole, :].rearrange("(w p) f -> p w f", p=P),
                             k.x[:, 0:REAL_WIN - 1, :]).then_inc(wrote, 16)
                sp.dma_start(result[whole:NODES, :], k.x[0:LAST_ROWS, REAL_WIN - 1, :]).then_inc(wrote, 16)
                sp.wait_ge(wrote, 32)


def gnn_kernel(nc, x, src, dst, edge_attr_64, edge_type_8, edge_weight, L0_gnn_W0, L0_gnn_attn_l0, L0_gnn_attn_r0,
               L0_gnn_bias0, L0_gnn_W1, L0_gnn_attn_l1, L0_gnn_attn_r1, L0_gnn_bias1, L1_gnn_W1, L1_gnn_b1,
               L1_gnn_W2, L1_gnn_b2, L2_gnn_W, L2_gnn_b, L3_gnn_weights, out):
    k = Kept()
    k.pool_dma = [nc.alloc_semaphore(f"pool_dma{s}") for s in range(SLOTS)]
    k.pool_dma_count = 0

    def dram(name, shape, dt=F32):
        return nc.dram_tensor(name, shape, dt).ap()

    k.rec_d = dram("rec_d", [P, TILES, DREC])
    k.rec_s = dram("rec_s", [P, TILES, REC])
    k.pair_win = dram("pair_win", [2, P * PCOLS], I32)
    k.pair_first = dram("pair_first", [P * PCOLS], I32)
    k.pair_skip = dram("pair_skip", [P * PCOLS], I32)
    k.natural = dram("natural", [EDGES, REC])
    k.gat_rows = dram("gat_rows", [ROWS, R_GAT])
    k.gat_edges = dram("gat_edges", [P, TILES, R_GAT])
    nodes_1 = dram("nodes_1", [ROWS, FEAT])
    nodes_2 = dram("nodes_2", [ROWS, FEAT])
    nodes_3 = dram("nodes_3", [ROWS, FEAT + 1])
    nodes_4 = dram("nodes_4", [RELS * ROWS, FEAT])

    with ExitStack() as outer:
        top = Mem(nc, outer, "top")
        constants(nc, k, top)
        k.sorted = {w: top.sb(f"sorted_{w}", [P, TILES, REC]) for w in "ds"}
        k.pair = top.sb("pair", [P, WIN, 2 * HEADS])
        k.per_dst = top.sb("per_dst", [P, WIN])
        k.per_rel = top.sb("per_rel", [P, WIN, RELS])
        k.index = top.sb("index", [P, TILES], I32)
        k.in_order = top.sb("in_order", [1, 1], I32)
        sort_edges(nc, k, src, dst, edge_type_8, edge_weight, edge_attr_64)
        load_edges(nc, k, "d")
        k.x = top.sb("x", [P, WIN, FEAT])
        load_nodes(nc, k, x)

        with ExitStack() as ctx:
            m = Mem(nc, ctx, "attention")
            k.h = m.sb("h", [P, WIN, FEAT])
            half = -(-SCAT // SLOTS // 2)
            for n, (w, left, right, bias) in enumerate((
                    (L0_gnn_W0, L0_gnn_attn_l0, L0_gnn_attn_r0, L0_gnn_bias0),
                    (L0_gnn_W1, L0_gnn_attn_l1, L0_gnn_attn_r1, L0_gnn_bias1))):
                attention_rows(nc, k, f"rows{n}", (k.h if n else k.x)[:], w, left, right)
                attention_maxima(nc, k, f"maxima{n}")
                with ExitStack() as sums:
                    k.acc = Mem(nc, sums, f"attend{n}").sb("acc", [P, WIN, R_GAT + 1])
                    weigh, steps = weigh_attention(nc)
                    edge_pass(nc, k, f"attend{n}", "d", R_GAT + 1, weigh, steps, stream=k.gat_edges,
                              row_width=R_GAT, pair=k.pair, func=ACT.Exp, words=HEADS, counts=True,
                              scatter=[(0, half), (half * SLOTS, SCAT // SLOTS - half)][n])
                    attention_end(nc, k, f"elu{n}", bias, k.h)
            load_edges(nc, k, "s")
            residual_norm(nc, k, "norm0", k.h[:])

        with ExitStack() as ctx:
            m = Mem(nc, ctx, "bilinear")
            both = m.sb("both", [P, WIN, FEAT])
            store_nodes(nc, k, "store1", nodes_1, k.x[:])
            k.acc = m.sb("acc", [P, WIN, FEAT + RELS])
            weigh, steps = weigh_plain(nc, k, True)
            edge_pass(nc, k, "spread1", "s", FEAT + RELS, weigh, steps, table=nodes_1, index=index_first(nc, k, "s"))

            def interact(v, c):
                c.did(nc.vector.tensor_add(both[:], k.x[:], k.acc[:, :, 0:FEAT]))
                c.step(nc.vector.tensor_scalar(k.per_rel[:], k.acc[:, :, FEAT:FEAT + RELS], 1.0, None, ALU.max))
                c.did(nc.vector.reciprocal(k.per_rel[:], k.per_rel[:]))
                c.step(nc.vector.tensor_mul(k.acc[:, :, 0:FEAT], k.x[:], k.acc[:, :, 0:FEAT]))

            store_nodes(nc, k, "store2", nodes_2, k.acc[:, :, 0:FEAT], interact)
            weigh, steps = weigh_plain(nc, k, False)
            edge_pass(nc, k, "spread2", "s", FEAT, weigh, steps, table=nodes_2, index=index_first(nc, k, "s"))
            w12 = m.sb("w12", [P, 2, FEAT])
            load_weights(nc, k, "weights1", w12, (L1_gnn_W1, L1_gnn_W2))
            dense(nc, k, "dense1", [(both, w12[:, 0, :]), (k.acc[:, :, 0:FEAT], w12[:, 1, :])], both,
                  (L1_gnn_b1, L1_gnn_b2))
            residual_norm(nc, k, "norm1", both[:])

        with ExitStack() as ctx:
            m = Mem(nc, ctx, "mean")
            with ExitStack() as table:
                wide = Mem(nc, table, "store3").sb("wide", [P, WIN, FEAT + 1])
                square = Mem(nc, table, "square").sb("wide", [P, WIN, FEAT])

                def with_square(v, c):
                    c.did(nc.vector.tensor_copy(wide[:, :, 0:FEAT], k.x[:]))
                    c.step(nc.vector.tensor_mul(square[:], k.x[:], k.x[:]))
                    c.step(nc.vector.tensor_reduce(wide[:, :, FEAT], square[:], AX, ALU.add))

                store_nodes(nc, k, "store3", nodes_3, wide[:], with_square)
            k.acc = m.sb("acc", [P, WIN, FEAT + ATTR])
            weigh, steps = weigh_normed(nc)
            edge_pass(nc, k, "mean", "d", FEAT + ATTR, weigh, steps, table=nodes_3, index=index_first(nc, k, "d"),
                      row_width=FEAT + 1, attributes=edge_attr_64, func=ACT.Sqrt)
            wt = m.sb("wt", [P, 2, FEAT])
            turn_weights(nc, k, "weights2", wt, [(L2_gnn_W[:, 0:FEAT], wt[:, 0, :]),
                                                 (L2_gnn_W[:, FEAT:FEAT + ATTR], wt[0:ATTR, 1, :])])
            scale_means(nc, k, "means")
            delta = m.sb("delta", [P, WIN, FEAT])
            dense(nc, k, "dense2", [(k.acc[:, :, 0:FEAT], wt[:, 0, :]), (k.acc[:, :, FEAT:], wt[0:ATTR, 1, :])],
                  delta, (L2_gnn_b,))
            residual_norm(nc, k, "norm2", delta[:], normed=True)

        with ExitStack() as ctx:
            m = Mem(nc, ctx, "relations")
            with ExitStack() as table:
                wr = Mem(nc, table, "relations_w").sb("wr", [P, RELS, FEAT])
                turn_weights(nc, k, "weights3", wr, [(L3_gnn_weights[r], wr[:, r, :]) for r in range(RELS)])
                relation_rows(nc, k, "relation_rows", wr, nodes_4)
            k.acc = m.sb("acc", [P, WIN, FEAT])
            weigh, steps = weigh_relation(nc, k)
            edge_pass(nc, k, "relate", "s", FEAT, weigh, steps, table=nodes_4, index=index_relation(nc, k),
                      pair=k.per_rel)

            def relu(v, c):
                c.step(nc.vector.tensor_scalar(k.acc[:], k.acc[:], 0.0, None, ALU.max))

            residual_norm(nc, k, "norm3", k.acc[:], before=relu, result=out)


class Kept:
    pass


def load_weights(nc, k, name, to, weights):
    with ExitStack() as ctx:
        landed = Mem(nc, ctx, name).sem("landed")
        block = ctx.enter_context(nc.Block())

        @block.sync
        def _(sp):
            for n, w in enumerate(weights):
                sp.dma_start(to[:, n, :], w).then_inc(landed, 16)
            sp.wait_ge(landed, 16 * len(weights))


def scale_means(nc, k, name):
    with ExitStack() as ctx:
        chain = Mem(nc, ctx, name).sem("chain")
        block = ctx.enter_context(nc.Block())

        @block.vector
        def _(v):
            c = Chain(v, chain)
            c.step(nc.vector.tensor_mul(k.acc[:], k.acc[:],
                                        k.per_dst[:].unsqueeze(2).broadcast_to([P, WIN, FEAT + ATTR])))


_INS = ["x", "src", "dst", "edge_attr_64", "edge_type_8", "edge_weight", "L0_gnn_W0", "L0_gnn_attn_l0",
        "L0_gnn_attn_r0", "L0_gnn_bias0", "L0_gnn_W1", "L0_gnn_attn_l1", "L0_gnn_attn_r1", "L0_gnn_bias1",
        "L1_gnn_W1", "L1_gnn_b1", "L1_gnn_W2", "L1_gnn_b2", "L2_gnn_W", "L2_gnn_b", "L3_gnn_weights"]


def kernel(**inputs):
    import numpy as np
    from concourse import bacc
    from concourse.bass_utils import run_bass_kernel_spmd

    nc = bacc.Bacc("TRN2", target_bir_lowering=False, num_devices=1)
    arrays, args = {}, []
    for name in _INS:
        a = np.ascontiguousarray(inputs[name])
        arrays[f"in_{name}"] = a
        args.append(nc.dram_tensor(f"in_{name}", a.shape, mybir.dt.from_np(a.dtype), kind="ExternalInput").ap())
    out = nc.dram_tensor("out", (NODES, FEAT), F32, kind="ExternalOutput").ap()
    gnn_kernel(nc, *args, out)
    r = run_bass_kernel_spmd(nc, [arrays], core_ids=[0])
    return r.results[0]["out"]
```
